# Optimizing a Trainium2 kernel written in Bass

```python
import numpy as np
import jax
import jax.numpy as jnp

def _softmax(x, axis=-1):
    return jax.nn.softmax(x, axis=axis)

def _gelu(x):
    return jax.nn.gelu(x, approximate=True)

def _silu(x):
    return jax.nn.silu(x)

def _sigmoid(x):
    return jax.nn.sigmoid(x)

def _layernorm(x, axis=-1, eps=1e-05):
    m = jnp.mean(x, axis=axis, keepdims=True)
    v = jnp.var(x, axis=axis, keepdims=True)
    return (x - m) / jnp.sqrt(v + eps)

def _scatter_add(tgt, idx, src, axis=0):
    return tgt.at[idx].add(src)

def _segment_sum(src, seg, n):
    return jax.ops.segment_sum(src, seg, n)
kernel_name = 'mk_decoder_preln_d2_seqx_r4_0f6842'

def setup_inputs(seed: int=0):
    np.random.seed(seed)
    _w = jnp.asarray

    def _rec_inputs():
        import jax
        import jax.numpy as jnp
        _rk = jax.random.key(seed)
        x = -0.0003929 + 0.9999 * jax.random.normal(jax.random.fold_in(_rk, 1), (32, 256, 256), jnp.float32)
        _lenS = 256 - jax.random.randint(jax.random.fold_in(_rk, 7), (32,), 0, max(1, 256 // 4) + 1, jnp.int32)
        _lenS2 = 256 - jax.random.randint(jax.random.fold_in(_rk, 8), (32,), 0, max(1, 256 // 4) + 1, jnp.int32)
        _ctx_1024P = jax.random.normal(jax.random.fold_in(_rk, 11), (32, 16, 256), jnp.float32)
        _ctx_1024c = jax.random.dirichlet(jax.random.fold_in(_rk, 511), 0.3 * jnp.ones((16,), jnp.float32), (32, 256))
        _ctx_1024t = jnp.einsum('bsk,bkd->bsd', _ctx_1024c, _ctx_1024P)
        _ctx_1024t = _ctx_1024t * jax.lax.rsqrt(jnp.mean(jnp.square(_ctx_1024t)) + 1e-12) * 0.953939
        ctx_1024 = 2.81802e-05 + 1.00001 * (_ctx_1024t + 0.3 * jax.random.normal(jax.random.fold_in(_rk, 611), (32, 256, 256), jnp.float32))
        return (x, ctx_1024, _lenS2)
    x, ctx_1024, _lenS2 = _rec_inputs()

    def _L0_attn_setup():
        import jax, jax.numpy as jnp
        import numpy as np
        DIM = 256
        NH = 16
        HD = DIM // NH
        DROPE = 16
        MAXSEQ = 512
        LAT = 64
        BATCH = 2
        SEQ = 512

        def _rope_freqs(max_seq, head_dim):
            inv = 1.0 / 10000.0 ** (jnp.arange(0, head_dim, 2, dtype=jnp.float32) / head_dim)
            ang = jnp.arange(max_seq, dtype=jnp.float32)[:, None] * inv[None, :]
            return (jnp.cos(ang), jnp.sin(ang))

        def _apply_decoupled_rope(x, cosf, sinf, d_rope):
            b, d1, d2, hd = x.shape
            half = d_rope // 2
            xr = x[..., :d_rope].astype(jnp.float32).reshape(b, d1, d2, half, 2)
            xa, xb = (xr[..., 0], xr[..., 1])
            c = cosf[:d1, :half][None, :, None, :]
            s = sinf[:d1, :half][None, :, None, :]
            rot = jnp.stack([xa * c - xb * s, xa * s + xb * c], axis=-1)
            rot = rot.reshape(b, d1, d2, d_rope)
            return jnp.concatenate([rot, x[..., d_rope:]], axis=-1)
        key = jax.random.key(seed)
        ks = jax.random.split(key, 8)

        def w(k, o, i):
            return jax.random.normal(k, (o, i), jnp.float32) / np.sqrt(i).astype(np.float32)
        return {'x': jax.random.normal(ks[0], (BATCH, SEQ, DIM), jnp.float32), 'wq': w(ks[1], NH * HD, DIM), 'wk_a': w(ks[2], LAT, DIM), 'wk_b': w(ks[3], NH * HD, LAT), 'wv_a': w(ks[4], LAT, DIM), 'wv_b': w(ks[5], NH * HD, LAT), 'wo': w(ks[6], DIM, NH * HD)}
    _L0_attn_all = _L0_attn_setup()
    _L0_attn_in = {k: v for k, v in _L0_attn_all.items() if k in ('wq', 'wk_a', 'wk_b', 'wv_a', 'wv_b', 'wo')}
    del _L0_attn_all

    def _L0_xattn_setup():
        import math
        import jax, jax.numpy as jnp
        import numpy as np
        D_MODEL, N_HEADS, D_K = (256, 16, 64)
        B, S = (4, 1024)
        key = jax.random.key(seed)
        ks = jax.random.split(key, 11)
        scale = 1.0 / math.sqrt(D_MODEL)
        hd = N_HEADS * D_K
        return {'query': jax.random.normal(ks[0], (B, S, D_MODEL), jnp.float32), 'key': jax.random.normal(ks[1], (B, S, D_MODEL), jnp.float32), 'value': jax.random.normal(ks[2], (B, S, D_MODEL), jnp.float32), 'Wq': jax.random.normal(ks[3], (hd, D_MODEL), jnp.float32) * scale, 'bq': jnp.zeros((hd,), jnp.float32), 'Wk': jax.random.normal(ks[4], (hd, D_MODEL), jnp.float32) * scale, 'bk': jnp.zeros((hd,), jnp.float32), 'Wv': jax.random.normal(ks[5], (hd, D_MODEL), jnp.float32) * scale, 'bv': jnp.zeros((hd,), jnp.float32), 'Wo': jax.random.normal(ks[6], (D_MODEL, hd), jnp.float32) * scale, 'bo': jnp.zeros((D_MODEL,), jnp.float32)}
    _L0_xattn_all = _L0_xattn_setup()
    _L0_xattn_in = {k: v for k, v in _L0_xattn_all.items() if k in ('Wq', 'bq', 'Wk', 'bk', 'Wv', 'bv', 'Wo', 'bo')}
    del _L0_xattn_all

    def _L0_ffn_setup():
        import jax, jax.numpy as jnp
        import numpy as np
        CAPACITY_FACTOR = 0.5
        key = jax.random.key(seed)
        ks = jax.random.split(key, 5)
        B, S, D, F = (4, 1024, 256, 1024)
        scale_in = 1.0 / np.sqrt(D)
        scale_ff = 1.0 / np.sqrt(F)
        return {'hidden_states': jax.random.normal(ks[0], (B, S, D), dtype=jnp.float32), 'w_router': jax.random.normal(ks[1], (D,), dtype=jnp.float32) * scale_in, 'W1': jax.random.normal(ks[2], (D, F), dtype=jnp.float32) * scale_in, 'b1': jnp.zeros((F,), dtype=jnp.float32), 'W2': jax.random.normal(ks[3], (F, D), dtype=jnp.float32) * scale_ff, 'b2': jnp.zeros((D,), dtype=jnp.float32)}
    _L0_ffn_all = _L0_ffn_setup()
    _L0_ffn_in = {k: v for k, v in _L0_ffn_all.items() if k in ('w_router', 'W1', 'b1', 'W2', 'b2')}
    del _L0_ffn_all

    def _L1_attn_setup():
        import jax, jax.numpy as jnp
        import numpy as np
        B, S, HID = (2, 512, 256)
        H = 16
        D = HID // H
        SPARSITY = 0.9

        def _sparse_attn(x, Wq, bq, Wk, bk, Wv, bv, Wo, bo):
            b, s, hid = x.shape
            d = hid // H

            def heads(y):
                return y.reshape(b, s, H, d).transpose(0, 2, 1, 3)
            Q = heads(x @ Wq + bq)
            K = heads(x @ Wk + bk)
            V = heads(x @ Wv + bv)
            scores = jnp.einsum('bhqd,bhkd->bhqk', Q, K) / np.sqrt(d)
            k_keep = int(s * (1.0 - SPARSITY))
            vals, idx = jax.lax.top_k(scores, k_keep)
            n = b * H * s
            rows = jnp.arange(n)[:, None]
            sparse = jnp.zeros((n, s), scores.dtype).at[rows, idx.reshape(n, k_keep)].set(vals.reshape(n, k_keep)).reshape(b, H, s, s)
            attn = jax.nn.softmax(sparse, axis=-1)
            out = jnp.einsum('bhqk,bhkd->bhqd', attn, V)
            out = out.transpose(0, 2, 1, 3).reshape(b, s, hid)
            return out @ Wo + bo
        key = jax.random.key(seed)
        ks = jax.random.split(key, 5)
        sc = 1.0 / np.sqrt(HID)
        inp = {'x': jax.random.normal(ks[0], (B, S, HID), jnp.float32)}
        for i, name in enumerate(['q', 'k', 'v', 'o']):
            inp[f'W{name}'] = jax.random.normal(ks[i + 1], (HID, HID), jnp.float32) * sc
            inp[f'b{name}'] = jnp.zeros((HID,), jnp.float32)
        return inp
    _L1_attn_all = _L1_attn_setup()
    _L1_attn_in = {k: v for k, v in _L1_attn_all.items() if k in ('Wq', 'bq', 'Wk', 'bk', 'Wv', 'bv', 'Wo', 'bo')}
    del _L1_attn_all

    def _L1_xattn_setup():
        import jax, jax.numpy as jnp
        import numpy as np
        import math
        B, S, D = (4, 512, 256)
        H = 16
        DH = D // H
        NEG = -1e+20
        key = jax.random.key(seed)
        ks = jax.random.split(key, 8)
        Q_batch = jax.random.normal(ks[0], (B, S, D), dtype=jnp.float32)
        K_batch = jax.random.normal(ks[1], (B, S, D), dtype=jnp.float32)
        V_batch = jax.random.normal(ks[2], (B, S, D), dtype=jnp.float32)
        valid_lens = jax.random.randint(ks[3], (B,), 0, S).astype(jnp.int64)
        sc = 1.0 / math.sqrt(D)
        Wq = jax.random.normal(ks[4], (D, D), dtype=jnp.float32) * sc
        Wk = jax.random.normal(ks[5], (D, D), dtype=jnp.float32) * sc
        Wv = jax.random.normal(ks[6], (D, D), dtype=jnp.float32) * sc
        Wo = jax.random.normal(ks[7], (D, D), dtype=jnp.float32) * sc
        return {'Q_batch': Q_batch, 'K_batch': K_batch, 'V_batch': V_batch, 'valid_lens': valid_lens, 'Wq': Wq, 'Wk': Wk, 'Wv': Wv, 'Wo': Wo}
    _L1_xattn_all = _L1_xattn_setup()
    _L1_xattn_in = {k: v for k, v in _L1_xattn_all.items() if k in ('Wq', 'Wk', 'Wv', 'Wo')}
    del _L1_xattn_all

    def _L1_ffn_setup():
        import jax, jax.numpy as jnp
        import numpy as np
        THRESH_FACTOR = 0.7

        def ternary_quantize(w):
            delta = THRESH_FACTOR * jnp.mean(jnp.abs(w))
            return jnp.where(w > delta, 1.0, jnp.where(w < -delta, -1.0, 0.0)).astype(w.dtype)
        key = jax.random.key(seed)
        k1, k2, k3 = jax.random.split(key, 3)
        B, S, D_IN, D_OUT = (8, 1024, 256, 256)
        inp = {'input': jax.random.normal(k1, (B, S, D_IN), dtype=jnp.float32), 'weight': jax.random.normal(k2, (D_OUT, D_IN), dtype=jnp.float32) * (1.0 / np.sqrt(D_IN)), 'alpha': jnp.ones((1,), dtype=jnp.float32), 'bias': jax.random.normal(k3, (D_OUT,), dtype=jnp.float32) * (1.0 / np.sqrt(D_IN))}
        return inp
    _L1_ffn_all = _L1_ffn_setup()
    _L1_ffn_in = {k: v for k, v in _L1_ffn_all.items() if k in ('weight', 'alpha', 'bias')}
    del _L1_ffn_all
    return {'x': x, 'ctx_1024': ctx_1024, '_lenS2': _lenS2, 'L0_attn_wq': _L0_attn_in['wq'], 'L0_attn_wk_a': _L0_attn_in['wk_a'], 'L0_attn_wk_b': _L0_attn_in['wk_b'], 'L0_attn_wv_a': _L0_attn_in['wv_a'], 'L0_attn_wv_b': _L0_attn_in['wv_b'], 'L0_attn_wo': _L0_attn_in['wo'], 'L0_xattn_Wq': _L0_xattn_in['Wq'], 'L0_xattn_bq': _L0_xattn_in['bq'], 'L0_xattn_Wk': _L0_xattn_in['Wk'], 'L0_xattn_bk': _L0_xattn_in['bk'], 'L0_xattn_Wv': _L0_xattn_in['Wv'], 'L0_xattn_bv': _L0_xattn_in['bv'], 'L0_xattn_Wo': _L0_xattn_in['Wo'], 'L0_xattn_bo': _L0_xattn_in['bo'], 'L0_ffn_w_router': _L0_ffn_in['w_router'], 'L0_ffn_W1': _L0_ffn_in['W1'], 'L0_ffn_b1': _L0_ffn_in['b1'], 'L0_ffn_W2': _L0_ffn_in['W2'], 'L0_ffn_b2': _L0_ffn_in['b2'], 'L1_attn_Wq': _L1_attn_in['Wq'], 'L1_attn_bq': _L1_attn_in['bq'], 'L1_attn_Wk': _L1_attn_in['Wk'], 'L1_attn_bk': _L1_attn_in['bk'], 'L1_attn_Wv': _L1_attn_in['Wv'], 'L1_attn_bv': _L1_attn_in['bv'], 'L1_attn_Wo': _L1_attn_in['Wo'], 'L1_attn_bo': _L1_attn_in['bo'], 'L1_xattn_Wq': _L1_xattn_in['Wq'], 'L1_xattn_Wk': _L1_xattn_in['Wk'], 'L1_xattn_Wv': _L1_xattn_in['Wv'], 'L1_xattn_Wo': _L1_xattn_in['Wo'], 'L1_ffn_weight': _L1_ffn_in['weight'], 'L1_ffn_alpha': _L1_ffn_in['alpha'], 'L1_ffn_bias': _L1_ffn_in['bias']}

def reference(x, ctx_1024, _lenS2, L0_attn_wq, L0_attn_wk_a, L0_attn_wk_b, L0_attn_wv_a, L0_attn_wv_b, L0_attn_wo, L0_xattn_Wq, L0_xattn_bq, L0_xattn_Wk, L0_xattn_bk, L0_xattn_Wv, L0_xattn_bv, L0_xattn_Wo, L0_xattn_bo, L0_ffn_w_router, L0_ffn_W1, L0_ffn_b1, L0_ffn_W2, L0_ffn_b2, L1_attn_Wq, L1_attn_bq, L1_attn_Wk, L1_attn_bk, L1_attn_Wv, L1_attn_bv, L1_attn_Wo, L1_attn_bo, L1_xattn_Wq, L1_xattn_Wk, L1_xattn_Wv, L1_xattn_Wo, L1_ffn_weight, L1_ffn_alpha, L1_ffn_bias):
    import jax
    import jax.numpy as jnp

    def _L0_attn_ref(x, wq, wk_a, wk_b, wv_a, wv_b, wo):
        import jax, jax.numpy as jnp
        import numpy as np
        DIM = 256
        NH = 16
        HD = DIM // NH
        DROPE = 16
        MAXSEQ = 512
        LAT = 64
        BATCH = 2
        SEQ = 512

        def _rope_freqs(max_seq, head_dim):
            inv = 1.0 / 10000.0 ** (jnp.arange(0, head_dim, 2, dtype=jnp.float32) / head_dim)
            ang = jnp.arange(max_seq, dtype=jnp.float32)[:, None] * inv[None, :]
            return (jnp.cos(ang), jnp.sin(ang))

        def _apply_decoupled_rope(x, cosf, sinf, d_rope):
            b, d1, d2, hd = x.shape
            half = d_rope // 2
            xr = x[..., :d_rope].astype(jnp.float32).reshape(b, d1, d2, half, 2)
            xa, xb = (xr[..., 0], xr[..., 1])
            c = cosf[:d1, :half][None, :, None, :]
            s = sinf[:d1, :half][None, :, None, :]
            rot = jnp.stack([xa * c - xb * s, xa * s + xb * c], axis=-1)
            rot = rot.reshape(b, d1, d2, d_rope)
            return jnp.concatenate([rot, x[..., d_rope:]], axis=-1)
        b, s, _ = x.shape
        q = (x @ wq.T).reshape(b, s, NH, HD).transpose(0, 2, 1, 3)
        k = (x @ wk_a.T @ wk_b.T).reshape(b, s, NH, HD).transpose(0, 2, 1, 3)
        v = (x @ wv_a.T @ wv_b.T).reshape(b, s, NH, HD).transpose(0, 2, 1, 3)
        cosf, sinf = _rope_freqs(MAXSEQ, HD)
        q = _apply_decoupled_rope(q, cosf, sinf, DROPE)
        k = _apply_decoupled_rope(k, cosf, sinf, DROPE)
        scores = jnp.einsum('bhqd,bhkd->bhqk', q, k) / np.float32(np.sqrt(HD))
        attn = jax.nn.softmax(scores, axis=-1)
        out = jnp.einsum('bhqk,bhkd->bhqd', attn, v)
        out = out.transpose(0, 2, 1, 3).reshape(b, s, NH * HD)
        return out @ wo.T

    def _L0_xattn_ref(query, key, value, Wq, bq, Wk, bk, Wv, bv, Wo, bo):
        import math
        import jax, jax.numpy as jnp
        import numpy as np
        D_MODEL, N_HEADS, D_K = (256, 16, 64)
        B, S = (4, 1024)
        b, s, _ = query.shape
        q = (query @ Wq.T + bq).reshape(b, s, N_HEADS, D_K)
        k = (key @ Wk.T + bk).reshape(b, s, N_HEADS, D_K)
        v = (value @ Wv.T + bv).reshape(b, s, N_HEADS, D_K)
        inv_sqrt_dk = 1.0 / math.sqrt(D_K)
        scores = jnp.einsum('bshd,bsgd->bshg', q, k) * inv_sqrt_dk
        attn = jax.nn.softmax(scores, axis=-1)
        out = jnp.einsum('bshg,bsgd->bshd', attn, v)
        out = jnp.transpose(out, (0, 2, 1, 3)).reshape(b, -1, N_HEADS * D_K)
        return out @ Wo.T + bo

    def _L0_ffn_ref(hidden_states, w_router, W1, b1, W2, b2):
        import jax, jax.numpy as jnp
        import numpy as np
        CAPACITY_FACTOR = 0.5
        'Mixture-of-Depths block: route top-k tokens through an FFN inner block,\n            scatter back with sigmoid router weights; bypassed tokens pass through.'
        B, S, D = hidden_states.shape
        k = int(S * CAPACITY_FACTOR)
        scores = jnp.einsum('bsd,d->bs', hidden_states, w_router)
        top_scores, top_idx = jax.lax.top_k(scores, k)
        weights = jax.nn.sigmoid(top_scores)
        selected = jnp.take_along_axis(hidden_states, top_idx[:, :, None], axis=1)
        h = jax.nn.gelu(jnp.einsum('bkd,df->bkf', selected, W1) + b1)
        processed = jnp.einsum('bkf,fd->bkd', h, W2) + b2
        update = weights[:, :, None] * processed

        def scatter_one(xb, ib, ub):
            return xb.at[ib].add(ub)
        output = jax.vmap(scatter_one)(hidden_states, top_idx, update)
        return output

    def _L1_attn_ref(x, Wq, bq, Wk, bk, Wv, bv, Wo, bo):
        import jax, jax.numpy as jnp
        import numpy as np
        B, S, HID = (2, 512, 256)
        H = 16
        D = HID // H
        SPARSITY = 0.9

        def _sparse_attn(x, Wq, bq, Wk, bk, Wv, bv, Wo, bo):
            b, s, hid = x.shape
            d = hid // H

            def heads(y):
                return y.reshape(b, s, H, d).transpose(0, 2, 1, 3)
            Q = heads(x @ Wq + bq)
            K = heads(x @ Wk + bk)
            V = heads(x @ Wv + bv)
            scores = jnp.einsum('bhqd,bhkd->bhqk', Q, K) / np.sqrt(d)
            k_keep = int(s * (1.0 - SPARSITY))
            vals, idx = jax.lax.top_k(scores, k_keep)
            n = b * H * s
            rows = jnp.arange(n)[:, None]
            sparse = jnp.zeros((n, s), scores.dtype).at[rows, idx.reshape(n, k_keep)].set(vals.reshape(n, k_keep)).reshape(b, H, s, s)
            attn = jax.nn.softmax(sparse, axis=-1)
            out = jnp.einsum('bhqk,bhkd->bhqd', attn, V)
            out = out.transpose(0, 2, 1, 3).reshape(b, s, hid)
            return out @ Wo + bo
        return _sparse_attn(x, Wq, bq, Wk, bk, Wv, bv, Wo, bo)

    def _L1_xattn_ref(Q_batch, K_batch, V_batch, valid_lens, Wq, Wk, Wv, Wo):
        import jax, jax.numpy as jnp
        import numpy as np
        import math
        B, S, D = (4, 512, 256)
        H = 16
        DH = D // H
        NEG = -1e+20
        b, nq, _ = Q_batch.shape
        nk = K_batch.shape[1]
        q = (Q_batch @ Wq).reshape(b, nq, H, DH).transpose(0, 2, 1, 3)
        k = (K_batch @ Wk).reshape(b, nk, H, DH).transpose(0, 2, 1, 3)
        v = (V_batch @ Wv).reshape(b, nk, H, DH).transpose(0, 2, 1, 3)
        scores = jnp.einsum('bhqd,bhkd->bhqk', q, k) / math.sqrt(DH)
        key_pos = jnp.arange(nk)
        mask = key_pos[None, None, None, :] < valid_lens[:, None, None, None]
        scores = jnp.where(mask, scores, NEG)
        w = jax.nn.softmax(scores, axis=-1)
        o = jnp.einsum('bhqk,bhkd->bhqd', w, v)
        o = o.transpose(0, 2, 1, 3).reshape(b, nq, H * DH)
        return o @ Wo

    def _L1_ffn_ref(input, weight, alpha, bias):
        import jax, jax.numpy as jnp
        import numpy as np
        THRESH_FACTOR = 0.7

        def ternary_quantize(w):
            delta = THRESH_FACTOR * jnp.mean(jnp.abs(w))
            return jnp.where(w > delta, 1.0, jnp.where(w < -delta, -1.0, 0.0)).astype(w.dtype)
        w_ternary = ternary_quantize(weight)
        w_eff = w_ternary * alpha
        out = jnp.einsum('bsd,od->bso', input, w_eff) + bias
        return out
    x = x + _L0_attn_ref(_layernorm(x, axis=-1), L0_attn_wq, L0_attn_wk_a, L0_attn_wk_b, L0_attn_wv_a, L0_attn_wv_b, L0_attn_wo)
    x = x + _L0_xattn_ref(_layernorm(x, axis=-1), ctx_1024, ctx_1024, L0_xattn_Wq, L0_xattn_bq, L0_xattn_Wk, L0_xattn_bk, L0_xattn_Wv, L0_xattn_bv, L0_xattn_Wo, L0_xattn_bo)
    x = x + _L0_ffn_ref(_layernorm(x, axis=-1), L0_ffn_w_router, L0_ffn_W1, L0_ffn_b1, L0_ffn_W2, L0_ffn_b2)
    x = x + _L1_attn_ref(_layernorm(x, axis=-1), L1_attn_Wq, L1_attn_bq, L1_attn_Wk, L1_attn_bk, L1_attn_Wv, L1_attn_bv, L1_attn_Wo, L1_attn_bo)
    x = x + _L1_xattn_ref(_layernorm(x, axis=-1), ctx_1024, ctx_1024, _lenS2, L1_xattn_Wq, L1_xattn_Wk, L1_xattn_Wv, L1_xattn_Wo)
    x = x + _L1_ffn_ref(_layernorm(x, axis=-1), L1_ffn_weight, L1_ffn_alpha, L1_ffn_bias)
    return x

_drawn_inputs = setup_inputs


def setup_inputs(seed=0):
    import zlib

    import numpy as np

    out = dict(_drawn_inputs(seed))
    spreads = {'L0_xattn_bq': (0.0, 0.1),
     'L0_xattn_bk': (0.0, 0.1),
     'L0_xattn_bv': (0.0, 0.1),
     'L0_xattn_bo': (0.0, 0.1),
     'L0_ffn_b1': (0.0, 0.539),
     'L0_ffn_b2': (0.0, 0.383),
     'L1_attn_bq': (0.0, 0.8),
     'L1_attn_bk': (0.0, 2.0),
     'L1_attn_bv': (0.0, 0.1),
     'L1_attn_bo': (0.0, 0.1)}
    factors = {'L1_ffn_bias': 8.0}
    for name, (base, spread) in spreads.items():
        noise = np.random.default_rng([zlib.crc32(name.encode()), seed]).standard_normal(out[name].shape)
        drawn = base * np.exp(spread * noise) if base else spread * noise
        out[name] = jnp.asarray(drawn.astype(out[name].dtype))
    for name, factor in factors.items():
        out[name] = (out[name] * factor).astype(out[name].dtype)
    return out
```

```python
import numpy as np
import concourse.bass as bass
from concourse import mybir
from contextlib import ExitStack

F32 = mybir.dt.float32
BF16 = mybir.dt.bfloat16
I32 = mybir.dt.int32
ALU = mybir.AluOpType
ACT = mybir.ActivationFunctionType
AX = mybir.AxisListType

P = 128
B, S, D = 32, 256, 256
H, HD = 16, 16
XD = 64
FF = 1024
NT = S // P
ND = D // P
HT = P // HD
QR = 8
KEEP = int(S * (1.0 - 0.9))
CAP = S // 2
NJ, NU = 16, 16
QUADS = NJ // 2
EPS = 1e-5
BIG = 2.0 ** 100
FAR = 2.0 ** 100
NEG = -4.0e20
ROUNDS = (KEEP + 7) // 8
assert KEEP % 8 == 1 and ROUNDS == 4

WEIGHTS = {
    "wq0": [P, ND, D], "wq0s": [P, ND, D], "wlat": [P, ND, P], "wkb": [P, D], "wkbs": [P, D],
    "wvb": [P, D], "wo0": [P, ND, D], "ropec": [P, D], "ropes": [P, D], "hmask": [P, HT],
    "xwq": [P, ND, H * XD], "xwk": [P, ND, H * XD], "xwv": [P, ND, H * XD], "xwo": [P, 8, D],
    "xb": [XD, 3, H], "xbo": [P, D], "wrt": [P, ND, P], "w1": [P, ND, FF], "b1": [P, FF // P],
    "w2": [P, FF // P, D], "b2": [1, D],
    "swq": [P, ND, D], "swk": [P, ND, D], "swv": [P, ND, D], "swo": [P, ND, D],
    "sbq": [P, ND], "sbk": [P, ND], "sbv": [P, D], "sbo": [P, D],
    "cwq": [P, ND, D], "cwk": [P, ND, D], "cwv": [P, ND, D], "cwo": [P, ND, D],
    "wt": [P, ND, D], "alpha": [P, 1], "fbias": [P, D],
    "ident": [P, P], "lower": [P, NT, S], "iota": [P, S], "groupq": [8, NJ * H * NU], "groupk": [8, NJ * H * NU],
}


def program(nc, x_in, ctx_in, lens_in, w_in, out):
    es = ExitStack()
    with es:
        def sb(name, shape, dt=F32):
            return es.enter_context(nc.sbuf_tensor(name, shape, dt))

        used = []

        def sem(name):
            s = es.enter_context(nc.semaphore(name))
            used.append(s)
            return s

        skip = ("groupq", "groupk", "wt", "wq0s", "wkbs", "ropec", "ropes")
        w = {n: sb(n, shape) for n, shape in WEIGHTS.items() if n not in skip}
        weff = sb("weff", [P, ND, D])
        ones = sb("ones", [P, P])
        ones_b = sb("ones_b", [1, P], BF16)
        half_neg = sb("half_neg", [P, NT])
        bq8 = sb("bq8", [XD, H])
        tern = sb("tern", [P, 4])

        bankA = [es.enter_context(nc.psum_tensor(f"bankA{i}", [P, 512], F32)) for i in range(4)]
        bankB = [es.enter_context(nc.psum_tensor(f"bankB{i}", [P, 512], F32)) for i in range(4)]

        xa = sb("xa", [P, NT, D])
        x1 = x2 = xa
        x3 = sb("x3", [P, NT, D])
        ctxA = sb("ctxA", [P, ND, S])
        ctxB = sb("ctxB", [P, ND, S])

        def attention_buffers(p, qm, pr, pt, ot, onT, kq):
            kT, qT = (kq[:, 512 * k:512 * k + 512].rearrange("p (e s) -> p e s", e=ND) for k in range(2))
            return dict(
                p=p, qm=qm, kT=kT, va=sb(p + "va", [P, NT, H, 2 * HD]),
                qr=qm.shape[1], nm=sb(p + "nm", [P, H, NT]), pr=pr, pt=pt, ot=ot, rd=sb(p + "rd", [P, NT, H]), on=qT, onT=onT, qT=qT)

        vT_qm = sb("vT_qm", [P, NJ * H * NU])
        xq_area = sb("xq_area", [P, NJ * H * NU])
        part = lambda k: xq_area[:, 1024 * k:1024 * (k + 1)]
        lnA = dict(st=sb("lnA_st", [P, NT, 6]), mv=sb("lnA_mv", [P, NT, 2]), rs=sb("lnA_rs", [P, NT]),
                   xn=sb("lnA_xn", [P, NT, D]), xT=sb("lnA_xT", [P, ND, S]))
        lnB = dict(st=sb("lnB_st", [P, NT, 6]), mv=sb("lnB_mv", [P, NT, 2]), rs=sb("lnB_rs", [P, NT]),
                   xn=sb("lnB_xn", [P, NT, D]), xT=sb("lnB_xT", [P, ND, S]))
        a_kq = sb("a_kq", [P, 2 * ND * S])
        bufA = attention_buffers("a_", vT_qm[:, :].rearrange("p (h s) -> p h s", h=H),
                                 part(0).rearrange("p (k t s) -> p k t s", k=2, t=NT),
                                 part(1).rearrange("p (k t s) -> p k t s", k=2, t=NT),
                                 part(2).rearrange("p (c s) -> p c s", c=4), lnA["xT"], a_kq)
        bufB = attention_buffers("b_", sb("b_qm", [P, QR, S]), sb("b_pr", [P, 2, NT, S]), sb("b_pt", [P, 2, NT, S]),
                                 sb("b_ot", [P, 4, S]), lnB["xT"], sb("b_kq", [P, 2 * ND * S]))
        latT = lnA["xn"][:, 0, :]
        xqT = xq_area[0:XD + 8, :].rearrange("p (g h u) -> p g (h u)", g=2 * NJ, h=H)
        xkT = vT_qm[0:XD + 8, :].rearrange("p (g h u) -> p g (h u)", g=2 * NJ, h=H)
        xvT = vT_qm[0:XD, :].rearrange("p (g h u) -> p g (h u)", g=2 * NJ, h=H)
        xv = sb("xv", [P, 2 * NJ, XD])
        xnm = sb("xnm", [P, 2 * NJ])
        xrs = sb("xrs", [P, 2 * NJ])
        xrr = sb("xrr", [P, 2 * NJ])
        xp = sb("xp", [P, 2, 4, P])
        xpn = xp
        xpt = a_kq[:].rearrange("p (b i c) -> p b i c", b=2, i=4)
        xot = sb("xot", [P, QUADS, H, 2, 8])
        scol = sb("scol", [P, NT])
        srow = xv[:, 24:28, :].rearrange("p g c -> p (g c)")
        area = xv[:, :, :].rearrange("p g c -> p (g c)")
        tmpd = area[:, 0:512].rearrange("p (t s) -> p t s", t=NT)
        gt = sb("gt", [P, NT])
        eq = sb("eq", [P, NT])
        rank = sb("rank", [P, NT])
        gate = sb("gate", [P, NT])
        gate1 = sb("gate1", [P, NT])
        gate2 = sb("gate2", [P, NT])
        pick = area[:, 512:768].rearrange("p (t c) -> p t c", t=NT)
        pickT = area[:, 768:1024].rearrange("p (t c) -> p t c", t=NT)
        selT = area[:, 1024:1280].rearrange("p (t c) -> p t c", t=ND)
        yff = area[:, 1280:1536]
        hid = xot[:, 0:4].rearrange("p a h b c -> p (a h b c)").rearrange("p (f c) -> p f c", c=CAP)
        xh = xa
        sc = sb("sc", [P, 3, NT, S])
        wk = sb("wk", [P, 2, NT, S])
        m8 = sb("m8", [P, 2, ROUNDS, NT, 8])
        taken = bufB["pr"]
        sp_ = taken
        mx0 = sb("mx0", [P, H, NT])
        x4 = sb("x4", [P, NT, D])
        x5 = x4
        xo = x4
        lenb = sb("lenb", [1, 1], I32)
        lenf = sb("lenf", [1, 1])
        mrow = sb("mrow", [1, NT, S], BF16)

        w["wt"] = x4
        tern2 = x3
        w["wq0s"] = xq_area[:, 0:512].rearrange("p (e s) -> p e s", e=ND)
        w["wkbs"] = xq_area[:, 512:768]
        w["ropec"] = xq_area[:, 768:1024]
        w["ropes"] = xq_area[:, 1024:1280]

        s_w = sem("weights_loaded")
        s_set = sem("setup_done")
        s_sum = sem("weight_sum_ready")
        s_rope = sem("rotated")
        with nc.Block() as block:
            nload = len(w)

            @block.sync
            def _(sp):
                for n in WEIGHTS:
                    if n in w:
                        sp.dma_start(w[n][:], w_in[n]).then_inc(s_w, 16)
                sp.wait_ge(s_w, 16 * nload)

            @block.tensor
            def _(pe):
                pe.wait_ge(s_set, 3)
                nc.tensor.matmul(bankA[0][:, 0:1], ones[:], tern[:, 0:1], start=True, stop=True).then_inc(s_sum, 1)

            @block.vector
            def _(dve):
                nc.vector.memset(ones[:], 1.0).then_inc(s_set, 1)
                nc.vector.memset(ones_b[:], 1.0).then_inc(s_set, 1)
                dve.wait_ge(s_w, 16 * nload)
                nc.vector.tensor_reduce(tern[:, 0:1], w["wt"][:], AX.XY, ALU.add,
                                        apply_absolute_value=True).then_inc(s_set, 1)
                nc.vector.memset(half_neg[:], -0.5).then_inc(s_set, 1)
                nc.vector.memset(bufA["va"][:], 1.0).then_inc(s_set, 1)
                nc.vector.memset(bufB["va"][:], 1.0).then_inc(s_set, 1)
                nc.vector.tensor_scalar(bq8[:], w["xb"][:, 0, :], XD ** -0.5, None, ALU.mult).then_inc(s_set, 1)
                for wt, ws, wide in ((w["wq0"], w["wq0s"], True), (w["wkb"], w["wkbs"], False)):
                    cos, sin = w["ropec"][:], w["ropes"][:]
                    if wide:
                        cos, sin = (a.unsqueeze(1).broadcast_to([P, ND, D]) for a in (cos, sin))
                    nc.vector.tensor_tensor(wt[:], wt[:], cos, ALU.mult).then_inc(s_rope, 1)
                    nc.vector.tensor_tensor(ws[:], ws[:], sin, ALU.mult).then_inc(s_rope, 1)
                dve.wait_ge(s_rope, 4)
                nc.vector.tensor_tensor(w["wq0"][:], w["wq0"][:], w["wq0s"][:], ALU.add).then_inc(s_rope, 1)
                nc.vector.tensor_tensor(w["wkb"][:], w["wkb"][:], w["wkbs"][:], ALU.add).then_inc(s_rope, 1)
                dve.wait_ge(s_rope, 6)
                dve.wait_ge(s_sum, 1)
                nc.vector.tensor_scalar(tern[:, 1:2], bankA[0][:, 0:1], 1.0 / (D * D), 0.7, ALU.mult, ALU.mult).then_inc(s_set, 1)
                nc.vector.tensor_scalar(tern[:, 2:3], bankA[0][:, 0:1], 1.0 / (D * D), -0.7, ALU.mult, ALU.mult).then_inc(s_set, 1)
                dve.wait_ge(s_set, 9)
                nc.vector.tensor_scalar(weff[:], w["wt"][:], tern[:, 1:2], w["alpha"][:, 0:1], ALU.is_gt, ALU.mult).then_inc(s_set, 1)
                nc.vector.tensor_scalar(tern2[:], w["wt"][:], tern[:, 2:3], w["alpha"][:, 0:1], ALU.is_lt, ALU.mult).then_inc(s_set, 1)
                dve.wait_ge(s_set, 11)
                nc.vector.tensor_tensor(weff[:], weff[:], tern2[:], ALU.subtract).then_inc(s_set, 1)
                dve.wait_ge(s_set, 12)

        class Signals(dict):
            def __missing__(self, name):
                self[name] = sem(name)
                return self[name]

        g = Signals()

        def ln_dve(dve, k, x, ln, ready):
            for s, v in ready:
                dve.wait_ge(s, v)
            for t in range(NT):
                nc.vector.bn_stats(ln["st"][:, t, :], x[:, t, :]).then_inc(g[f"ln{k}_stat"], 1)
            dve.wait_ge(g[f"ln{k}_stat"], 2)
            for t in range(NT):
                nc.vector.bn_aggr(ln["mv"][:, t, :], ln["st"][:, t, :]).then_inc(g[f"ln{k}_stat"], 1)

        def ln_pool(pool, k, ln):
            pool.wait_ge(g[f"ln{k}_stat"], 4)
            nc.gpsimd.tensor_scalar(ln["rs"][:], ln["mv"][:, :, 1], EPS, 1.0, ALU.add, ALU.mult).then_inc(g[f"ln{k}_stat"], 1)
            pool.wait_ge(g[f"ln{k}_stat"], 5)
            nc.gpsimd.tensor_tensor(ln["rs"][:], ln["rs"][:], half_neg[:], ALU.pow).then_inc(g[f"ln{k}_rstd"], 1)

        def ln_dve2(dve, k, x, ln):
            dve.wait_ge(g[f"ln{k}_rstd"], 1)
            for t in range(NT):
                nc.vector.tensor_scalar(ln["xn"][:, t, :], x[:, t, :], ln["mv"][:, t, 0:1], ln["rs"][:, t:t + 1],
                                        ALU.subtract, ALU.mult).then_inc(g[f"ln{k}_xn"], 1)

        def ln_pe(pe, k, ln, bank):
            pe.wait_ge(g[f"ln{k}_xn"], 2)
            for d in range(ND):
                for t in range(NT):
                    last = nc.tensor.transpose(bank[:, d * S + t * P:d * S + (t + 1) * P],
                                               ln["xn"][:, t, d * P:(d + 1) * P], w["ident"][:])
            last.then_inc(g[f"ln{k}_tr"], 1)

        def ln_act(act, k, ln, bank):
            act.wait_ge(g[f"ln{k}_tr"], 1)
            nc.scalar.activation(ln["xT"][:].rearrange("p d s -> p (d s)"), bank[:], ACT.Copy).then_inc(g[f"ln{k}_xT"], 1)

        def project_T(bank, wt, xT, done):
            for e in range(ND):
                for d in range(ND):
                    last = nc.tensor.matmul(bank[:, e * S:(e + 1) * S], wt[:, d, e * P:(e + 1) * P], xT[:, d, :],
                                            start=(d == 0), stop=(d == ND - 1))
            last.then_inc(done, 1)

        def project_N(bank, xT, wt, done):
            for t in range(NT):
                for d in range(ND):
                    last = nc.tensor.matmul(bank[:, t * D:(t + 1) * D], xT[:, d, t * P:(t + 1) * P], wt[:, d, :],
                                            start=(d == 0), stop=(d == ND - 1))
            last.then_inc(done, 1)

        def at_scores(pe, n, b, bank, h, free, per, masked=False):
            pe.wait_ge(g[n + "_qm"], h // 2 + 1)
            if h >= 2:
                pe.wait_ge(free, per * (h - 1))
            if masked:
                nc.tensor.matmul(bank[:], ones_b[:], mrow[:].rearrange("p t s -> p (t s)"), start=True, stop=False,
                                 skip_group_check=True)
            for t in range(NT):
                last = nc.tensor.matmul(bank[:, t * S:(t + 1) * S], b["qm"][:, h % b["qr"], t * P:(t + 1) * P],
                                        b["kT"][:, h // HT, :], start=not masked, stop=True, skip_group_check=masked)
            last.then_inc(g[n + "_s"], 1)

        def at_transpose(pe, n, b, bank, h):
            pe.wait_ge(g[n + "_ex"], NT * (h + 1))
            if h >= 1:
                pe.wait_ge(g[n + "_pt"], h)
            for c in range(NT):
                for t in range(NT):
                    last = nc.tensor.transpose(bank[:, c * S + t * P:c * S + (t + 1) * P],
                                               b["pr"][:, h % 2, t, c * P:(c + 1) * P], w["ident"][:])
            last.then_inc(g[n + "_tr"], 1)

        def at_copy_pt(act, n, b, bank, h):
            act.wait_ge(g[n + "_tr"], h + 1)
            if h >= 2:
                act.wait_ge(g[n + "_pv"], h - 1)
            nc.scalar.activation(b["pt"][:, h % 2].rearrange("p c s -> p (c s)"), bank[:], ACT.Copy).then_inc(g[n + "_pt"], 1)

        def at_values(pe, n, b, bank, h):
            pe.wait_ge(g[n + "_pt"], h + 1)
            if h == 8:
                pe.wait_ge(g[n + "_ot"], 1)
            r, c = 32 * (h % 4), S * ((h // 4) % 2)
            for k in range(NT):
                last = nc.tensor.matmul(bank[r:r + 32, c:c + S], b["va"][:, k, h, :], b["pt"][:, h % 2, k, :],
                                        start=(k == 0), stop=(k == NT - 1))
            last.then_inc(g[n + "_pv"], 1)

        def at_copy_ot(act, n, b, bank, half):
            act.wait_ge(g[n + "_pv"], 8 * (half + 1))
            nc.scalar.activation(b["ot"][:, 2 * half:2 * half + 2].rearrange("p c s -> p (c s)"), bank[:], ACT.Copy).then_inc(g[n + "_ot"], 1)

        def at_out_pe1(pe, n, b, banks):
            pe.wait_ge(g[n + "_ot"], 2)
            for t in range(NT):
                for q in range(4):
                    last = nc.tensor.transpose(banks[t][:, q * P:(q + 1) * P], b["ot"][:, q, t * P:(t + 1) * P], w["ident"][:])
            last.then_inc(g[n + "_ott"], 1)

        def at_out_dve(dve, n, b, banks):
            dve.wait_ge(g[n + "_ott"], 1)
            for t in range(NT):
                v = banks[t][:].rearrange("p (h c) -> p h c", c=2 * HD)
                nc.vector.reciprocal(b["rd"][:, t, :], v[:, :, HD]).then_inc(g[n + "_rd"], 1)
            for t in range(NT):
                v = banks[t][:].rearrange("p (h c) -> p h c", c=2 * HD)
                dve.wait_ge(g[n + "_rd"], t + 1)
                nc.vector.tensor_tensor(b["on"][:, t, :].rearrange("p (h c) -> p h c", c=HD), v[:, :, 0:HD],
                                        b["rd"][:, t, :].unsqueeze(2).broadcast_to([P, H, HD]), ALU.mult).then_inc(g[n + "_on"], 1)

        def at_out_pe2(pe, n, b, bank):
            pe.wait_ge(g[n + "_on"], 2)
            for e in range(ND):
                for t in range(NT):
                    last = nc.tensor.transpose(bank[:, e * S + t * P:e * S + (t + 1) * P], b["on"][:, t, e * P:(e + 1) * P], w["ident"][:])
            last.then_inc(g[n + "_ont"], 1)

        def at_out_act(act, n, b, bank):
            act.wait_ge(g[n + "_ont"], 1)
            nc.scalar.activation(b["onT"][:].rearrange("p e s -> p (e s)"), bank[:], ACT.Copy).then_inc(g[n + "_onT"], 1)

        def at_mask_q(pool, n, b, c):
            h = 2 * c
            r = h % b["qr"]
            if h >= b["qr"]:
                pool.wait_ge(g[n + "_s"], h - b["qr"] + 2)
            nc.gpsimd.tensor_tensor(b["qm"][:, r:r + 2, :], b["qT"][:, h // HT, :].unsqueeze(1).broadcast_to([P, 2, S]),
                                    w["hmask"][:, h % HT:h % HT + 2].unsqueeze(2).broadcast_to([P, 2, S]),
                                    ALU.mult).then_inc(g[n + "_qm"], 1)

        def at_mask_later(pool, n, b, s):
            if s % 2 == 0 and QR // 2 <= (s + 6) // 2 < H // 2:
                at_mask_q(pool, n, b, (s + 6) // 2)

        HS = H + 2

        def tensor_a(pe):
            b = bufA
            yield 0
            ln_pe(pe, 0, lnA, bankA[0])
            yield 1
            pe.wait_ge(g["ln0_xT"], 1)
            xT = lnA["xT"]
            for d in range(ND):
                last = nc.tensor.matmul(bankA[2][:, 0:S], w["wlat"][:, d, :], xT[:, d, :], start=(d == 0), stop=(d == ND - 1))
            last.then_inc(g["lat_ps"], 1)
            project_T(bankA[0], w["wq0"], xT, g["mla_q"])
            pe.wait_ge(g["latT"], 1)
            for e in range(ND):
                last = nc.tensor.matmul(bankA[1][:, e * S:(e + 1) * S], w["wkb"][:, e * P:(e + 1) * P], latT, start=True, stop=True)
            last.then_inc(g["mla_k"], 1)
            yield 2
            for t in range(NT):
                last = nc.tensor.matmul(bankA[2][:, t * D:(t + 1) * D], latT[:, t * P:(t + 1) * P], w["wvb"][:], start=True, stop=True)
            last.then_inc(g["mla_v"], 1)
            pe.wait_ge(g["mla_kT"], 1)
            pe.wait_ge(g["mla_va"], 1)
            for h in range(HS):
                yield 3 + h
                if h < H:
                    at_scores(pe, "mla", b, bankA[h % 2], h, g["mla_ex"], NT)
                if 1 <= h <= H:
                    at_transpose(pe, "mla", b, bankA[2], h - 1)
                if h >= 2:
                    at_values(pe, "mla", b, bankA[3], h - 2)
            yield 3 + HS
            at_out_pe1(pe, "mla", b, bankA[0:2])
            yield 4 + HS
            at_out_pe2(pe, "mla", b, bankA[2])
            yield 5 + HS
            pe.wait_ge(g["mla_onT"], 1)
            project_N(bankA[3], b["onT"], w["wo0"], g["mla_y"])
            n = 6 + HS
            yield n
            ln_pe(pe, 1, lnA, bankA[0])
            for k in range(12):
                which, quad = k // 4, k % 4
                yield n + 1 + k
                if k == 0:
                    pe.wait_ge(g["ln1_xT"], 1)
                    pe.wait_ge(g["ctxA_in"], 16)
                if k >= 2:
                    pe.wait_ge(g["hm_ev"], 4 * (k - 1))
                wt, src = (("xwv", ctxA), ("xwq", lnA["xT"]), ("xwk", ctxA))[which]
                for hp in range(2):
                    for d in range(ND):
                        c = (quad * 2 + hp) * P
                        last = nc.tensor.matmul(bankA[k % 2][:, hp * S:(hp + 1) * S], w[wt][:, d, c:c + P], src[:, d, :],
                                                start=(d == 0), stop=(d == ND - 1))
                last.then_inc(g["hm_proj"], 1)
                if 4 <= k < 8:
                    v = k - 4
                    pe.wait_ge(g["hm_ev"], 16)
                    if v >= 2:
                        pe.wait_ge(g["hm_vev"], v - 1)
                    for i in range(8):
                        gi = v * 8 + i
                        last = nc.tensor.transpose(bankA[2 + v % 2][:, i * XD:(i + 1) * XD],
                                                   xvT[:, gi, :], w["ident"][0:XD, 0:XD])
                    last.then_inc(g["hm_vtr"], 1)
            n += 13
            yield n
            n += 1
            for s in range(QUADS + 3):
                yield n + s
                if s == 0:
                    pe.wait_ge(g["hm_ev"], 48)
                    pe.wait_ge(g["group_in"], 32)
                if s < QUADS:
                    if s >= 2:
                        pe.wait_ge(g["hm_ex"], 4 * (s - 1))
                    for i in range(4):
                        j, uh = 2 * s + i // 2, i % 2
                        last = nc.tensor.matmul(bankA[s % 2][:, i * P:(i + 1) * P], xqT[:, 2 * j + uh, :],
                                                xkT[:, 2 * j + uh, :], start=True, stop=True)
                    last.then_inc(g["hm_s"], 1)
                if 2 <= s < QUADS + 2:
                    q = s - 2
                    pe.wait_ge(g["hm_pn"], q + 1)
                    pe.wait_ge(g["hm_vev"], 4)
                    if q >= 1:
                        pe.wait_ge(g["hm_pt"], q)
                    for i in range(4):
                        last = nc.tensor.transpose(bankA[2][:, i * P:(i + 1) * P], xpn[:, q % 2, i, :], w["ident"][:])
                    last.then_inc(g["hm_tr"], 1)
                if s >= 3:
                    q = s - 3
                    pe.wait_ge(g["hm_pt"], q + 1)
                    if q >= 1:
                        pe.wait_ge(g["hm_ot"], q)
                    for jo in range(2):
                        for uh in range(2):
                            i = jo * 2 + uh
                            last = nc.tensor.matmul(bankA[3][jo * XD:(jo + 1) * XD, uh * P:(uh + 1) * P],
                                                    xv[:, 4 * q + i, :], xpt[:, q % 2, i, :], start=True, stop=True)
                    last.then_inc(g["hm_o"], 1)
            n += QUADS + 3
            yield n
            pe.wait_ge(g["hm_ot"], QUADS)
            for t in range(NT):
                for jp in range(QUADS):
                    last = nc.tensor.matmul(bankA[0][:, t * D:(t + 1) * D],
                                            xot[:, jp, 8 * t:8 * t + 8].rearrange("p h a b -> p (h a b)"),
                                            w["xwo"][:, jp, :], start=(jp == 0), stop=(jp == QUADS - 1))
            last.then_inc(g["hm_y"], 1)
            n += 1
            yield n
            ln_pe(pe, 2, lnA, bankA[1])
            yield n + 1
            pe.wait_ge(g["ln2_xT"], 1)
            for d in range(ND):
                last = nc.tensor.matmul(bankA[2][:, 0:S], w["wrt"][:, d, :], lnA["xT"][:, d, :], start=(d == 0), stop=(d == ND - 1))
            last.then_inc(g["md_sps"], 1)
            yield n + 3
            pe.wait_ge(g["md_e"], 8)
            for d in range(ND):
                for t in range(NT):
                    last = nc.tensor.matmul(bankA[0][:, d * P:(d + 1) * P], lnA["xn"][:, t, d * P:(d + 1) * P], pick[:, t, :],
                                            start=(t == 0), stop=(t == NT - 1))
            last.then_inc(g["md_sel"], 1)
            for t in range(NT):
                last = nc.tensor.transpose(bankA[3][:, t * P:(t + 1) * P], pick[:, t, :], w["ident"][:])
            last.then_inc(g["md_ptr"], 1)
            yield n + 4
            pe.wait_ge(g["md_selT"], 1)
            for k in range(2):
                for f in range(4):
                    for d in range(ND):
                        c = (4 * k + f) * P
                        last = nc.tensor.matmul(bankA[1 + k][:, f * P:(f + 1) * P], w["w1"][:, d, c:c + P], selT[:, d, :],
                                                start=(d == 0), stop=(d == ND - 1))
                last.then_inc(g["md_h"], 1)
            yield n + 5
            pe.wait_ge(g["md_hid"], 8)
            for f in range(FF // P):
                nc.tensor.matmul(bankA[0][:, 0:D], hid[:, f, :], w["w2"][:, f, :], start=(f == 0), stop=False)
            nc.tensor.matmul(bankA[0][:, 0:D], ones[0:1, :], w["b2"][:], start=False, stop=True).then_inc(g["md_y"], 1)
            yield n + 6
            pe.wait_ge(g["md_yff"], 1)
            pe.wait_ge(g["md_pickT"], 1)
            for t in range(NT):
                last = nc.tensor.matmul(bankA[3][:, t * D:(t + 1) * D], pickT[:, t, :], yff[:], start=True, stop=True)
            last.then_inc(g["md_u"], 1)
            yield n + 7


        def exps(act, n, b, bank, h):
            act.wait_ge(g[n + "_nm"], h + 1)
            if h >= 2:
                act.wait_ge(g[n + "_tr"], h - 1)
            for t in range(NT):
                a = nc.scalar.activation(b["pr"][:, h % 2, t, :], bank[:, t * S:(t + 1) * S], ACT.Exp,
                                         bias=b["nm"][:, h, t:t + 1])
                a.then_inc(g[n + "_ex"], 1)

        def scalar_a(act):
            b = bufA
            yield 0
            ln_act(act, 0, lnA, bankA[0])
            yield 1
            act.wait_ge(g["lat_ps"], 1)
            nc.scalar.activation(latT, bankA[2][:, 0:S], ACT.Copy).then_inc(g["latT"], 1)
            act.wait_ge(g["mla_q"], 1)
            nc.scalar.activation(b["qT"][:].rearrange("p e s -> p (e s)"), bankA[0][:], ACT.Copy).then_inc(g["mla_qT"], 1)
            act.wait_ge(g["mla_k"], 1)
            nc.scalar.activation(b["kT"][:].rearrange("p e s -> p (e s)"), bankA[1][:], ACT.Copy).then_inc(g["mla_kT"], 1)
            yield 2
            act.wait_ge(g["mla_v"], 1)
            nc.scalar.activation(b["va"][:, :, :, 0:HD], bankA[2][:].rearrange("p (t h c) -> p t h c", t=NT, c=HD),
                                 ACT.Copy).then_inc(g["mla_va"], 1)
            for h in range(HS):
                yield 3 + h
                if 1 <= h <= H:
                    at_copy_pt(act, "mla", b, bankA[2], h - 1)
                if h < H:
                    exps(act, "mla", b, bankA[h % 2], h)
                if h == 10:
                    at_copy_ot(act, "mla", b, bankA[3], 0)
            yield 3 + HS
            at_copy_ot(act, "mla", b, bankA[3], 1)
            yield 4 + HS
            at_out_act(act, "mla", b, bankA[2])
            n = 6 + HS
            yield n
            ln_act(act, 1, lnA, bankA[0])
            for k in range(12):
                which, quad = k // 4, k % 4
                yield n + 1 + k
                act.wait_ge(g["hm_proj"], k + 1)
                if k == 8:
                    act.wait_ge(g["hm_vtr"], 4)
                dst = (xvT, xqT, xkT)[which]
                bias = (w["xb"][:, 2], bq8, w["xb"][:, 1])[which]
                for hp in range(2):
                    for o in range(2):
                        h = 4 * quad + 2 * hp + o
                        nc.scalar.activation(dst[0:XD, :, 8 * h:8 * h + 8].rearrange("p (j a) u -> p j a u", a=2),
                                             bankA[k % 2][o * XD:(o + 1) * XD, hp * S:(hp + 1) * S].rearrange("p (a u j) -> p j a u", a=2, j=NJ),
                                             ACT.Identity, bias=bias[:, h:h + 1],
                                             scale=(XD ** -0.5 if which == 1 else 1.0)).then_inc(g["hm_ev"], 1)
                if 4 <= k < 8:
                    v = k - 4
                    act.wait_ge(g["hm_vtr"], v + 1)
                    nc.scalar.activation(xv[:, 8 * v:8 * v + 8, :].rearrange("p g c -> p (g c)"), bankA[2 + v % 2][:], ACT.Copy).then_inc(g["hm_vev"], 1)
            n += 13
            yield n
            n += 1
            for s in range(QUADS + 3):
                yield n + s
                if 2 <= s < QUADS + 2:
                    q = s - 2
                    act.wait_ge(g["hm_tr"], q + 1)
                    if q >= 2:
                        act.wait_ge(g["hm_o"], q - 1)
                    nc.scalar.activation(xpt[:, q % 2].rearrange("p g c -> p (g c)"), bankA[2][:], ACT.Copy).then_inc(g["hm_pt"], 1)
                if s < QUADS:
                    act.wait_ge(g["hm_nm"], s + 1)
                    if s >= 2:
                        act.wait_ge(g["hm_pn"], s - 1)
                    for i in range(4):
                        c = 4 * s + i
                        nc.scalar.activation(xp[:, s % 2, i, :], bankA[s % 2][:, i * P:(i + 1) * P], ACT.Exp,
                                             bias=xnm[:, c:c + 1], accum_out=xrs[:, c:c + 1]).then_inc(g["hm_ex"], 1)
                if s >= 3:
                    q = s - 3
                    act.wait_ge(g["hm_o"], q + 1)
                    for uh in range(2):
                        a = nc.scalar.activation(xot[:, q, :, uh, :], bankA[3][:, uh * P:(uh + 1) * P].rearrange("p (h u) -> p h u", u=8), ACT.Copy)
                    a.then_inc(g["hm_ot"], 1)
            n += QUADS + 3
            n += 1
            yield n
            ln_act(act, 2, lnA, bankA[1])
            yield n + 1
            act.wait_ge(g["md_sps"], 1)
            nc.scalar.activation(srow[:], bankA[2][:, 0:S], ACT.Copy).then_inc(g["md_srow"], 1)
            yield n + 2
            act.wait_ge(g["md_e"], 2)
            nc.scalar.activation(gate[:], scol[:], ACT.Exp, scale=-1.0).then_inc(g["md_gate"], 1)
            yield n + 3
            act.wait_ge(g["md_sel"], 1)
            nc.scalar.activation(selT[:].rearrange("p d c -> p (d c)"), bankA[0][:, 0:D], ACT.Copy).then_inc(g["md_selT"], 1)
            act.wait_ge(g["md_ptr"], 1)
            nc.scalar.activation(pickT[:].rearrange("p d c -> p (d c)"), bankA[3][:, 0:D], ACT.Copy).then_inc(g["md_pickT"], 1)
            yield n + 4
            for k in range(2):
                act.wait_ge(g["md_h"], k + 1)
                for f in range(4):
                    nc.scalar.activation(hid[:, 4 * k + f, :], bankA[1 + k][:, f * P:(f + 1) * P], ACT.Gelu_apprx_tanh,
                                         bias=w["b1"][:, 4 * k + f:4 * k + f + 1]).then_inc(g["md_hid"], 1)
            yield n + 5
            act.wait_ge(g["md_y"], 1)
            nc.scalar.activation(yff[:], bankA[0][:, 0:D], ACT.Copy).then_inc(g["md_yff"], 1)
            yield n + 7

        def vector_a(dve):
            b = bufA
            link = chain(dve, "dveA")
            yield 0
            ln_dve(dve, 0, xa, lnA, [(g["x_in"], 16)])
            ln_dve2(dve, 0, xa, lnA)
            for h in range(HS):
                yield 3 + h
                if h < H:
                    dve.wait_ge(g["mla_s"], h + 1)
                    nc.vector.tensor_reduce(b["nm"][:, h, :], bankA[h % 2][:].rearrange("p (t s) -> p t s", t=NT), AX.X, ALU.max,
                                            negate=True).then_inc(g["mla_nm"], 1)
            yield 3 + HS
            at_out_dve(dve, "mla", b, bankA[0:2])
            yield 5 + HS
            dve.wait_ge(g["mla_y"], 1)
            nc.vector.tensor_tensor(x1[:].rearrange("p t d -> p (t d)"), bankA[3][:], xa[:].rearrange("p t d -> p (t d)"), ALU.add).then_inc(g["mla_x"], 1)
            n = 6 + HS
            yield n
            ln_dve(dve, 1, x1, lnA, [(g["mla_x"], 1)])
            ln_dve2(dve, 1, x1, lnA)
            n += 14
            for s in range(QUADS + 3):
                yield n + s
                if s < QUADS:
                    dve.wait_ge(g["hm_s"], s + 1)
                    nc.vector.tensor_reduce(xnm[:, 4 * s:4 * s + 4], bankA[s % 2][:].rearrange("p (i c) -> p i c", i=4), AX.X, ALU.max,
                                            negate=True).then_inc(g["hm_nm"], 1)
                if 1 <= s <= QUADS:
                    q = s - 1
                    dve.wait_ge(g["hm_ex"], 4 * q + 4)
                    nc.vector.reciprocal(xrr[:, 4 * q:4 * q + 4], xrs[:, 4 * q:4 * q + 4]).then_inc(g["hm_rr"], 1)
            n += QUADS + 3
            yield n
            dve.wait_ge(g["hm_y"], 1)
            dve.wait_ge(g["hm_xb"], 1)
            nc.vector.tensor_tensor(x2[:].rearrange("p t d -> p (t d)"), bankA[0][:], xh[:].rearrange("p t d -> p (t d)"), ALU.add).then_inc(g["hm_x2"], 1)
            n += 1
            yield n
            ln_dve(dve, 2, x2, lnA, [(g["hm_x2"], 1)])
            ln_dve2(dve, 2, x2, lnA)
            yield n + 2
            dve.wait_ge(g["md_srow"], 1)
            for t in range(NT):
                link(nc.vector.tensor_tensor(tmpd[:, t, 0:P], srow[:, t * P:(t + 1) * P], w["ident"][:], ALU.mult))
            for t in range(NT):
                nc.vector.tensor_reduce(scol[:, t:t + 1], tmpd[:, t, 0:P], AX.X, ALU.add).then_inc(g["md_e"], 1)
            dve.wait_ge(g["md_e"], 2)
            for t in range(NT):
                link(nc.vector.tensor_scalar(tmpd[:, t, :], srow[:], scol[:, t:t + 1], None, ALU.is_equal))
            for t in range(NT):
                link(nc.vector.tensor_tensor(tmpd[:, t, :], tmpd[:, t, :], w["lower"][:, t, :], ALU.mult))
            for t in range(NT):
                link(nc.vector.scalar_tensor_tensor(tmpd[:, t, :], srow[:], scol[:, t:t + 1], tmpd[:, t, :], ALU.is_gt, ALU.add))
            for t in range(NT):
                nc.vector.tensor_reduce(rank[:, t:t + 1], tmpd[:, t, :], AX.X, ALU.add).then_inc(g["md_e"], 1)
            dve.wait_ge(g["md_e"], 4)
            for t in range(NT):
                nc.vector.tensor_scalar(pick[:, t, :], w["iota"][:, 0:CAP], rank[:, t:t + 1], None, ALU.is_equal).then_inc(g["md_e"], 1)
            dve.wait_ge(g["md_gate"], 1)
            nc.vector.tensor_scalar(gate1[:], gate[:], 1.0, None, ALU.add).then_inc(g["md_e"], 1)
            dve.wait_ge(g["md_e"], 7)
            nc.vector.reciprocal(gate2[:], gate1[:]).then_inc(g["md_e"], 1)
            yield n + 6
            dve.wait_ge(g["md_u"], 1)
            dve.wait_ge(g["md_xh"], 1)
            dve.wait_ge(g["md_e"], 8)
            if waits_b():
                dve.wait_ge(g["spa_x"], 1)
            for t in range(NT):
                nc.vector.scalar_tensor_tensor(x3[:, t, :], bankA[3][:, t * D:(t + 1) * D], gate2[:, t:t + 1], xh[:, t, :],
                                               ALU.mult, ALU.add).then_inc(g["md_x3"], 1)
            yield n + 7

        def pool_a(pool):
            b = bufA
            yield 0
            ln_pool(pool, 0, lnA)
            yield 2
            pool.wait_ge(g["mla_qT"], 1)
            for c in range(H // 2):
                at_mask_q(pool, "mla", b, c)
            n = 6 + HS
            yield n
            ln_pool(pool, 1, lnA)
            pool.wait_ge(g["ln1_xn"], 2)
            nc.gpsimd.tensor_tensor(xh[:], x1[:], w["xbo"][:].unsqueeze(1).broadcast_to([P, NT, D]), ALU.add).then_inc(g["hm_xb"], 1)
            n += 14
            for s in range(QUADS + 3):
                yield n + s
                if 1 <= s <= QUADS:
                    q = s - 1
                    pool.wait_ge(g["hm_rr"], q + 1)
                    if q >= 2:
                        pool.wait_ge(g["hm_tr"], q - 1)
                    nc.gpsimd.tensor_tensor(xpn[:, q % 2], xp[:, q % 2],
                                            xrr[:, 4 * q:4 * q + 4].unsqueeze(2).broadcast_to([P, 4, P]), ALU.mult).then_inc(g["hm_pn"], 1)
            n += QUADS + 3
            n += 1
            yield n
            ln_pool(pool, 2, lnA)
            pool.wait_ge(g["ln2_xn"], 2)
            nc.gpsimd.tensor_tensor(xh[:], x2[:], lnA["xn"][:], ALU.add).then_inc(g["md_xh"], 1)
            yield n + 7

        BS = H + 4
        C0 = 3 + BS + 3
        L0 = C0 + 2 + HS + 3

        def tensor_b(pe):
            b = bufB
            yield 0
            ln_pe(pe, 3, lnB, bankB[0])
            yield 1
            pe.wait_ge(g["ln3_xT"], 1)
            project_T(bankB[1], w["swk"], lnB["xT"], g["spa_k"])
            project_T(bankB[0], w["swq"], lnB["xT"], g["spa_q"])
            project_N(bankB[2], lnB["xT"], w["swv"], g["spa_v"])
            yield 2
            pe.wait_ge(g["spa_kT"], 2)
            pe.wait_ge(g["spa_qT"], 2)
            pe.wait_ge(g["spa_va"], 1)
            for s in range(BS):
                yield 3 + s
                if s < H:
                    at_scores(pe, "spa", b, bankB[s % 2], s, g["sp_sc"], 1)
                if 3 <= s < H + 3:
                    at_transpose(pe, "spa", b, bankB[2], s - 3)
                if s >= 4:
                    at_values(pe, "spa", b, bankB[3], s - 4)
            yield 3 + BS
            at_out_pe1(pe, "spa", b, bankB[0:2])
            yield 4 + BS
            at_out_pe2(pe, "spa", b, bankB[2])
            yield 5 + BS
            pe.wait_ge(g["spa_onT"], 1)
            project_N(bankB[3], b["onT"], w["swo"], g["spa_y"])
            yield C0
            pe.wait_ge(g["ctxB_in"], 16)
            project_T(bankB[1], w["cwk"], ctxB, g["crs_k"])
            project_N(bankB[2], ctxB, w["cwv"], g["crs_v"])
            ln_pe(pe, 4, lnB, bankB[0])
            yield C0 + 1
            pe.wait_ge(g["ln4_xT"], 1)
            project_T(bankB[0], w["cwq"], lnB["xT"], g["crs_q"])
            pe.wait_ge(g["crs_kT"], 1)
            pe.wait_ge(g["crs_qT"], 1)
            pe.wait_ge(g["crs_va"], 1)
            pe.wait_ge(g["mask_row"], 1)
            for h in range(HS):
                yield C0 + 2 + h
                if h < H:
                    at_scores(pe, "crs", b, bankB[h % 2], h, g["crs_ex"], NT, masked=True)
                if 1 <= h <= H:
                    at_transpose(pe, "crs", b, bankB[2], h - 1)
                if h >= 2:
                    at_values(pe, "crs", b, bankB[3], h - 2)
            yield C0 + 2 + HS
            at_out_pe1(pe, "crs", b, bankB[0:2])
            at_out_pe2(pe, "crs", b, bankB[2])
            pe.wait_ge(g["crs_onT"], 1)
            project_N(bankB[3], b["onT"], w["cwo"], g["crs_y"])
            yield L0
            ln_pe(pe, 5, lnB, bankB[0])
            pe.wait_ge(g["ln5_xT"], 1)
            project_N(bankB[1], lnB["xT"], weff, g["lin_y"])
            yield L0 + 1

        def scalar_b(act):
            b = bufB
            yield 0
            ln_act(act, 3, lnB, bankB[0])
            yield 1
            for n, bank, dst, bias in (("spa_k", bankB[1], "kT", "sbk"), ("spa_q", bankB[0], "qT", "sbq")):
                act.wait_ge(g[n], 1)
                for e in range(ND):
                    nc.scalar.activation(b[dst][:, e, :], bank[:, e * S:(e + 1) * S], ACT.Identity,
                                         bias=w[bias][:, e:e + 1]).then_inc(g["spa_" + dst], 1)
            for s in range(BS):
                yield 3 + s
                if s < H:
                    act.wait_ge(g["spa_s"], s + 1)
                    if s >= 3:
                        act.wait_ge(g["sp_mul"], s - 2)
                    nc.scalar.activation(sc[:, s % 3].rearrange("p t s -> p (t s)"), bankB[s % 2][:], ACT.Copy).then_inc(g["sp_sc"], 1)
                if 3 <= s < H + 3:
                    h = s - 3
                    act.wait_ge(g["sp_mul"], h + 1)
                    act.wait_ge(g["spa_nm"], h + 1)
                    for t in range(NT):
                        nc.scalar.activation(b["pr"][:, h % 2, t, :], sp_[:, h % 2, t, :], ACT.Exp,
                                             bias=b["nm"][:, h, t:t + 1]).then_inc(g["spa_ex"], 1)
                    at_copy_pt(act, "spa", b, bankB[2], h)
                if 2 <= s < H + 2:
                    h = s - 2
                    act.wait_ge(g["sp_top"], h + 1)
                    if h >= 2:
                        act.wait_ge(g["spa_tr"], h - 1)
                    nc.scalar.activation(taken[:, h % 2].rearrange("p t s -> p (t s)"), wk[:, h % 2].rearrange("p t s -> p (t s)"),
                                         ACT.Relu, bias=-1.0, scale=-2.0 / BIG).then_inc(g["sp_tk"], 1)
                if s == 12:
                    at_copy_ot(act, "spa", b, bankB[3], 0)
            yield 3 + BS
            at_copy_ot(act, "spa", b, bankB[3], 1)
            yield 4 + BS
            at_out_act(act, "spa", b, bankB[2])
            yield C0
            act.wait_ge(g["crs_k"], 1)
            nc.scalar.activation(b["kT"][:].rearrange("p e s -> p (e s)"), bankB[1][:], ACT.Copy).then_inc(g["crs_kT"], 1)
            act.wait_ge(g["crs_v"], 1)
            nc.scalar.activation(b["va"][:, :, :, 0:HD], bankB[2][:].rearrange("p (t h c) -> p t h c", t=NT, c=HD),
                                 ACT.Copy).then_inc(g["crs_va"], 1)
            ln_act(act, 4, lnB, bankB[0])
            yield C0 + 1
            act.wait_ge(g["crs_q"], 1)
            nc.scalar.activation(b["qT"][:].rearrange("p e s -> p (e s)"), bankB[0][:], ACT.Copy).then_inc(g["crs_qT"], 1)
            for h in range(HS):
                yield C0 + 2 + h
                if 1 <= h <= H:
                    at_copy_pt(act, "crs", b, bankB[2], h - 1)
                if h < H:
                    exps(act, "crs", b, bankB[h % 2], h)
                if h == 10:
                    at_copy_ot(act, "crs", b, bankB[3], 0)
            yield C0 + 2 + HS
            at_copy_ot(act, "crs", b, bankB[3], 1)
            at_out_act(act, "crs", b, bankB[2])
            yield L0
            ln_act(act, 5, lnB, bankB[0])
            yield L0 + 1

        def vector_b(dve):
            b = bufB
            link = chain(dve, "dveB")
            yield 0
            ln_dve(dve, 3, x3, lnB, [])
            ln_dve2(dve, 3, x3, lnB)
            yield 1
            dve.wait_ge(g["spa_v"], 1)
            nc.vector.tensor_tensor(b["va"][:, :, :, 0:HD], bankB[2][:].rearrange("p (t h c) -> p t h c", t=NT, c=HD),
                                    w["sbv"][:].rearrange("p (h c) -> p h c", c=HD).unsqueeze(1).broadcast_to([P, NT, H, HD]),
                                    ALU.add).then_inc(g["spa_va"], 1)
            for s in range(BS):
                if 1 <= s <= H:
                    h = s - 1
                    k = h % 2
                    yield 3 + s
                    dve.wait_ge(g["sp_sc"], h + 1)
                    if h >= 2:
                        dve.wait_ge(g["sp_tk"], h - 1)
                        dve.wait_ge(g["sp_nm"], h - 1)
                    src = sc[:, h % 3]
                    n0 = link.n
                    for r in range(ROUNDS):
                        for t in range(NT):
                            if r:
                                link.wait(n0 + 2 * NT * r - NT + 1 + t)
                            link.inc(nc.vector.max(m8[:, k, r, t, :], src[:, t, :]))
                        if r == ROUNDS - 1:
                            link.wait(link.n)
                            link.inc(nc.vector.memset(m8[:, k, r, :, 1:8], -BIG))
                        for t in range(NT):
                            link.wait(link.n if r == ROUNDS - 1 else n0 + 2 * NT * r + 1 + t)
                            m = nc.vector.match_replace(out=wk[:, k, t, :], in_to_replace=m8[:, k, r, t, :], in_values=src[:, t, :],
                                                        imm_value=-BIG)
                            if r == ROUNDS - 1 and t == NT - 1:
                                m.then_inc(g["sp_top"], 1)
                            elif r == ROUNDS - 1:
                                link.inc(m)
                            else:
                                link.inc(m)
                        src = wk[:, k]
            yield 3 + BS
            at_out_dve(dve, "spa", b, bankB[0:2])
            yield 5 + BS
            dve.wait_ge(g["spa_y"], 1)
            dve.wait_ge(g["sp_xb"], 1)
            nc.vector.tensor_tensor(x4[:].rearrange("p t d -> p (t d)"), bankB[3][:], x3[:].rearrange("p t d -> p (t d)"), ALU.add).then_inc(g["spa_x"], 1)
            yield C0
            dve.wait_ge(g["len_in"], 16)
            link(nc.vector.tensor_copy(lenf[:], lenb[:]))
            nc.vector.tensor_scalar(mrow[:], w["iota"][0:1, :].unsqueeze(1).broadcast_to([1, NT, S]), lenf[:, 0:1], NEG,
                                    ALU.is_ge, ALU.mult).then_inc(g["mask_row"], 1)
            ln_dve(dve, 4, x4, lnB, [(g["spa_x"], 1)])
            ln_dve2(dve, 4, x4, lnB)
            for h in range(HS):
                yield C0 + 2 + h
                if h < H:
                    dve.wait_ge(g["crs_s"], h + 1)
                    nc.vector.tensor_reduce(b["nm"][:, h, :], bankB[h % 2][:].rearrange("p (t s) -> p t s", t=NT), AX.X, ALU.max,
                                            negate=True).then_inc(g["crs_nm"], 1)
            yield C0 + 2 + HS
            at_out_dve(dve, "crs", b, bankB[0:2])
            dve.wait_ge(g["crs_y"], 1)
            nc.vector.tensor_tensor(x5[:].rearrange("p t d -> p (t d)"), bankB[3][:], x4[:].rearrange("p t d -> p (t d)"), ALU.add).then_inc(g["crs_x"], 1)
            yield L0
            ln_dve(dve, 5, x5, lnB, [(g["crs_x"], 1)])
            ln_dve2(dve, 5, x5, lnB)
            dve.wait_ge(g["lin_y"], 1)
            dve.wait_ge(g["lin_xb"], 1)
            nc.vector.tensor_tensor(xo[:].rearrange("p t d -> p (t d)"), bankB[1][:], xo[:].rearrange("p t d -> p (t d)"), ALU.add).then_inc(g["lin_o"], 1)
            yield L0 + 1

        def pool_b(pool):
            b = bufB
            yield 0
            ln_pool(pool, 3, lnB)
            pool.wait_ge(g["ln3_xn"], 2)
            nc.gpsimd.tensor_tensor(x3[:], x3[:], w["sbo"][:].unsqueeze(1).broadcast_to([P, NT, D]), ALU.add).then_inc(g["sp_xb"], 1)
            yield 1
            pool.wait_ge(g["spa_qT"], 2)
            for c in range(QR // 2):
                at_mask_q(pool, "spa", b, c)
            for s in range(BS):
                yield 3 + s
                at_mask_later(pool, "spa", b, s)
                if 2 <= s < H + 2:
                    h = s - 2
                    pool.wait_ge(g["sp_top"], h + 1)
                    nc.gpsimd.tensor_scalar(mx0[:, h, :], m8[:, h % 2, 0, :, 0], 0.0, -1.0, ALU.max, ALU.mult).then_inc(g["sp_nm"], 1)
                    pool.wait_ge(g["sp_nm"], h + 1)
                    nc.gpsimd.tensor_copy(b["nm"][:, h, :], mx0[:, h, :]).then_inc(g["spa_nm"], 1)
                    pool.wait_ge(g["sp_tk"], h + 1)
                    nc.gpsimd.tensor_tensor(sp_[:, h % 2], taken[:, h % 2], sc[:, h % 3], ALU.mult).then_inc(g["sp_mul"], 1)
            yield C0
            ln_pool(pool, 4, lnB)
            yield C0 + 1
            pool.wait_ge(g["crs_qT"], 1)
            for c in range(QR // 2):
                at_mask_q(pool, "crs", b, c)
            for h in range(HS):
                yield C0 + 2 + h
                at_mask_later(pool, "crs", b, h)
            yield L0
            ln_pool(pool, 5, lnB)
            pool.wait_ge(g["ln5_xn"], 2)
            nc.gpsimd.tensor_tensor(xo[:], x5[:], w["fbias"][:].unsqueeze(1).broadcast_to([P, NT, D]), ALU.add).then_inc(g["lin_xb"], 1)
            yield L0 + 1

        NA, NB = 6 + HS + 14 + QUADS + 3 + 1 + 8, L0 + 2
        mode = {"both": True}

        def waits_b():
            return mode["both"]

        def chain(eng, name):
            def link(ins):
                link.inc(ins)
                link.wait(link.n)

            def inc(ins):
                link.n += 1
                ins.then_inc(g[name], 1)
                return ins

            def wait(v):
                eng.wait_ge(g[name], v)
            link.n = 0
            link.inc = inc
            link.wait = wait
            return link

        def merged(a, b):
            ka = next(a) / NA if a else 2.0
            kb = next(b) / NB if b else 2.0
            while a or b:
                if ka <= kb:
                    v = next(a, None)
                    a, ka = (a, v / NA) if v is not None else (None, 2.0)
                else:
                    v = next(b, None)
                    b, kb = (b, v / NB) if v is not None else (None, 2.0)

        def one_pass(ia, ib):
            mode["both"] = ia is not None and ib is not None
            A, Bs = ia is not None, ib is not None
            with nc.Block() as block:
                @block.sync
                def _(sp):
                    if A:
                        sp.dma_start(xa[:], x_in[ia]).then_inc(g["x_in"], 16)
                    if Bs:
                        sp.dma_start(lenb[:], lens_in[ib]).then_inc(g["len_in"], 16)
                        sp.dma_start(ctxB[:], ctx_in[ib]).then_inc(g["ctxB_in"], 16)
                    if A:
                        sp.dma_start(ctxA[:], ctx_in[ia]).then_inc(g["ctxA_in"], 16)
                    if A:
                        sp.wait_ge(g["mla_onT"], 1)
                        sp.dma_start(xq_area[XD:XD + 8, :], w_in["groupq"]).then_inc(g["group_in"], 16)
                        sp.dma_start(vT_qm[XD:XD + 8, :], w_in["groupk"]).then_inc(g["group_in"], 16)
                    if Bs:
                        sp.wait_ge(g["lin_o"], 1)
                        sp.dma_start(out[ib], xo[:]).then_inc(g["x_stored"], 16)
                        sp.wait_ge(g["x_stored"], 16)

                @block.tensor
                def _(pe):
                    merged(tensor_a(pe) if A else None, tensor_b(pe) if Bs else None)

                @block.scalar
                def _(act):
                    merged(scalar_a(act) if A else None, scalar_b(act) if Bs else None)

                @block.vector
                def _(dve):
                    merged(vector_a(dve) if A else None, vector_b(dve) if Bs else None)

                @block.gpsimd
                def _(pool):
                    merged(pool_a(pool) if A else None, pool_b(pool) if Bs else None)

            with nc.Block() as block:
                @block.sync
                def _(sp):
                    for s in used:
                        sp.sem_clear(s)

        nb = out.shape[0]
        one_pass(0, None)
        if nb > 1:
            with nc.Fori(0, nb - 1) as i:
                one_pass(i + 1, i)
        one_pass(None, nb - 1)


def layouts(inp):
    c = lambda a: np.ascontiguousarray(a)
    f = np.float32
    i = {k: np.asarray(v) for k, v in inp.items()}
    rows = lambda a, n=P: c(a.reshape(a.shape[0] // n, n, a.shape[1]).transpose(1, 0, 2))
    swap = np.arange(D) ^ 1
    head = np.arange(H, dtype=f)[:, None]
    inv = f(1.0) / f(10000.0) ** (np.arange(0, HD, 2, dtype=f) / f(HD))
    ang = (head * inv[None, :]).astype(f)
    cos, sin = (np.repeat(t(ang).astype(f), 2, 1).reshape(1, D) for t in (np.cos, np.sin))
    p = np.arange(P)
    ropec = np.repeat(cos, P, 0)
    ropes = np.repeat(sin * np.where(np.arange(D) % 2 == 0, -1.0, 1.0)[None, :], P, 0)
    padrow = lambda a, top: np.concatenate([a, np.zeros((P - a.shape[0], a.shape[1]), f)][:: 1 if top else -1], 0)
    wide = lambda v: c(np.broadcast_to(v[None, :], (P, v.shape[0])))
    cols = lambda v, n=P: c(v.reshape(-1, n).T)
    u8 = np.tile(np.arange(8), 2 * NJ * H)
    onehot = (u8[None, :] == np.arange(8)[:, None]).astype(f)
    tok = p[:, None] + P * np.arange(NT)[None, :]
    w = {
        "wq0": rows(i["L0_attn_wq"].T), "wq0s": rows(i["L0_attn_wq"].T[:, swap]),
        "wlat": rows(np.concatenate([i["L0_attn_wk_a"].T, i["L0_attn_wv_a"].T], 1)),
        "wkb": padrow(i["L0_attn_wk_b"].T, True), "wkbs": padrow(i["L0_attn_wk_b"].T[:, swap], True),
        "wvb": padrow(i["L0_attn_wv_b"].T, False), "wo0": rows(i["L0_attn_wo"].T),
        "ropec": ropec, "ropes": ropes, "hmask": 0.25 * (p[:, None] // HD == np.arange(HT)[None, :]),
        "xwq": rows(i["L0_xattn_Wq"].T), "xwk": rows(i["L0_xattn_Wk"].T), "xwv": rows(i["L0_xattn_Wv"].T),
        "xwo": rows(i["L0_xattn_Wo"].T),
        "xb": np.stack([cols(i["L0_xattn_b" + k], XD) for k in "qkv"], 1), "xbo": wide(i["L0_xattn_bo"]),
        "wrt": rows(np.repeat(i["L0_ffn_w_router"][:, None], P, 1)),
        "w1": rows(i["L0_ffn_W1"]), "b1": cols(i["L0_ffn_b1"]), "w2": rows(i["L0_ffn_W2"]), "b2": i["L0_ffn_b2"][None, :],
        "swq": rows(i["L1_attn_Wq"]), "swk": rows(i["L1_attn_Wk"]), "swv": rows(i["L1_attn_Wv"]), "swo": rows(i["L1_attn_Wo"]),
        "sbq": cols(i["L1_attn_bq"]), "sbk": cols(i["L1_attn_bk"]), "sbv": wide(i["L1_attn_bv"]), "sbo": wide(i["L1_attn_bo"]),
        "cwq": rows(i["L1_xattn_Wq"]), "cwk": rows(i["L1_xattn_Wk"]), "cwv": rows(i["L1_xattn_Wv"]), "cwo": rows(i["L1_xattn_Wo"]),
        "wt": rows(i["L1_ffn_weight"].T), "alpha": c(np.broadcast_to(i["L1_ffn_alpha"][None, :], (P, 1))), "fbias": wide(i["L1_ffn_bias"]),
        "ident": np.eye(P), "iota": np.broadcast_to(np.arange(S)[None, :], (P, S)),
        "lower": np.arange(S)[None, None, :] < tok[:, :, None],
        "groupq": onehot, "groupk": -FAR * (1 - onehot),
    }
    w = {k: c(v if v.dtype == f else v.astype(f)) for k, v in w.items()}
    x = c(i["x"].reshape(-1, NT, P, D).transpose(0, 2, 1, 3))
    ctx = c(i["ctx_1024"].reshape(-1, S, ND, P).transpose(0, 3, 2, 1))
    return w, x, ctx, c(i["_lenS2"].reshape(-1, 1, 1))


def declare(nc, nb):
    ext = lambda n, s, dt, k="ExternalInput": nc.dram_tensor(n, tuple(s), dt, kind=k).ap()
    w_in = {n: ext("w_" + n, s, F32) for n, s in WEIGHTS.items()}
    x_in = ext("x_in", (nb, P, NT, D), F32)
    ctx_in = ext("ctx_in", (nb, P, ND, S), F32)
    lens_in = ext("lens_in", (nb, 1, 1), I32)
    out = ext("out", (nb, P, NT, D), F32, "ExternalOutput")
    program(nc, x_in, ctx_in, lens_in, w_in, out)


def kernel(**inputs):
    import concourse.bacc as bacc
    from concourse.bass_utils import run_bass_kernel_spmd
    w, x, ctx, lens = layouts(inputs)
    arrays = {"w_" + k: v for k, v in w.items()}
    arrays.update(x_in=x, ctx_in=ctx, lens_in=lens)
    nc = bacc.Bacc("TRN2", target_bir_lowering=False, num_devices=1)
    declare(nc, B)
    r = run_bass_kernel_spmd(nc, [arrays], core_ids=[0])
    y = r.results[0]["out"]
    return np.ascontiguousarray(y.transpose(0, 2, 1, 3).reshape(B, S, D))
```

```python
import numpy as np
import concourse.bass as bass
from concourse import mybir
from contextlib import ExitStack

F32 = mybir.dt.float32
BF16 = mybir.dt.bfloat16
I32 = mybir.dt.int32
ALU = mybir.AluOpType
ACT = mybir.ActivationFunctionType
AX = mybir.AxisListType

P = 128
B, S, D = 32, 256, 256
H, HD = 16, 16
XD = 64
FF = 1024
NT = S // P
ND = D // P
HT = P // HD
QR = 8
KEEP = int(S * (1.0 - 0.9))
CAP = S // 2
NJ, NU = 16, 16
QUADS = NJ // 2
EPS = 1e-5
BIG = 2.0 ** 100
FAR = 2.0 ** 100
NEG = -4.0e20
ROUNDS = (KEEP + 7) // 8
assert KEEP % 8 == 1 and ROUNDS == 4

WEIGHTS = {
    "wq0": [P, ND, D], "wq0s": [P, ND, D], "wlat": [P, ND, P], "wkb": [P, D], "wkbs": [P, D],
    "ropec": [P, D], "ropes": [P, D], "ident": [P, P], "wvb": [P, D], "wo0": [P, ND, D], "hmask": [P, HT],
    "xwq": [P, ND, H * XD], "xwk": [P, ND, H * XD], "xwv": [P, ND, H * XD], "xwo": [P, 8, D],
    "xb": [XD, 3, H], "xbo": [P, D], "wrt": [P, ND, P], "w1": [P, ND, FF], "b1": [P, FF // P],
    "w2": [P, FF // P, D], "b2": [1, D],
    "swq": [P, ND, D], "swk": [P, ND, D], "swv": [P, ND, D], "swo": [P, ND, D],
    "sbq": [P, ND], "sbk": [P, ND], "sbv": [P, D], "sbo": [P, D],
    "cwq": [P, ND, D], "cwk": [P, ND, D], "cwv": [P, ND, D], "cwo": [P, ND, D],
    "wt": [P, ND, D], "alpha": [P, 1], "fbias": [P, D],
    "lower": [P, NT, S], "iota": [P, S], "groupq": [8, NJ * H * NU], "groupk": [8, NJ * H * NU],
}


FIRST = list(WEIGHTS)[:11]


def program(nc, x_in, ctx_in, lens_in, w_in, out):
    es = ExitStack()
    with es:
        def sb(name, shape, dt=F32):
            return es.enter_context(nc.sbuf_tensor(name, shape, dt))

        def sem(name):
            return es.enter_context(nc.semaphore(name))

        skip = ("groupq", "groupk", "wt", "wq0s", "wkbs", "ropec", "ropes")
        w = {n: sb(n, shape) for n, shape in WEIGHTS.items() if n not in skip}
        weff = sb("weff", [P, ND, D])
        ones = sb("ones", [P, P])
        ones_b = sb("ones_b", [1, P], BF16)
        half_neg = sb("half_neg", [P, NT])
        bq8 = sb("bq8", [XD, H])
        tern = sb("tern", [P, 4])

        bankA = [es.enter_context(nc.psum_tensor(f"bankA{i}", [P, 512], F32)) for i in range(4)]
        bankB = [es.enter_context(nc.psum_tensor(f"bankB{i}", [P, 512], F32)) for i in range(4)]

        xin = sb("xin", [P, NT, D])
        xa = sb("xa", [P, NT, D])
        x1 = x2 = xa
        x3 = sb("x3", [P, NT, D])
        x3b = sb("x3b", [P, NT, D])
        ctxA = sb("ctxA", [P, ND, S])
        ctxB = sb("ctxB", [P, ND, S])

        def attention_buffers(p, qm, pr, pt, ot, onT, kq):
            kT, qT = (kq[:, 512 * k:512 * k + 512].rearrange("p (e s) -> p e s", e=ND) for k in range(2))
            return dict(
                p=p, qm=qm, kT=kT, va=sb(p + "va", [P, NT, H, 2 * HD]),
                qr=qm.shape[1], nm=sb(p + "nm", [P, H, NT]), pr=pr, pt=pt, ot=ot, rd=sb(p + "rd", [P, 2, NT, HT]), on=qT, onT=onT, qT=qT)

        vT_qm = sb("vT_qm", [P, NJ * H * NU])
        xq_area = sb("xq_area", [P, NJ * H * NU])
        part = lambda k: xq_area[:, 1024 * k:1024 * (k + 1)]
        lnA = dict(st=sb("lnA_st", [P, NT, 6]), mv=sb("lnA_mv", [P, NT, 2]), rs=sb("lnA_rs", [P, NT]),
                   xn=sb("lnA_xn", [P, NT, D]), xT=sb("lnA_xT", [P, ND, S]))
        lnB = dict(st=sb("lnB_st", [P, NT, 6]), mv=sb("lnB_mv", [P, NT, 2]), rs=sb("lnB_rs", [P, NT]),
                   xn=sb("lnB_xn", [P, NT, D]), xT=sb("lnB_xT", [P, ND, S]))
        lnM = dict(st=sb("lnM_st", [P, NT, 6]), mv=sb("lnM_mv", [P, NT, 2]), rs=sb("lnM_rs", [P, NT]),
                   xn=part(3)[:, 0:512].rearrange("p (t d) -> p t d", t=NT), xT=part(3)[:, 512:1024].rearrange("p (d s) -> p d s", d=ND))
        a_kq = sb("a_kq", [P, 2 * ND * S])
        bufA = attention_buffers("a_", vT_qm[:, :].rearrange("p (h s) -> p h s", h=H),
                                 part(0).rearrange("p (k t s) -> p k t s", k=2, t=NT),
                                 part(1).rearrange("p (k t s) -> p k t s", k=2, t=NT),
                                 part(2).rearrange("p (c s) -> p c s", c=4), lnA["xT"], a_kq)
        bufB = attention_buffers("b_", sb("b_qm", [P, QR, S]), sb("b_pr", [P, 2, NT, S]), sb("b_pt", [P, 2, NT, S]),
                                 sb("b_ot", [P, 4, S]), lnB["xT"], sb("b_kq", [P, 2 * ND * S]))
        latT = lnM["xn"][:, 0, :]
        xqT = xq_area[0:XD + 8, :].rearrange("p (g h u) -> p g (h u)", g=2 * NJ, h=H)
        xkT = vT_qm[0:XD + 8, :].rearrange("p (g h u) -> p g (h u)", g=2 * NJ, h=H)
        xvT = vT_qm[0:XD, :].rearrange("p (g h u) -> p g (h u)", g=2 * NJ, h=H)
        xv = sb("xv", [P, 2 * NJ, XD])
        xnm = sb("xnm", [P, 2 * NJ])
        xrs = sb("xrs", [P, 2 * NJ])
        xrr = sb("xrr", [P, 2 * NJ])
        xp = sb("xp", [P, 2, 4, P])
        xpn = xp
        xpt = a_kq[:].rearrange("p (b i c) -> p b i c", b=2, i=4)
        xot = sb("xot", [P, QUADS, H, 2, 8])
        scol = sb("scol", [P, NT])
        srow = xv[:, 24:28, :].rearrange("p g c -> p (g c)")
        area = xv[:, :, :].rearrange("p g c -> p (g c)")
        tmpd = area[:, 0:512].rearrange("p (t s) -> p t s", t=NT)
        gt = sb("gt", [P, NT])
        eq = sb("eq", [P, NT])
        rank = sb("rank", [P, NT])
        gate = sb("gate", [P, NT])
        gate1 = sb("gate1", [P, NT])
        gate2 = sb("gate2", [P, NT])
        pick = area[:, 512:768].rearrange("p (t c) -> p t c", t=NT)
        pickT = area[:, 768:1024].rearrange("p (t c) -> p t c", t=NT)
        selT = area[:, 1024:1280].rearrange("p (t c) -> p t c", t=ND)
        yff = area[:, 1280:1536]
        hid = xot[:, 0:4].rearrange("p a h b c -> p (a h b c)").rearrange("p (f c) -> p f c", c=CAP)
        xh = xa
        sc = sb("sc", [P, 3, NT, S])
        wk = sb("wk", [P, 2, NT, S])
        m8 = sb("m8", [P, 2, ROUNDS, NT, 8])
        taken = bufB["pr"]
        sp_ = taken
        mx0 = sb("mx0", [P, H, NT])
        x4 = sb("x4", [P, NT, D])
        x5 = x4
        xo = x4
        lenb = sb("lenb", [1, 1], I32)
        lenf = sb("lenf", [1, 1])
        mrow = sb("mrow", [1, NT, S], BF16)

        w["wt"] = x4
        tern2 = x3
        w["wq0s"] = xq_area[:, 0:512].rearrange("p (e s) -> p e s", e=ND)
        w["wkbs"] = xq_area[:, 512:768]
        w["ropec"] = xq_area[:, 768:1024]
        w["ropes"] = xq_area[:, 1024:1280]

        s_w = sem("first_weights_loaded")
        s_w2 = sem("other_weights_loaded")
        s_set = sem("setup_done")
        s_sum = sem("weight_sum_ready")
        s_rope = sem("rotated")
        s_stored = sem("output_stored")
        others = []
        class Signals(dict):
            def __missing__(self, name):
                self[name] = sem(name)
                return self[name]

        g = Signals()

        with nc.Block() as block:
            @block.sync
            def _(sp):
                for n in FIRST:
                    sp.dma_start(w[n][:], w_in[n]).then_inc(s_w, 16)
                sp.dma_start(xin[:], x_in[0]).then_inc(g["x_in"], 16)
                for n in WEIGHTS:
                    if n in w and n not in FIRST:
                        sp.dma_start(w[n][:], w_in[n]).then_inc(s_w2, 16)
                        others.append(n)

            @block.vector
            def _(dve):
                nc.vector.memset(ones[:], 1.0).then_inc(s_set, 1)
                nc.vector.memset(ones_b[:], 1.0).then_inc(s_set, 1)
                nc.vector.memset(half_neg[:], -0.5).then_inc(s_set, 1)
                nc.vector.memset(bufA["va"][:], 1.0).then_inc(s_set, 1)
                nc.vector.memset(bufB["va"][:], 1.0).then_inc(s_set, 1)
                dve.wait_ge(s_w, 16 * len(FIRST))
                for wt, ws, wide in ((w["wq0"], w["wq0s"], True), (w["wkb"], w["wkbs"], False)):
                    cos, sin = w["ropec"][:], w["ropes"][:]
                    if wide:
                        cos, sin = (a.unsqueeze(1).broadcast_to([P, ND, D]) for a in (cos, sin))
                    nc.vector.tensor_tensor(wt[:], wt[:], cos, ALU.mult).then_inc(s_rope, 1)
                    nc.vector.tensor_tensor(ws[:], ws[:], sin, ALU.mult).then_inc(s_rope, 1)
                dve.wait_ge(s_rope, 4)
                nc.vector.tensor_tensor(w["wq0"][:], w["wq0"][:], w["wq0s"][:], ALU.add).then_inc(s_rope, 1)
                nc.vector.tensor_tensor(w["wkb"][:], w["wkb"][:], w["wkbs"][:], ALU.add).then_inc(s_rope, 1)
                dve.wait_ge(s_rope, 6)
                dve.wait_ge(s_set, 5)

        def setup_rest():
            n0 = 5
            with nc.Block() as block:
                @block.sync
                def _(sp):
                    sp.wait_ge(s_w2, 16 * len(others))

                @block.tensor
                def _(pe):
                    pe.wait_ge(s_set, n0 + 1)
                    nc.tensor.matmul(bankA[0][:, 0:1], ones[:], tern[:, 0:1], start=True, stop=True).then_inc(s_sum, 1)

                @block.vector
                def _(dve):
                    dve.wait_ge(s_w2, 16 * len(others))
                    nc.vector.tensor_reduce(tern[:, 0:1], w["wt"][:], AX.XY, ALU.add,
                                            apply_absolute_value=True).then_inc(s_set, 1)
                    nc.vector.tensor_scalar(bq8[:], w["xb"][:, 0, :], XD ** -0.5, None, ALU.mult).then_inc(s_set, 1)
                    dve.wait_ge(s_sum, 1)
                    nc.vector.tensor_scalar(tern[:, 1:2], bankA[0][:, 0:1], 1.0 / (D * D), 0.7, ALU.mult, ALU.mult).then_inc(s_set, 1)
                    nc.vector.tensor_scalar(tern[:, 2:3], bankA[0][:, 0:1], 1.0 / (D * D), -0.7, ALU.mult, ALU.mult).then_inc(s_set, 1)
                    dve.wait_ge(s_set, n0 + 4)
                    nc.vector.tensor_scalar(weff[:], w["wt"][:], tern[:, 1:2], w["alpha"][:, 0:1], ALU.is_gt, ALU.mult).then_inc(s_set, 1)
                    nc.vector.tensor_scalar(tern2[:], w["wt"][:], tern[:, 2:3], w["alpha"][:, 0:1], ALU.is_lt, ALU.mult).then_inc(s_set, 1)
                    dve.wait_ge(s_set, n0 + 6)
                    nc.vector.tensor_tensor(weff[:], weff[:], tern2[:], ALU.subtract).then_inc(s_set, 1)
                    dve.wait_ge(s_set, n0 + 7)

        def ln_dve(dve, k, x, ln, ready):
            for s, v in ready:
                dve.wait_ge(s, v)
            for t in range(NT):
                nc.vector.bn_stats(ln["st"][:, t, :], x[:, t, :]).then_inc(g[f"ln{k}_stat"], 1)
            dve.wait_ge(g[f"ln{k}_stat"], 2)
            for t in range(NT):
                nc.vector.bn_aggr(ln["mv"][:, t, :], ln["st"][:, t, :]).then_inc(g[f"ln{k}_stat"], 1)

        def ln_pool(pool, k, ln):
            pool.wait_ge(g[f"ln{k}_stat"], 4)
            nc.gpsimd.tensor_scalar(ln["rs"][:], ln["mv"][:, :, 1], EPS, 1.0, ALU.add, ALU.mult).then_inc(g[f"ln{k}_stat"], 1)
            pool.wait_ge(g[f"ln{k}_stat"], 5)
            nc.gpsimd.tensor_tensor(ln["rs"][:], ln["rs"][:], half_neg[:], ALU.pow).then_inc(g[f"ln{k}_rstd"], 1)

        def ln_dve2(dve, k, x, ln):
            dve.wait_ge(g[f"ln{k}_rstd"], 1)
            for t in range(NT):
                nc.vector.tensor_scalar(ln["xn"][:, t, :], x[:, t, :], ln["mv"][:, t, 0:1], ln["rs"][:, t:t + 1],
                                        ALU.subtract, ALU.mult).then_inc(g[f"ln{k}_xn"], 1)

        def ln_pe(pe, k, ln, bank):
            pe.wait_ge(g[f"ln{k}_xn"], 2)
            for d in range(ND):
                for t in range(NT):
                    last = nc.tensor.transpose(bank[:, d * S + t * P:d * S + (t + 1) * P],
                                               ln["xn"][:, t, d * P:(d + 1) * P], w["ident"][:])
            last.then_inc(g[f"ln{k}_tr"], 1)

        def ln_act(act, k, ln, bank):
            act.wait_ge(g[f"ln{k}_tr"], 1)
            nc.scalar.activation(ln["xT"][:].rearrange("p d s -> p (d s)"), bank[:], ACT.Copy).then_inc(g[f"ln{k}_xT"], 1)

        def project_T(bank, wt, xT, done):
            for e in range(ND):
                for d in range(ND):
                    last = nc.tensor.matmul(bank[:, e * S:(e + 1) * S], wt[:, d, e * P:(e + 1) * P], xT[:, d, :],
                                            start=(d == 0), stop=(d == ND - 1))
            last.then_inc(done, 1)

        def project_N(bank, xT, wt, done):
            for t in range(NT):
                for d in range(ND):
                    last = nc.tensor.matmul(bank[:, t * D:(t + 1) * D], xT[:, d, t * P:(t + 1) * P], wt[:, d, :],
                                            start=(d == 0), stop=(d == ND - 1))
            last.then_inc(done, 1)

        def at_scores(pe, n, b, bank, h, free, per, masked=False):
            pe.wait_ge(g[n + "_qm"], h // 2 + 1)
            if h >= 2:
                pe.wait_ge(free, per * (h - 1))
            if masked:
                nc.tensor.matmul(bank[:], ones_b[:], mrow[:].rearrange("p t s -> p (t s)"), start=True, stop=False,
                                 skip_group_check=True)
            for t in range(NT):
                last = nc.tensor.matmul(bank[:, t * S:(t + 1) * S], b["qm"][:, h % b["qr"], t * P:(t + 1) * P],
                                        b["kT"][:, h // HT, :], start=not masked, stop=True, skip_group_check=masked)
            last.then_inc(g[n + "_s"], 1)

        def at_transpose(pe, n, b, bank, h):
            pe.wait_ge(g[n + "_ex"], NT * (h + 1))
            if h >= 1:
                pe.wait_ge(g[n + "_pt"], h)
            for c in range(NT):
                for t in range(NT):
                    last = nc.tensor.transpose(bank[:, c * S + t * P:c * S + (t + 1) * P],
                                               b["pr"][:, h % 2, t, c * P:(c + 1) * P], w["ident"][:])
            last.then_inc(g[n + "_tr"], 1)

        def at_copy_pt(act, n, b, bank, h):
            act.wait_ge(g[n + "_tr"], h + 1)
            if h >= 2:
                act.wait_ge(g[n + "_pv"], h // 2)
            nc.scalar.activation(b["pt"][:, h % 2].rearrange("p c s -> p (c s)"), bank[:], ACT.Copy).then_inc(g[n + "_pt"], 1)

        def at_values(pe, n, b, bank, h):
            pe.wait_ge(g[n + "_pt"], h + 2)
            if h == 8:
                pe.wait_ge(g[n + "_ot"], 1)
            c = P * ((h // 2) % 4)
            for k in range(NT):
                for j in range(2):
                    for t in range(NT):
                        r = 32 * (2 * j + t)
                        last = nc.tensor.matmul(bank[r:r + 32, c:c + P], b["va"][:, k, h + j, :], b["pt"][:, j, k, t * P:(t + 1) * P],
                                                start=(k == 0), stop=(k == NT - 1))
            last.then_inc(g[n + "_pv"], 1)

        def at_copy_ot(act, n, b, bank, half):
            act.wait_ge(g[n + "_pv"], 4 * (half + 1))
            nc.scalar.activation(b["ot"][:, 2 * half:2 * half + 2].rearrange("p c s -> p (c s)"), bank[:], ACT.Copy).then_inc(g[n + "_ot"], 1)

        def at_out_pe1(pe, n, b, banks):
            pe.wait_ge(g[n + "_ot"], 2)
            for half in range(2):
                for q in range(4):
                    last = nc.tensor.transpose(banks[half][:, q * P:(q + 1) * P],
                                               b["ot"][:, 2 * half + q // 2, (q % 2) * P:(q % 2 + 1) * P], w["ident"][:])
            last.then_inc(g[n + "_ott"], 1)

        def at_out_dve(dve, n, b, banks):
            dve.wait_ge(g[n + "_ott"], 1)
            view = lambda k: banks[k][:].rearrange("p (h t c) -> p t h c", t=NT, c=2 * HD)
            for half in range(2):
                nc.vector.reciprocal(b["rd"][:, half], view(half)[:, :, :, HD]).then_inc(g[n + "_rd"], 1)
            for half in range(2):
                dve.wait_ge(g[n + "_rd"], half + 1)
                nc.vector.tensor_tensor(b["on"][:, :, half * P:(half + 1) * P].rearrange("p t (h c) -> p t h c", c=HD),
                                        view(half)[:, :, :, 0:HD],
                                        b["rd"][:, half].unsqueeze(3).broadcast_to([P, NT, HT, HD]), ALU.mult).then_inc(g[n + "_on"], 1)

        def at_out_pe2(pe, n, b, bank):
            pe.wait_ge(g[n + "_on"], 2)
            for e in range(ND):
                for t in range(NT):
                    last = nc.tensor.transpose(bank[:, e * S + t * P:e * S + (t + 1) * P], b["on"][:, t, e * P:(e + 1) * P], w["ident"][:])
            last.then_inc(g[n + "_ont"], 1)

        def at_out_act(act, n, b, bank):
            act.wait_ge(g[n + "_ont"], 1)
            nc.scalar.activation(b["onT"][:].rearrange("p e s -> p (e s)"), bank[:], ACT.Copy).then_inc(g[n + "_onT"], 1)

        def at_mask_q(pool, n, b, c):
            h = 2 * c
            r = h % b["qr"]
            if h >= b["qr"]:
                pool.wait_ge(g[n + "_s"], h - b["qr"] + 2)
            nc.gpsimd.tensor_tensor(b["qm"][:, r:r + 2, :], b["qT"][:, h // HT, :].unsqueeze(1).broadcast_to([P, 2, S]),
                                    w["hmask"][:, h % HT:h % HT + 2].unsqueeze(2).broadcast_to([P, 2, S]),
                                    ALU.mult).then_inc(g[n + "_qm"], 1)

        def at_mask_later(pool, n, b, s):
            if s % 2 == 0 and QR // 2 <= (s + 6) // 2 < H // 2:
                at_mask_q(pool, n, b, (s + 6) // 2)

        HS = H + 3

        def exps(act, n, b, bank, h):
            act.wait_ge(g[n + "_nm"], h + 1)
            if h >= 2:
                act.wait_ge(g[n + "_tr"], h - 1)
            for t in range(NT):
                a = nc.scalar.activation(b["pr"][:, h % 2, t, :], bank[:, t * S:(t + 1) * S], ACT.Exp,
                                         bias=b["nm"][:, h, t:t + 1])
                a.then_inc(g[n + "_ex"], 1)


        def scores_max(dve, n, b, bank, h):
            dve.wait_ge(g[n + "_s"], h + 1)
            nc.vector.tensor_reduce(b["nm"][:, h, :], bank[:].rearrange("p (t s) -> p t s", t=NT), AX.X, ALU.max,
                                    negate=True).then_inc(g[n + "_nm"], 1)

        def copy_all(act, dst, bank, ready, done):
            act.wait_ge(ready, 1)
            nc.scalar.activation(dst[:].rearrange("p e s -> p (e s)"), bank[:], ACT.Copy).then_inc(done, 1)

        def copy_values(act, n, b, bank):
            act.wait_ge(g[n + "_v"], 1)
            nc.scalar.activation(b["va"][:, :, :, 0:HD], bank[:].rearrange("p (t h c) -> p t h c", t=NT, c=HD),
                                 ACT.Copy).then_inc(g[n + "_va"], 1)

        def add_rows(dve, out, bank, rows, ready, done):
            dve.wait_ge(ready, 1)
            nc.vector.tensor_tensor(out[:].rearrange("p t d -> p (t d)"), bank[:], rows[:].rearrange("p t d -> p (t d)"), ALU.add).then_inc(done, 1)

        A1 = 0
        A2 = A1 + 12
        A3 = A2 + QUADS + 3
        M0 = A3 + 8
        AO = M0 + HS
        NA = AO + 2

        def tensor_a(pe):
            b = bufA
            if mode["mix"]:
                for k in range(12):
                    which, quad = k // 4, k % 4
                    yield A1 + k
                    if k == 4:
                        pe.wait_ge(g["ln1_xT"], 1)
                    if k >= 2:
                        pe.wait_ge(g["hm_ev"], 4 * (k - 1))
                    wt, src = (("xwv", ctxA), ("xwq", lnA["xT"]), ("xwk", ctxA))[which]
                    for hp in range(2):
                        for d in range(ND):
                            c = (quad * 2 + hp) * P
                            last = nc.tensor.matmul(bankA[k % 2][:, hp * S:(hp + 1) * S], w[wt][:, d, c:c + P], src[:, d, :],
                                                    start=(d == 0), stop=(d == ND - 1))
                    last.then_inc(g["hm_proj"], 1)
                    if k == 1:
                        yield A1 + 1.6
                        ln_pe(pe, 1, lnA, bankA[2])
                    if 4 <= k < 8:
                        yield A1 + k + 0.5
                        v = k - 4
                        pe.wait_ge(g["hm_ev"], 16)
                        if v >= 2:
                            pe.wait_ge(g["hm_vev"], v - 1)
                        for i in range(8):
                            last = nc.tensor.transpose(bankA[2 + v % 2][:, i * XD:(i + 1) * XD], xvT[:, v * 8 + i, :], w["ident"][0:XD, 0:XD])
                        last.then_inc(g["hm_vtr"], 1)
                for s in range(QUADS + 3):
                    yield A2 + s
                    if s == 0:
                        pe.wait_ge(g["hm_ev"], 48)
                        pe.wait_ge(g["group_in"], 32)
                    if 2 <= s < QUADS + 2:
                        q = s - 2
                        pe.wait_ge(g["hm_pn"], q + 1)
                        pe.wait_ge(g["hm_vev"], 4)
                        if q >= 1:
                            pe.wait_ge(g["hm_pt"], q)
                        for i in range(4):
                            last = nc.tensor.transpose(bankA[2][:, i * P:(i + 1) * P], xpn[:, q % 2, i, :], w["ident"][:])
                        last.then_inc(g["hm_tr"], 1)
                    if s < QUADS:
                        if s >= 2:
                            pe.wait_ge(g["hm_ex"], 4 * (s - 1))
                        for i in range(4):
                            c = 4 * s + i
                            last = nc.tensor.matmul(bankA[s % 2][:, i * P:(i + 1) * P], xqT[:, c, :], xkT[:, c, :], start=True, stop=True)
                        last.then_inc(g["hm_s"], 1)
                    if s >= 3:
                        q = s - 3
                        pe.wait_ge(g["hm_pt"], q + 1)
                        if q >= 1:
                            pe.wait_ge(g["hm_ot"], q)
                        for uh in range(2):
                            for jo in range(2):
                                i = jo * 2 + uh
                                last = nc.tensor.matmul(bankA[3][jo * XD:(jo + 1) * XD, uh * P:(uh + 1) * P],
                                                        xv[:, 4 * q + i, :], xpt[:, q % 2, i, :], start=True, stop=True)
                        last.then_inc(g["hm_o"], 1)
                yield A3
                pe.wait_ge(g["hm_ot"], QUADS)
                for t in range(NT):
                    for jp in range(QUADS):
                        last = nc.tensor.matmul(bankA[0][:, t * D:(t + 1) * D],
                                                xot[:, jp, 8 * t:8 * t + 8].rearrange("p h a b -> p (h a b)"),
                                                w["xwo"][:, jp, :], start=(jp == 0), stop=(jp == QUADS - 1))
                last.then_inc(g["hm_y"], 1)
            if mode["mla"]:
                yield A3 + 0.3
                ln_pe(pe, 0, lnM, bankA[3])
            if mode["mix"]:
                yield A3 + 1.8
                ln_pe(pe, 2, lnA, bankA[1])
                yield A3 + 2.2
                pe.wait_ge(g["ln2_xT"], 1)
                for d in range(ND):
                    last = nc.tensor.matmul(bankA[2][:, 0:S], w["wrt"][:, d, :], lnA["xT"][:, d, :], start=(d == 0), stop=(d == ND - 1))
                last.then_inc(g["md_sps"], 1)
            if mode["mla"]:
                yield A3 + 2.5
                pe.wait_ge(g["ln0_xT"], 1)
                for d in range(ND):
                    last = nc.tensor.matmul(bankA[3][:, 0:S], w["wlat"][:, d, :], lnM["xT"][:, d, :], start=(d == 0), stop=(d == ND - 1))
                last.then_inc(g["lat_ps"], 1)
                project_T(bankA[1], w["wq0"], lnM["xT"], g["mla_q"])
                yield A3 + 3.2
                pe.wait_ge(g["latT"], 1)
                if mode["mix"]:
                    pe.wait_ge(g["md_srow"], 1)
                for e in range(ND):
                    last = nc.tensor.matmul(bankA[2][:, e * S:(e + 1) * S], w["wkb"][:, e * P:(e + 1) * P], latT, start=True, stop=True)
                last.then_inc(g["mla_k"], 1)
                for t in range(NT):
                    last = nc.tensor.matmul(bankA[3][:, t * D:(t + 1) * D], latT[:, t * P:(t + 1) * P], w["wvb"][:], start=True, stop=True)
                last.then_inc(g["mla_v"], 1)
            if mode["mix"]:
                yield A3 + 4
                pe.wait_ge(g["md_e"], 6)
                for d in range(ND):
                    for t in range(NT):
                        last = nc.tensor.matmul(bankA[0][:, d * P:(d + 1) * P], lnA["xn"][:, t, d * P:(d + 1) * P], pick[:, t, :],
                                                start=(t == 0), stop=(t == NT - 1))
                last.then_inc(g["md_sel"], 1)
                if mode["mla"]:
                    pe.wait_ge(g["mla_va"], 1)
                for t in range(NT):
                    last = nc.tensor.transpose(bankA[3][:, t * P:(t + 1) * P], pick[:, t, :], w["ident"][:])
                last.then_inc(g["md_ptr"], 1)
                for k in range(2):
                    yield A3 + 5 + 0.3 * k
                    pe.wait_ge(g["md_selT"], 1)
                    if mode["mla"]:
                        pe.wait_ge(g[("mla_qT", "mla_kT")[k]], 1)
                    for f in range(4):
                        for d in range(ND):
                            c = (4 * k + f) * P
                            last = nc.tensor.matmul(bankA[1 + k][:, f * P:(f + 1) * P], w["w1"][:, d, c:c + P], selT[:, d, :],
                                                    start=(d == 0), stop=(d == ND - 1))
                    last.then_inc(g["md_h"], 1)
                yield A3 + 6
                for f in range(FF // P):
                    pe.wait_ge(g["md_hid"], f + 1)
                    nc.tensor.matmul(bankA[0][:, 0:D], hid[:, f, :], w["w2"][:, f, :], start=(f == 0), stop=False)
                nc.tensor.matmul(bankA[0][:, 0:D], ones[0:1, :], w["b2"][:], start=False, stop=True).then_inc(g["md_y"], 1)
                yield A3 + 7
                pe.wait_ge(g["md_yff"], 1)
                pe.wait_ge(g["md_pickT"], 1)
                for t in range(NT):
                    last = nc.tensor.matmul(bankA[3][:, t * D:(t + 1) * D], pickT[:, t, :], yff[:], start=True, stop=True)
                last.then_inc(g["md_u"], 1)
            if mode["mla"]:
                for h in range(HS):
                    yield M0 + h
                    if h == 0:
                        pe.wait_ge(g["mla_kT"], 1)
                        pe.wait_ge(g["mla_va"], 1)
                    if h >= 4 and h % 2 == 0:
                        at_values(pe, "mla", b, bankA[3], h - 4)
                    if 2 <= h < H + 2:
                        at_transpose(pe, "mla", b, bankA[2], h - 2)
                    if h < H:
                        at_scores(pe, "mla", b, bankA[h % 2], h, g["mla_ex"], NT)
                yield AO + 0.2
                at_out_pe1(pe, "mla", b, bankA[0:2])
                yield AO + 0.8 + 0.8
                at_out_pe2(pe, "mla", b, bankA[2])
                yield AO + 1.2
                pe.wait_ge(g["mla_onT"], 1)
                project_N(bankA[3], b["onT"], w["wo0"], g["mla_y"])

        def scalar_a(act):
            b = bufA
            if mode["mix"]:
                for k in range(12):
                    which, quad = k // 4, k % 4
                    yield A1 + k + 0.4
                    act.wait_ge(g["hm_proj"], k + 1)
                    if k == 8:
                        act.wait_ge(g["hm_vtr"], 4)
                    dst = (xvT, xqT, xkT)[which]
                    bias = (w["xb"][:, 2], bq8, w["xb"][:, 1])[which]
                    for hp in range(2):
                        for o in range(2):
                            h = 4 * quad + 2 * hp + o
                            nc.scalar.activation(dst[0:XD, :, 8 * h:8 * h + 8].rearrange("p (j a) u -> p j a u", a=2),
                                                 bankA[k % 2][o * XD:(o + 1) * XD, hp * S:(hp + 1) * S].rearrange("p (a u j) -> p j a u", a=2, j=NJ),
                                                 ACT.Identity, bias=bias[:, h:h + 1],
                                                 scale=(XD ** -0.5 if which == 1 else 1.0)).then_inc(g["hm_ev"], 1)
                    if k == 2:
                        yield A1 + 2.9
                        ln_act(act, 1, lnA, bankA[2])
                    if 4 <= k < 8:
                        v = k - 4
                        yield A1 + k + 0.8
                        act.wait_ge(g["hm_vtr"], v + 1)
                        nc.scalar.activation(xv[:, 8 * v:8 * v + 8, :].rearrange("p g c -> p (g c)"), bankA[2 + v % 2][:], ACT.Copy).then_inc(g["hm_vev"], 1)
                for s in range(QUADS + 3):
                    yield A2 + s + 0.2
                    if 2 <= s < QUADS + 2:
                        q = s - 2
                        act.wait_ge(g["hm_tr"], q + 1)
                        if q >= 2:
                            act.wait_ge(g["hm_o"], q - 1)
                        nc.scalar.activation(xpt[:, q % 2].rearrange("p g c -> p (g c)"), bankA[2][:], ACT.Copy).then_inc(g["hm_pt"], 1)
                    yield A2 + s + 0.5
                    if s < QUADS:
                        act.wait_ge(g["hm_nm"], s + 1)
                        for i in range(4):
                            c = 4 * s + i
                            nc.scalar.activation(xp[:, s % 2, i, :], bankA[s % 2][:, i * P:(i + 1) * P], ACT.Exp,
                                                 bias=xnm[:, c:c + 1], accum_out=xrs[:, c:c + 1]).then_inc(g["hm_ex"], 1)
                    yield A2 + s + 0.8
                    if s >= 3:
                        q = s - 3
                        act.wait_ge(g["hm_o"], q + 1)
                        for uh in range(2):
                            a = nc.scalar.activation(xot[:, q, :, uh, :], bankA[3][:, uh * P:(uh + 1) * P].rearrange("p (h u) -> p h u", u=8), ACT.Copy)
                        a.then_inc(g["hm_ot"], 1)
            if mode["mla"]:
                yield A3 + 0.6
                ln_act(act, 0, lnM, bankA[3])
            if mode["mix"]:
                yield A3 + 2
                ln_act(act, 2, lnA, bankA[1])
                yield A3 + 2.6
                act.wait_ge(g["md_sps"], 1)
                nc.scalar.activation(srow[:], bankA[2][:, 0:S], ACT.Copy).then_inc(g["md_srow"], 1)
            if mode["mla"]:
                yield A3 + 2.8
                act.wait_ge(g["lat_ps"], 1)
                nc.scalar.activation(latT, bankA[3][:, 0:S], ACT.Copy).then_inc(g["latT"], 1)
                copy_all(act, b["qT"], bankA[1], g["mla_q"], g["mla_qT"])
                yield A3 + 3.5
                copy_all(act, b["kT"], bankA[2], g["mla_k"], g["mla_kT"])
                copy_values(act, "mla", b, bankA[3])
            if mode["mix"]:
                yield A3 + 3.6
                act.wait_ge(g["md_e"], 2)
                nc.scalar.activation(gate[:], scol[:], ACT.Exp, scale=-1.0).then_inc(g["md_gate"], 1)
                yield A3 + 4.4
                act.wait_ge(g["md_sel"], 1)
                nc.scalar.activation(selT[:].rearrange("p d c -> p (d c)"), bankA[0][:, 0:D], ACT.Copy).then_inc(g["md_selT"], 1)
                act.wait_ge(g["md_ptr"], 1)
                nc.scalar.activation(pickT[:].rearrange("p d c -> p (d c)"), bankA[3][:, 0:D], ACT.Copy).then_inc(g["md_pickT"], 1)
                yield A3 + 5.5
                for k in range(2):
                    act.wait_ge(g["md_h"], k + 1)
                    for f in range(4):
                        nc.scalar.activation(hid[:, 4 * k + f, :], bankA[1 + k][:, f * P:(f + 1) * P], ACT.Gelu_apprx_tanh,
                                             bias=w["b1"][:, 4 * k + f:4 * k + f + 1]).then_inc(g["md_hid"], 1)
                yield A3 + 6.7
                act.wait_ge(g["md_y"], 1)
                nc.scalar.activation(yff[:], bankA[0][:, 0:D], ACT.Copy).then_inc(g["md_yff"], 1)
            if mode["mla"]:
                for h in range(HS):
                    yield M0 + 0.2 + h
                    if 2 <= h < H + 2:
                        at_copy_pt(act, "mla", b, bankA[2], h - 2)
                    yield M0 + 0.7 + h
                    if h < H:
                        exps(act, "mla", b, bankA[h % 2], h)
                    if h == 11:
                        at_copy_ot(act, "mla", b, bankA[3], 0)
                yield AO
                at_copy_ot(act, "mla", b, bankA[3], 1)
                yield AO + 1
                at_out_act(act, "mla", b, bankA[2])

        def vector_a(dve):
            b = bufA
            link = chain(dve, "dveA")
            if mode["mix"]:
                yield A1 + 0.5 + 0.2
                ln_dve(dve, 1, x1, lnA, [])
                yield A1 + 1.2
                ln_dve2(dve, 1, x1, lnA)
                for s in range(QUADS + 1):
                    yield A2 + s + 0.4
                    if s < QUADS:
                        dve.wait_ge(g["hm_s"], s + 1)
                        nc.vector.tensor_reduce(xnm[:, 4 * s:4 * s + 4], bankA[s % 2][:].rearrange("p (i c) -> p i c", i=4), AX.X, ALU.max,
                                                negate=True).then_inc(g["hm_nm"], 1)
                    if s >= 1:
                        q = s - 1
                        dve.wait_ge(g["hm_ex"], 4 * q + 4)
                        nc.vector.reciprocal(xrr[:, 4 * q:4 * q + 4], xrs[:, 4 * q:4 * q + 4]).then_inc(g["hm_rr"], 1)
            if mode["mla"]:
                yield A2 + QUADS + 0.5
                ln_dve(dve, 0, xin, lnM, [(g["x_in"], 16)])
                yield A2 + QUADS + 1 - 0.2
                ln_dve2(dve, 0, xin, lnM)
            if mode["mix"]:
                yield A3 + 0.9
                dve.wait_ge(g["hm_xb"], 1)
                add_rows(dve, x2, bankA[0], xh, g["hm_y"], g["hm_x2"])
                yield A3 + 1 + 0.3
                ln_dve(dve, 2, x2, lnA, [(g["hm_x2"], 1)])
                yield A3 + 1.5
                ln_dve2(dve, 2, x2, lnA)
                yield A3 + 3
                dve.wait_ge(g["md_srow"], 1)
                for t in range(NT):
                    link(nc.vector.tensor_tensor(tmpd[:, t, 0:P], srow[:, t * P:(t + 1) * P], w["ident"][:], ALU.mult))
                for t in range(NT):
                    nc.vector.tensor_reduce(scol[:, t:t + 1], tmpd[:, t, 0:P], AX.X, ALU.add).then_inc(g["md_e"], 1)
                dve.wait_ge(g["md_e"], 2)
                for t in range(NT):
                    link.inc(nc.vector.tensor_scalar(tmpd[:, t, :], srow[:], scol[:, t:t + 1], None, ALU.is_equal))
                for t in range(NT):
                    link.wait(link.n + t - 1 - t)
                    link.inc(nc.vector.tensor_tensor(tmpd[:, t, :], tmpd[:, t, :], w["lower"][:, t, :], ALU.mult))
                for t in range(NT):
                    link.wait(link.n - 1)
                    link.inc(nc.vector.scalar_tensor_tensor(tmpd[:, t, :], srow[:], scol[:, t:t + 1], tmpd[:, t, :], ALU.is_gt, ALU.add))
                for t in range(NT):
                    link.wait(link.n - 1 + t)
                    nc.vector.tensor_reduce(rank[:, t:t + 1], tmpd[:, t, :], AX.X, ALU.add).then_inc(g["md_e"], 1)
                for t in range(NT):
                    dve.wait_ge(g["md_e"], 3 + t)
                    nc.vector.tensor_scalar(pick[:, t, :], w["iota"][:, 0:CAP], rank[:, t:t + 1], None, ALU.is_equal).then_inc(g["md_e"], 1)
                yield A3 + 4.5
                dve.wait_ge(g["md_gate"], 1)
                nc.vector.tensor_scalar(gate1[:], gate[:], 1.0, None, ALU.add).then_inc(g["md_e"], 1)
                dve.wait_ge(g["md_e"], 7)
                nc.vector.reciprocal(gate2[:], gate1[:]).then_inc(g["md_e"], 1)
                yield A3 + 7.6
                dve.wait_ge(g["md_u"], 1)
                dve.wait_ge(g["md_xh"], 1)
                dve.wait_ge(g["md_e"], 8)
                if waits_b():
                    dve.wait_ge(g["sp_xb"], 1)
                for t in range(NT):
                    nc.vector.scalar_tensor_tensor(x3[:, t, :], bankA[3][:, t * D:(t + 1) * D], gate2[:, t:t + 1], xh[:, t, :],
                                                   ALU.mult, ALU.add).then_inc(g["md_x3"], 1)
            if mode["mla"]:
                for h in range(H):
                    yield M0 + 0.4 + h
                    scores_max(dve, "mla", b, bankA[h % 2], h)
                yield AO + 0.5
                at_out_dve(dve, "mla", b, bankA[0:2])
                yield AO + 1.7
                add_rows(dve, x1, bankA[3], xin, g["mla_y"], g["mla_x"])

        def pool_a(pool):
            b = bufA
            if mode["mix"]:
                yield A1 + 0.7
                ln_pool(pool, 1, lnA)
                yield A1 + 2
                pool.wait_ge(g["ln1_xn"], 2)
                nc.gpsimd.tensor_tensor(xh[:], x1[:], w["xbo"][:].unsqueeze(1).broadcast_to([P, NT, D]), ALU.add).then_inc(g["hm_xb"], 1)
                for q in range(QUADS):
                    yield A2 + q + 1.6
                    pool.wait_ge(g["hm_rr"], q + 1)
                    nc.gpsimd.tensor_tensor(xpn[:, q % 2], xp[:, q % 2],
                                            xrr[:, 4 * q:4 * q + 4].unsqueeze(2).broadcast_to([P, 4, P]), ALU.mult).then_inc(g["hm_pn"], 1)
            if mode["mla"]:
                yield A2 + QUADS + 0.7
                ln_pool(pool, 0, lnM)
            if mode["mix"]:
                yield A3 + 1.2
                ln_pool(pool, 2, lnA)
                yield A3 + 2
                pool.wait_ge(g["ln2_xn"], 2)
                nc.gpsimd.tensor_tensor(xh[:], x2[:], lnA["xn"][:], ALU.add).then_inc(g["md_xh"], 1)
            if mode["mla"]:
                yield A3 + 3.6
                pool.wait_ge(g["mla_qT"], 1)
                for c in range(H // 2):
                    yield A3 + 3.6 + 0.7 * c
                    at_mask_q(pool, "mla", b, c)

        BS = H + 4
        BO = 3 + BS
        C0 = BO + 2
        CO = C0 + 2 + HS
        L0 = CO + 2
        NB = L0 + 2

        def tensor_b(pe):
            b = bufB
            yield 0.4
            ln_pe(pe, 3, lnB, bankB[0])
            yield 0.7
            pe.wait_ge(g["ln3_xT"], 1)
            project_T(bankB[0], w["swq"], lnB["xT"], g["spa_q"])
            project_T(bankB[1], w["swk"], lnB["xT"], g["spa_k"])
            yield 2.2
            project_N(bankB[2], lnB["xT"], w["swv"], g["spa_v"])
            for s in range(BS):
                yield 3 + s
                if s == 0:
                    pe.wait_ge(g["spa_kT"], 2)
                if s < H:
                    at_scores(pe, "spa", b, bankB[s % 2], s, g["sp_sc"], 1)
                if s == 5:
                    pe.wait_ge(g["spa_va"], 1)
                if s >= 5 and s % 2 == 1:
                    at_values(pe, "spa", b, bankB[3], s - 5)
                if 3 <= s < H + 3:
                    at_transpose(pe, "spa", b, bankB[2], s - 3)
            yield BO + 0.2
            at_out_pe1(pe, "spa", b, bankB[0:2])
            yield BO + 0.8
            at_out_pe2(pe, "spa", b, bankB[2])
            pe.wait_ge(g["ctxB_in"], 16)
            project_T(bankB[1], w["cwk"], ctxB, g["crs_k"])
            project_N(bankB[0], ctxB, w["cwv"], g["crs_v"])
            yield BO + 1.3
            pe.wait_ge(g["spa_onT"], 1)
            project_N(bankB[3], b["onT"], w["swo"], g["spa_y"])
            yield C0 + 0.8
            ln_pe(pe, 4, lnB, bankB[2])
            yield C0 + 1.2
            pe.wait_ge(g["ln4_xT"], 1)
            pe.wait_ge(g["crs_va"], 1)
            project_T(bankB[0], w["cwq"], lnB["xT"], g["crs_q"])
            for h in range(HS):
                yield C0 + 2 + h
                if h == 0:
                    pe.wait_ge(g["crs_kT"], 1)
                    pe.wait_ge(g["mask_row"], 1)
                if h >= 4 and h % 2 == 0:
                    at_values(pe, "crs", b, bankB[3], h - 4)
                if 2 <= h < H + 2:
                    at_transpose(pe, "crs", b, bankB[2], h - 2)
                if h < H:
                    at_scores(pe, "crs", b, bankB[h % 2], h, g["crs_ex"], NT, masked=True)
            yield CO + 0.2
            at_out_pe1(pe, "crs", b, bankB[0:2])
            yield CO + 0.8
            at_out_pe2(pe, "crs", b, bankB[2])
            yield CO + 1.2
            pe.wait_ge(g["crs_onT"], 1)
            project_N(bankB[3], b["onT"], w["cwo"], g["crs_y"])
            yield L0 + 0.8
            ln_pe(pe, 5, lnB, bankB[0])
            yield L0 + 1.2
            pe.wait_ge(g["ln5_xT"], 1)
            project_N(bankB[1], lnB["xT"], weff, g["lin_y"])

        def scalar_b(act):
            b = bufB
            yield 0.5
            ln_act(act, 3, lnB, bankB[0])
            yield 0.8
            for n, bank, dst, bias in (("spa_q", bankB[0], "qT", "sbq"), ("spa_k", bankB[1], "kT", "sbk")):
                act.wait_ge(g[n], 1)
                for e in range(ND):
                    nc.scalar.activation(b[dst][:, e, :], bank[:, e * S:(e + 1) * S], ACT.Identity,
                                         bias=w[bias][:, e:e + 1]).then_inc(g["spa_" + dst], 1)
            for s in range(BS):
                yield 3.1 + s
                if 2 <= s < H + 2:
                    h = s - 2
                    act.wait_ge(g["sp_top"], h + 1)
                    if h >= 2:
                        act.wait_ge(g["spa_tr"], h - 1)
                    nc.scalar.activation(taken[:, h % 2].rearrange("p t s -> p (t s)"), wk[:, h % 2].rearrange("p t s -> p (t s)"),
                                         ACT.Relu, bias=-1.0, scale=-2.0 / BIG).then_inc(g["sp_tk"], 1)
                yield 3.2 + s
                if s < H:
                    act.wait_ge(g["spa_s"], s + 1)
                    if s >= 3:
                        act.wait_ge(g["sp_mul"], s - 2)
                    nc.scalar.activation(sc[:, s % 3].rearrange("p t s -> p (t s)"), bankB[s % 2][:], ACT.Copy).then_inc(g["sp_sc"], 1)
                yield 3.3 + s
                if 3 <= s < H + 3:
                    at_copy_pt(act, "spa", b, bankB[2], s - 3)
                yield 3.6 + s
                if 2 <= s < H + 2:
                    h = s - 2
                    act.wait_ge(g["sp_mul"], h + 1)
                    act.wait_ge(g["spa_nm"], h + 1)
                    for t in range(NT):
                        nc.scalar.activation(b["pr"][:, h % 2, t, :], sp_[:, h % 2, t, :], ACT.Exp,
                                             bias=b["nm"][:, h, t:t + 1]).then_inc(g["spa_ex"], 1)
                if s == 12:
                    at_copy_ot(act, "spa", b, bankB[3], 0)
            yield BO
            at_copy_ot(act, "spa", b, bankB[3], 1)
            yield BO + 1
            at_out_act(act, "spa", b, bankB[2])
            yield BO + 1.4
            copy_all(act, b["kT"], bankB[1], g["crs_k"], g["crs_kT"])
            copy_values(act, "crs", b, bankB[0])
            yield C0 + 1
            ln_act(act, 4, lnB, bankB[2])
            yield C0 + 1.6
            copy_all(act, b["qT"], bankB[0], g["crs_q"], g["crs_qT"])
            for h in range(HS):
                yield C0 + 2.2 + h
                if 2 <= h < H + 2:
                    at_copy_pt(act, "crs", b, bankB[2], h - 2)
                yield C0 + 2.7 + h
                if h < H:
                    exps(act, "crs", b, bankB[h % 2], h)
                if h == 11:
                    at_copy_ot(act, "crs", b, bankB[3], 0)
            yield CO
            at_copy_ot(act, "crs", b, bankB[3], 1)
            yield CO + 1
            at_out_act(act, "crs", b, bankB[2])
            yield L0 + 1
            ln_act(act, 5, lnB, bankB[0])

        def vector_b(dve):
            b = bufB
            link = chain(dve, "dveB")
            yield 0
            ln_dve(dve, 3, x3, lnB, [])
            yield 0.3
            ln_dve2(dve, 3, x3, lnB)
            yield 3.2
            dve.wait_ge(g["spa_v"], 1)
            nc.vector.tensor_tensor(b["va"][:, :, :, 0:HD], bankB[2][:].rearrange("p (t h c) -> p t h c", t=NT, c=HD),
                                    w["sbv"][:].rearrange("p (h c) -> p h c", c=HD).unsqueeze(1).broadcast_to([P, NT, H, HD]),
                                    ALU.add).then_inc(g["spa_va"], 1)
            for h in range(H):
                k = h % 2
                yield 4 + h
                dve.wait_ge(g["sp_sc"], h + 1)
                if h >= 2:
                    dve.wait_ge(g["sp_tk"], h - 1)
                    dve.wait_ge(g["sp_nm"], h - 1)
                src = sc[:, h % 3]
                n0 = link.n
                for r in range(ROUNDS):
                    if r:
                        yield 4 + h + r / ROUNDS
                    for t in range(NT):
                        if r:
                            link.wait(n0 + 2 * NT * r - NT + 1 + t)
                        link.inc(nc.vector.max(m8[:, k, r, t, :], src[:, t, :]))
                    if r == ROUNDS - 1:
                        link.wait(link.n)
                        link.inc(nc.vector.memset(m8[:, k, r, :, 1:8], -BIG))
                    for t in range(NT):
                        link.wait(link.n if r == ROUNDS - 1 else n0 + 2 * NT * r + 1 + t)
                        m = nc.vector.match_replace(out=wk[:, k, t, :], in_to_replace=m8[:, k, r, t, :], in_values=src[:, t, :],
                                                    imm_value=-BIG)
                        if r == ROUNDS - 1 and t == NT - 1:
                            m.then_inc(g["sp_top"], 1)
                        else:
                            link.inc(m)
                    src = wk[:, k]
            yield BO + 0.5
            at_out_dve(dve, "spa", b, bankB[0:2])
            dve.wait_ge(g["len_in"], 16)
            link(nc.vector.tensor_copy(lenf[:], lenb[:]))
            nc.vector.tensor_scalar(mrow[:], w["iota"][0:1, :].unsqueeze(1).broadcast_to([1, NT, S]), lenf[:, 0:1], NEG,
                                    ALU.is_ge, ALU.mult).then_inc(g["mask_row"], 1)
            yield BO + 1.8
            dve.wait_ge(g["sp_xb"], 1)
            add_rows(dve, x4, bankB[3], x3b, g["spa_y"], g["spa_x"])
            yield C0
            ln_dve(dve, 4, x4, lnB, [(g["spa_x"], 1)])
            yield C0 + 0.5
            ln_dve2(dve, 4, x4, lnB)
            for h in range(H):
                yield C0 + 2.4 + h
                scores_max(dve, "crs", b, bankB[h % 2], h)
            yield CO + 0.5
            at_out_dve(dve, "crs", b, bankB[0:2])
            yield CO + 1.7
            add_rows(dve, x5, bankB[3], x4, g["crs_y"], g["crs_x"])
            yield L0
            ln_dve(dve, 5, x5, lnB, [(g["crs_x"], 1)])
            yield L0 + 0.5
            ln_dve2(dve, 5, x5, lnB)
            yield L0 + 1.7
            dve.wait_ge(g["lin_xb"], 1)
            add_rows(dve, xo, bankB[1], xo, g["lin_y"], g["lin_o"])

        def pool_b(pool):
            b = bufB
            yield 0.2
            ln_pool(pool, 3, lnB)
            for c in range(QR // 2):
                yield 0.9 + 0.5 * c
                pool.wait_ge(g["spa_qT"], 1)
                at_mask_q(pool, "spa", b, c)
            for s in range(BS):
                yield 3.1 + s
                if s == 1:
                    pool.wait_ge(g["ln3_xn"], 2)
                    nc.gpsimd.tensor_tensor(x3b[:], x3[:], w["sbo"][:].unsqueeze(1).broadcast_to([P, NT, D]), ALU.add).then_inc(g["sp_xb"], 1)
                if s == 2:
                    pool.wait_ge(g["spa_qT"], 2)
                at_mask_later(pool, "spa", b, s)
                if 2 <= s < H + 2:
                    yield 3.3 + s
                    h = s - 2
                    pool.wait_ge(g["sp_top"], h + 1)
                    nc.gpsimd.tensor_scalar(mx0[:, h, :], m8[:, h % 2, 0, :, 0], 0.0, -1.0, ALU.max, ALU.mult).then_inc(g["sp_nm"], 1)
                    pool.wait_ge(g["sp_nm"], h + 1)
                    nc.gpsimd.tensor_copy(b["nm"][:, h, :], mx0[:, h, :]).then_inc(g["spa_nm"], 1)
                    pool.wait_ge(g["sp_tk"], h + 1)
                    nc.gpsimd.tensor_tensor(sp_[:, h % 2], taken[:, h % 2], sc[:, h % 3], ALU.mult).then_inc(g["sp_mul"], 1)
            yield C0 + 0.2
            ln_pool(pool, 4, lnB)
            yield C0 + 1.7
            pool.wait_ge(g["crs_qT"], 1)
            for c in range(QR // 2):
                at_mask_q(pool, "crs", b, c)
            for h in range(HS):
                yield C0 + 2.1 + h + 0.1
                at_mask_later(pool, "crs", b, h)
            yield L0 + 0.2
            ln_pool(pool, 5, lnB)
            yield L0 + 1.1
            pool.wait_ge(g["ln5_xn"], 2)
            nc.gpsimd.tensor_tensor(xo[:], x5[:], w["fbias"][:].unsqueeze(1).broadcast_to([P, NT, D]), ALU.add).then_inc(g["lin_xb"], 1)

        LEN_A = [(0, 2.2), (A1 + 4, 1.83), (A1 + 8, 1.65), (A2, 2.3), (A3, 4.23), (A3 + 3, 2.5), (A3 + 5, 3), (M0, 2.37), (M0 + 8, 1.84), (AO, 3)]
        LEN_B = [(0, 2.5), (1, 1.5), (2, 1.5), (3, 5.5), (4, 5.5), (11, 5.26), (BO, 2.98), (C0, 1.54), (C0 + 2, 1.96), (C0 + 10, 1.98), (CO, 3.99), (L0, 7.63)]

        def shares(n, lengths):
            each = [max((f, v) for f, v in lengths if f <= k)[1] for k in range(n + 1)]
            return lambda t: (sum(each[:int(t)]) + (t - int(t)) * each[int(t)]) / sum(each[:n])

        keyA = shares(NA, LEN_A)
        keyB = shares(NB, LEN_B)
        mode = {}

        def waits_b():
            return mode["b"]

        def chain(eng, name):
            def link(ins):
                link.inc(ins)
                link.wait(link.n)

            def inc(ins):
                link.n += 1
                ins.then_inc(g[name], 1)
                return ins

            def wait(v):
                eng.wait_ge(g[name], v)
            link.n = 0
            link.inc = inc
            link.wait = wait
            return link

        def merged(a, b):
            ka = keyA(next(a)) if a else 3.0
            kb = keyB(next(b)) if b else 3.0
            while a or b:
                if ka <= kb:
                    v = next(a, None)
                    a, ka = (a, keyA(v)) if v is not None else (None, 3.0)
                else:
                    v = next(b, None)
                    b, kb = (b, keyB(v)) if v is not None else (None, 3.0)

        def one_pass(mix, mla, ib, first=False, last=False):
            A, Bs = mix or mla is not None, ib is not None
            mode["mix"], mode["mla"], mode["b"] = mix, mla is not None, Bs
            with nc.Block() as block:
                @block.sync
                def _(sp):
                    if mode["mla"] and not first:
                        sp.dma_start(xin[:], x_in[mla]).then_inc(g["x_in"], 16)
                    if mode["mla"] and mix and not Bs:
                        sp.dma_start(lenb[:], lens_in[0]).then_inc(s_stored, 16)
                    if Bs:
                        sp.wait_ge(s_stored, 16)
                        sp.sem_clear(s_stored)
                        sp.dma_start(ctxB[:], ctx_in[ib]).then_inc(g["ctxB_in"], 16)
                        sp.dma_start(lenb[:], lens_in[ib]).then_inc(g["len_in"], 16)
                    if mix:
                        sp.dma_start(xq_area[XD:XD + 8, :], w_in["groupq"]).then_inc(g["group_in"], 16)
                        sp.dma_start(vT_qm[XD:XD + 8, :], w_in["groupk"]).then_inc(g["group_in"], 16)
                    if mode["mla"]:
                        if mix:
                            sp.wait_ge(g["hm_proj"], 12)
                        sp.dma_start(ctxA[:], ctx_in[mla]).then_inc(g["ctxA_in"], 16)
                        sp.wait_ge(g["ctxA_in"], 16)
                    if Bs:
                        sp.wait_ge(g["lin_o"], 1)
                        sp.dma_start(out[ib], xo[:]).then_inc(s_stored, 16)
                        if last:
                            sp.wait_ge(s_stored, 16)

                @block.tensor
                def _(pe):
                    merged(tensor_a(pe) if A else None, tensor_b(pe) if Bs else None)

                @block.scalar
                def _(act):
                    merged(scalar_a(act) if A else None, scalar_b(act) if Bs else None)

                @block.vector
                def _(dve):
                    merged(vector_a(dve) if A else None, vector_b(dve) if Bs else None)

                @block.gpsimd
                def _(pool):
                    merged(pool_a(pool) if A else None, pool_b(pool) if Bs else None)

            with nc.Block() as block:
                @block.sync
                def _(sp):
                    sp.sem_clear(range(min(s.num for s in g.values()), max(s.num for s in g.values()) + 1))

        nb = out.shape[0]
        one_pass(False, 0, None, first=True)
        setup_rest()
        one_pass(True, 1, None)
        if nb > 2:
            with nc.Fori(0, nb - 2) as i:
                one_pass(True, i + 2, i)
        one_pass(True, None, nb - 2)
        one_pass(False, None, nb - 1, last=True)


def layouts(inp):
    c = lambda a: np.ascontiguousarray(a)
    f = np.float32
    i = {k: np.asarray(v) for k, v in inp.items()}
    rows = lambda a, n=P: c(a.reshape(a.shape[0] // n, n, a.shape[1]).transpose(1, 0, 2))
    swap = np.arange(D) ^ 1
    head = np.arange(H, dtype=f)[:, None]
    inv = f(1.0) / f(10000.0) ** (np.arange(0, HD, 2, dtype=f) / f(HD))
    ang = (head * inv[None, :]).astype(f)
    cos, sin = (np.repeat(t(ang).astype(f), 2, 1).reshape(1, D) for t in (np.cos, np.sin))
    p = np.arange(P)
    ropec = np.repeat(cos, P, 0)
    ropes = np.repeat(sin * np.where(np.arange(D) % 2 == 0, -1.0, 1.0)[None, :], P, 0)
    padrow = lambda a, top: np.concatenate([a, np.zeros((P - a.shape[0], a.shape[1]), f)][:: 1 if top else -1], 0)
    wide = lambda v: c(np.broadcast_to(v[None, :], (P, v.shape[0])))
    cols = lambda v, n=P: c(v.reshape(-1, n).T)
    u8 = np.tile(np.arange(8), 2 * NJ * H)
    onehot = (u8[None, :] == np.arange(8)[:, None]).astype(f)
    tok = p[:, None] + P * np.arange(NT)[None, :]
    w = {
        "wq0": rows(i["L0_attn_wq"].T), "wq0s": rows(i["L0_attn_wq"].T[:, swap]),
        "wlat": rows(np.concatenate([i["L0_attn_wk_a"].T, i["L0_attn_wv_a"].T], 1)),
        "wkb": padrow(i["L0_attn_wk_b"].T, True), "wkbs": padrow(i["L0_attn_wk_b"].T[:, swap], True),
        "wvb": padrow(i["L0_attn_wv_b"].T, False), "wo0": rows(i["L0_attn_wo"].T),
        "ropec": ropec, "ropes": ropes, "hmask": 0.25 * (p[:, None] // HD == np.arange(HT)[None, :]),
        "xwq": rows(i["L0_xattn_Wq"].T), "xwk": rows(i["L0_xattn_Wk"].T), "xwv": rows(i["L0_xattn_Wv"].T),
        "xwo": rows(i["L0_xattn_Wo"].T),
        "xb": np.stack([cols(i["L0_xattn_b" + k], XD) for k in "qkv"], 1), "xbo": wide(i["L0_xattn_bo"]),
        "wrt": rows(np.repeat(i["L0_ffn_w_router"][:, None], P, 1)),
        "w1": rows(i["L0_ffn_W1"]), "b1": cols(i["L0_ffn_b1"]), "w2": rows(i["L0_ffn_W2"]), "b2": i["L0_ffn_b2"][None, :],
        "swq": rows(i["L1_attn_Wq"]), "swk": rows(i["L1_attn_Wk"]), "swv": rows(i["L1_attn_Wv"]), "swo": rows(i["L1_attn_Wo"]),
        "sbq": cols(i["L1_attn_bq"]), "sbk": cols(i["L1_attn_bk"]), "sbv": wide(i["L1_attn_bv"]), "sbo": wide(i["L1_attn_bo"]),
        "cwq": rows(i["L1_xattn_Wq"]), "cwk": rows(i["L1_xattn_Wk"]), "cwv": rows(i["L1_xattn_Wv"]), "cwo": rows(i["L1_xattn_Wo"]),
        "wt": rows(i["L1_ffn_weight"].T), "alpha": c(np.broadcast_to(i["L1_ffn_alpha"][None, :], (P, 1))), "fbias": wide(i["L1_ffn_bias"]),
        "ident": np.eye(P), "iota": np.broadcast_to(np.arange(S)[None, :], (P, S)),
        "lower": np.arange(S)[None, None, :] < tok[:, :, None],
        "groupq": onehot, "groupk": -FAR * (1 - onehot),
    }
    w = {k: c(v if v.dtype == f else v.astype(f)) for k, v in w.items()}
    x = c(i["x"].reshape(-1, NT, P, D).transpose(0, 2, 1, 3))
    ctx = c(i["ctx_1024"].reshape(-1, S, ND, P).transpose(0, 3, 2, 1))
    return w, x, ctx, c(i["_lenS2"].reshape(-1, 1, 1))


def declare(nc, nb):
    ext = lambda n, s, dt, k="ExternalInput": nc.dram_tensor(n, tuple(s), dt, kind=k).ap()
    w_in = {n: ext("w_" + n, s, F32) for n, s in WEIGHTS.items()}
    x_in = ext("x_in", (nb, P, NT, D), F32)
    ctx_in = ext("ctx_in", (nb, P, ND, S), F32)
    lens_in = ext("lens_in", (nb, 1, 1), I32)
    out = ext("out", (nb, P, NT, D), F32, "ExternalOutput")
    program(nc, x_in, ctx_in, lens_in, w_in, out)


def kernel(**inputs):
    import concourse.bacc as bacc
    from concourse.bass_utils import run_bass_kernel_spmd
    w, x, ctx, lens = layouts(inputs)
    arrays = {"w_" + k: v for k, v in w.items()}
    arrays.update(x_in=x, ctx_in=ctx, lens_in=lens)
    nc = bacc.Bacc("TRN2", target_bir_lowering=False, num_devices=1)
    declare(nc, B)
    r = run_bass_kernel_spmd(nc, [arrays], core_ids=[0])
    y = r.results[0]["out"]
    return np.ascontiguousarray(y.transpose(0, 2, 1, 3).reshape(B, S, D))
```

```python
import numpy as np
import concourse.bass as bass
from concourse import mybir
from contextlib import ExitStack

F32 = mybir.dt.float32
BF16 = mybir.dt.bfloat16
I32 = mybir.dt.int32
ALU = mybir.AluOpType
ACT = mybir.ActivationFunctionType
AX = mybir.AxisListType

P = 128
B, S, D = 32, 256, 256
H, HD = 16, 16
XD = 64
FF = 1024
NT = S // P
ND = D // P
HT = P // HD
QR = 8
KEEP = int(S * (1.0 - 0.9))
CAP = S // 2
NJ, NU = 16, 16
QUADS = NJ // 2
EPS = 1e-5
BIG = 2.0 ** 100
FAR = 2.0 ** 100
NEG = -4.0e20
ROUNDS = (KEEP + 7) // 8
assert KEEP % 8 == 1 and ROUNDS == 4

WEIGHTS = {
    "wq0": [P, ND, D], "wq0s": [P, ND, D], "wlat": [P, ND, P], "wkb": [P, D], "wkbs": [P, D],
    "ropec": [P, D], "ropes": [P, D], "ident": [P, P], "wvb": [P, D], "wo0": [P, ND, D], "hmask": [P, HT],
    "xwq": [P, ND, H * XD], "xwk": [P, ND, H * XD], "xwv": [P, ND, H * XD], "xwo": [P, 8, D],
    "xb": [XD, 3, H], "xbo": [P, D], "wrt": [P, ND, P], "w1": [P, ND, FF], "b1": [P, FF // P],
    "w2": [P, FF // P, D], "b2": [1, D],
    "swq": [P, ND, D], "swk": [P, ND, D], "swv": [P, ND, D], "swo": [P, ND, D],
    "sbq": [P, ND], "sbk": [P, ND], "sbv": [P, D], "sbo": [P, D],
    "cwq": [P, ND, D], "cwk": [P, ND, D], "cwv": [P, ND, D], "cwo": [P, ND, D],
    "wt": [P, ND, D], "alpha": [P, 1], "fbias": [P, D],
    "lower": [P, NT, S], "iota": [P, S], "groupq": [8, NJ * H * NU], "groupk": [8, NJ * H * NU],
}


FIRST = list(WEIGHTS)[:11]


def program(nc, x_in, ctx_in, lens_in, w_in, out):
    es = ExitStack()
    with es:
        def sb(name, shape, dt=F32):
            return es.enter_context(nc.sbuf_tensor(name, shape, dt))

        def sem(name):
            return es.enter_context(nc.semaphore(name))

        skip = ("groupq", "groupk", "wt", "wq0s", "wkbs", "ropec", "ropes")
        w = {n: sb(n, shape) for n, shape in WEIGHTS.items() if n not in skip}
        weff = sb("weff", [P, ND, D])
        ones = sb("ones", [P, P])
        ones_b = sb("ones_b", [1, P], BF16)
        half_neg = sb("half_neg", [P, NT])
        bq8 = sb("bq8", [XD, H])
        tern = sb("tern", [P, 4])

        bankA = [es.enter_context(nc.psum_tensor(f"bankA{i}", [P, 512], F32)) for i in range(4)]
        bankB = [es.enter_context(nc.psum_tensor(f"bankB{i}", [P, 512], F32)) for i in range(4)]

        xin = sb("xin", [P, NT, D])
        xa = sb("xa", [P, NT, D])
        x1 = x2 = xa
        x3 = sb("x3", [P, NT, D])
        x3b = sb("x3b", [P, NT, D])
        ctxA = sb("ctxA", [P, ND, S])
        ctxB = sb("ctxB", [P, ND, S])

        def attention_buffers(p, qm, pr, pt, ot, onT, kq):
            kT, qT = (kq[:, 512 * k:512 * k + 512].rearrange("p (e s) -> p e s", e=ND) for k in range(2))
            return dict(
                p=p, qm=qm, kT=kT, va=sb(p + "va", [P, NT, H, 2 * HD]),
                qr=qm.shape[1], nm=sb(p + "nm", [P, H, NT]), pr=pr, pt=pt, ot=ot, rd=sb(p + "rd", [P, 2, NT, HT]), on=qT, onT=onT, qT=qT)

        vT_qm = sb("vT_qm", [P, NJ * H * NU])
        xq_area = sb("xq_area", [P, NJ * H * NU])
        part = lambda k: xq_area[:, 1024 * k:1024 * (k + 1)]
        lnA = dict(st=sb("lnA_st", [P, NT, 6]), mv=sb("lnA_mv", [P, NT, 2]), rs=sb("lnA_rs", [P, NT]),
                   xn=sb("lnA_xn", [P, NT, D]), xT=sb("lnA_xT", [P, ND, S]))
        lnB = dict(st=sb("lnB_st", [P, NT, 6]), mv=sb("lnB_mv", [P, NT, 2]), rs=sb("lnB_rs", [P, NT]),
                   xn=sb("lnB_xn", [P, NT, D]), xT=sb("lnB_xT", [P, ND, S]))
        lnM = dict(st=sb("lnM_st", [P, NT, 6]), mv=sb("lnM_mv", [P, NT, 2]), rs=sb("lnM_rs", [P, NT]),
                   xn=part(3)[:, 0:512].rearrange("p (t d) -> p t d", t=NT), xT=part(3)[:, 512:1024].rearrange("p (d s) -> p d s", d=ND))
        a_kq = sb("a_kq", [P, 2 * ND * S])
        bufA = attention_buffers("a_", vT_qm[:, :].rearrange("p (h s) -> p h s", h=H),
                                 part(0).rearrange("p (k t s) -> p k t s", k=2, t=NT),
                                 part(1).rearrange("p (k t s) -> p k t s", k=2, t=NT),
                                 part(2).rearrange("p (c s) -> p c s", c=4), lnM["xT"], a_kq)
        bufB = attention_buffers("b_", sb("b_qm", [P, QR, S]), sb("b_pr", [P, 2, NT, S]), sb("b_pt", [P, 2, NT, S]),
                                 sb("b_ot", [P, 4, S]), lnB["xT"], sb("b_kq", [P, 2 * ND * S]))
        latT = lnM["xn"][:, 0, :]
        xqT = xq_area[0:XD + 8, :].rearrange("p (g h u) -> p g (h u)", g=2 * NJ, h=H)
        xkT = vT_qm[0:XD + 8, :].rearrange("p (g h u) -> p g (h u)", g=2 * NJ, h=H)
        xvT = vT_qm[0:XD, :].rearrange("p (g h u) -> p g (h u)", g=2 * NJ, h=H)
        xv = sb("xv", [P, 2 * NJ, XD])
        xnm = sb("xnm", [P, 2 * NJ])
        xrs = sb("xrs", [P, 2 * NJ])
        xrr = sb("xrr", [P, 2 * NJ])
        xp2 = sb("xp", [P, 2, 4, P])
        xp = [xp2[:, 0], xp2[:, 1], lnA["xT"][:].rearrange("p d (i c) -> p (d i) c", c=P)]
        xpt = a_kq[:].rearrange("p (b i c) -> p b i c", b=2, i=4)
        xot = sb("xot", [P, QUADS, H, 2, 8])
        scol = sb("scol", [P, NT])
        srow = xv[:, 24:28, :].rearrange("p g c -> p (g c)")
        area = xv[:, :, :].rearrange("p g c -> p (g c)")
        tmpd = area[:, 0:512].rearrange("p (t s) -> p t s", t=NT)
        rank = sb("rank", [P, NT])
        gate = sb("gate", [P, NT])
        gate1 = sb("gate1", [P, NT])
        gate2 = sb("gate2", [P, NT])
        pick = area[:, 512:768].rearrange("p (t c) -> p t c", t=NT)
        pickT = area[:, 768:1024].rearrange("p (t c) -> p t c", t=NT)
        selT = area[:, 1024:1280].rearrange("p (t c) -> p t c", t=ND)
        yff = area[:, 1280:1536]
        hid = xot[:, 0:4].rearrange("p a h b c -> p (a h b c)").rearrange("p (f c) -> p f c", c=CAP)
        xh = xa
        sc = sb("sc", [P, 3, NT, S])
        wk = sb("wk", [P, 2, NT, S])
        m8 = sb("m8", [P, 2, ROUNDS - 1, NT, 8])
        m8_last = sb("m8_last", [P, 2, NT, 16])
        taken = bufB["pr"]
        sp_ = taken
        bufC = dict(bufB, kT=sc[:, 1], qT=sc[:, 2], on=sc[:, 2],
                    va=wk[:].rearrange("p a t s -> p (a t s)").rearrange("p (k h c) -> p k h c", k=NT, h=H))
        mx0 = sb("mx0", [P, H, NT])
        x4 = sb("x4", [P, NT, D])
        x5 = x4
        xo = x4
        lenb = sb("lenb", [1, 1], I32)
        lenf = sb("lenf", [1, 1])
        mrow = sb("mrow", [1, NT, S], BF16)

        w["wt"] = x4
        tern2 = x3
        w["wq0s"] = xq_area[:, 0:512].rearrange("p (e s) -> p e s", e=ND)
        w["wkbs"] = xq_area[:, 512:768]
        w["ropec"] = xq_area[:, 768:1024]
        w["ropes"] = xq_area[:, 1024:1280]

        s_w = sem("first_weights_loaded")
        s_w2 = sem("other_weights_loaded")
        s_set = sem("setup_done")
        s_sum = sem("weight_sum_ready")
        s_rope = sem("rotated")
        s_stored = sem("output_stored")
        others = []
        class Signals(dict):
            def __missing__(self, name):
                self[name] = sem(name)
                return self[name]

        g = Signals()

        with nc.Block() as block:
            @block.sync
            def _(sp):
                for n in FIRST:
                    sp.dma_start(w[n][:], w_in[n]).then_inc(s_w, 16)
                sp.dma_start(xin[:], x_in[0]).then_inc(g["x_in"], 16)
                for n in WEIGHTS:
                    if n in w and n not in FIRST:
                        sp.dma_start(w[n][:], w_in[n]).then_inc(s_w2, 16)
                        others.append(n)

            @block.vector
            def _(dve):
                nc.vector.memset(ones[:], 1.0).then_inc(s_set, 1)
                nc.vector.memset(ones_b[:], 1.0).then_inc(s_set, 1)
                nc.vector.memset(half_neg[:], -0.5).then_inc(s_set, 1)
                nc.vector.memset(m8_last[:], -BIG).then_inc(s_set, 1)
                nc.vector.memset(bufA["va"][:], 1.0).then_inc(s_set, 1)
                nc.vector.memset(bufB["va"][:], 1.0).then_inc(s_set, 1)
                dve.wait_ge(s_w, 16 * len(FIRST))
                for wt, ws, wide in ((w["wq0"], w["wq0s"], True), (w["wkb"], w["wkbs"], False)):
                    cos, sin = w["ropec"][:], w["ropes"][:]
                    if wide:
                        cos, sin = (a.unsqueeze(1).broadcast_to([P, ND, D]) for a in (cos, sin))
                    nc.vector.tensor_tensor(wt[:], wt[:], cos, ALU.mult).then_inc(s_rope, 1)
                    nc.vector.tensor_tensor(ws[:], ws[:], sin, ALU.mult).then_inc(s_rope, 1)
                dve.wait_ge(s_rope, 4)
                nc.vector.tensor_tensor(w["wq0"][:], w["wq0"][:], w["wq0s"][:], ALU.add).then_inc(s_rope, 1)
                nc.vector.tensor_tensor(w["wkb"][:], w["wkb"][:], w["wkbs"][:], ALU.add).then_inc(s_rope, 1)
                dve.wait_ge(s_rope, 6)
                dve.wait_ge(s_set, 6)

        def setup_rest():
            n0 = 6
            with nc.Block() as block:
                @block.sync
                def _(sp):
                    sp.wait_ge(s_w2, 16 * len(others))

                @block.tensor
                def _(pe):
                    pe.wait_ge(s_set, n0 + 1)
                    nc.tensor.matmul(bankA[0][:, 0:1], ones[:], tern[:, 0:1], start=True, stop=True).then_inc(s_sum, 1)

                @block.vector
                def _(dve):
                    dve.wait_ge(s_w2, 16 * len(others))
                    nc.vector.tensor_reduce(tern[:, 0:1], w["wt"][:], AX.XY, ALU.add,
                                            apply_absolute_value=True).then_inc(s_set, 1)
                    nc.vector.tensor_scalar(bq8[:], w["xb"][:, 0, :], XD ** -0.5, None, ALU.mult).then_inc(s_set, 1)
                    dve.wait_ge(s_sum, 1)
                    nc.vector.tensor_scalar(tern[:, 1:2], bankA[0][:, 0:1], 1.0 / (D * D), 0.7, ALU.mult, ALU.mult).then_inc(s_set, 1)
                    nc.vector.tensor_scalar(tern[:, 2:3], bankA[0][:, 0:1], 1.0 / (D * D), -0.7, ALU.mult, ALU.mult).then_inc(s_set, 1)
                    dve.wait_ge(s_set, n0 + 4)
                    nc.vector.tensor_scalar(weff[:], w["wt"][:], tern[:, 1:2], w["alpha"][:, 0:1], ALU.is_gt, ALU.mult).then_inc(s_set, 1)
                    nc.vector.tensor_scalar(tern2[:], w["wt"][:], tern[:, 2:3], w["alpha"][:, 0:1], ALU.is_lt, ALU.mult).then_inc(s_set, 1)
                    dve.wait_ge(s_set, n0 + 6)
                    nc.vector.tensor_tensor(weff[:], weff[:], tern2[:], ALU.subtract).then_inc(s_set, 1)
                    dve.wait_ge(s_set, n0 + 7)

        def ln_dve(dve, k, x, ln, ready):
            for s, v in ready:
                dve.wait_ge(s, v)
            for t in range(NT):
                nc.vector.bn_stats(ln["st"][:, t, :], x[:, t, :]).then_inc(g[f"ln{k}_stat"], 1)
            dve.wait_ge(g[f"ln{k}_stat"], 2)
            for t in range(NT):
                nc.vector.bn_aggr(ln["mv"][:, t, :], ln["st"][:, t, :]).then_inc(g[f"ln{k}_stat"], 1)

        def ln_pool(pool, k, ln):
            pool.wait_ge(g[f"ln{k}_stat"], 4)
            nc.gpsimd.tensor_scalar(ln["rs"][:], ln["mv"][:, :, 1], EPS, 1.0, ALU.add, ALU.mult).then_inc(g[f"ln{k}_stat"], 1)
            pool.wait_ge(g[f"ln{k}_stat"], 5)
            nc.gpsimd.tensor_tensor(ln["rs"][:], ln["rs"][:], half_neg[:], ALU.pow).then_inc(g[f"ln{k}_rstd"], 1)

        def ln_dve2(dve, k, x, ln):
            dve.wait_ge(g[f"ln{k}_rstd"], 1)
            for t in range(NT):
                nc.vector.tensor_scalar(ln["xn"][:, t, :], x[:, t, :], ln["mv"][:, t, 0:1], ln["rs"][:, t:t + 1],
                                        ALU.subtract, ALU.mult).then_inc(g[f"ln{k}_xn"], 1)

        def ln_pe(pe, k, ln, bank):
            pe.wait_ge(g[f"ln{k}_xn"], 2)
            for d in range(ND):
                for t in range(NT):
                    last = nc.tensor.transpose(bank[:, d * S + t * P:d * S + (t + 1) * P],
                                               ln["xn"][:, t, d * P:(d + 1) * P], w["ident"][:])
            last.then_inc(g[f"ln{k}_tr"], 1)

        def ln_act(act, k, ln, bank):
            act.wait_ge(g[f"ln{k}_tr"], 1)
            nc.scalar.activation(ln["xT"][:].rearrange("p d s -> p (d s)"), bank[:], ACT.Copy).then_inc(g[f"ln{k}_xT"], 1)

        def project_T(bank, wt, xT, done):
            for e in range(ND):
                for d in range(ND):
                    last = nc.tensor.matmul(bank[:, e * S:(e + 1) * S], wt[:, d, e * P:(e + 1) * P], xT[:, d, :],
                                            start=(d == 0), stop=(d == ND - 1))
            last.then_inc(done, 1)

        def project_N(bank, xT, wt, done):
            for t in range(NT):
                for d in range(ND):
                    last = nc.tensor.matmul(bank[:, t * D:(t + 1) * D], xT[:, d, t * P:(t + 1) * P], wt[:, d, :],
                                            start=(d == 0), stop=(d == ND - 1))
            last.then_inc(done, 1)

        def at_scores(pe, n, b, bank, h, free, per, masked=False):
            pe.wait_ge(g[n + "_qm"], h // 2 + 1)
            if h >= 2:
                pe.wait_ge(free, per * (h - 1))
            if masked:
                nc.tensor.matmul(bank[:], ones_b[:], mrow[:].rearrange("p t s -> p (t s)"), start=True, stop=False,
                                 skip_group_check=True)
            for t in range(NT):
                last = nc.tensor.matmul(bank[:, t * S:(t + 1) * S], b["qm"][:, h % b["qr"], t * P:(t + 1) * P],
                                        b["kT"][:, h // HT, :], start=not masked, stop=True, skip_group_check=masked)
            last.then_inc(g[n + "_s"], 1)

        def at_transpose(pe, n, b, bank, h):
            pe.wait_ge(g[n + "_ex"], NT * (h + 1))
            if h >= 1:
                pe.wait_ge(g[n + "_pt"], h)
            for c in range(NT):
                for t in range(NT):
                    last = nc.tensor.transpose(bank[:, c * S + t * P:c * S + (t + 1) * P],
                                               b["pr"][:, h % 2, t, c * P:(c + 1) * P], w["ident"][:])
            last.then_inc(g[n + "_tr"], 1)

        def at_copy_pt(act, n, b, bank, h):
            act.wait_ge(g[n + "_tr"], h + 1)
            if h >= 2:
                act.wait_ge(g[n + "_pv"], h // 2)
            nc.scalar.activation(b["pt"][:, h % 2].rearrange("p c s -> p (c s)"), bank[:], ACT.Copy).then_inc(g[n + "_pt"], 1)

        def at_values(pe, n, b, bank, h):
            pe.wait_ge(g[n + "_pt"], h + 2)
            if h == 8:
                pe.wait_ge(g[n + "_ot"], 1)
            c = P * ((h // 2) % 4)
            for k in range(NT):
                for j in range(2):
                    for t in range(NT):
                        r = 32 * (2 * j + t)
                        last = nc.tensor.matmul(bank[r:r + 32, c:c + P], b["va"][:, k, h + j, :], b["pt"][:, j, k, t * P:(t + 1) * P],
                                                start=(k == 0), stop=(k == NT - 1))
            last.then_inc(g[n + "_pv"], 1)

        def at_copy_ot(act, n, b, bank, half):
            act.wait_ge(g[n + "_pv"], 4 * (half + 1))
            nc.scalar.activation(b["ot"][:, 2 * half:2 * half + 2].rearrange("p c s -> p (c s)"), bank[:], ACT.Copy).then_inc(g[n + "_ot"], 1)

        def at_out_pe1(pe, n, b, banks):
            pe.wait_ge(g[n + "_ot"], 2)
            for half in range(2):
                for q in range(4):
                    last = nc.tensor.transpose(banks[half][:, q * P:(q + 1) * P],
                                               b["ot"][:, 2 * half + q // 2, (q % 2) * P:(q % 2 + 1) * P], w["ident"][:])
            last.then_inc(g[n + "_ott"], 1)

        def at_out_dve(dve, n, b, banks):
            dve.wait_ge(g[n + "_ott"], 1)
            view = lambda k: banks[k][:].rearrange("p (h t c) -> p t h c", t=NT, c=2 * HD)
            for half in range(2):
                nc.vector.reciprocal(b["rd"][:, half], view(half)[:, :, :, HD]).then_inc(g[n + "_rd"], 1)
            for half in range(2):
                dve.wait_ge(g[n + "_rd"], half + 1)
                nc.vector.tensor_tensor(b["on"][:, :, half * P:(half + 1) * P].rearrange("p t (h c) -> p t h c", c=HD),
                                        view(half)[:, :, :, 0:HD],
                                        b["rd"][:, half].unsqueeze(3).broadcast_to([P, NT, HT, HD]), ALU.mult).then_inc(g[n + "_on"], 1)

        def at_out_pe2(pe, n, b, bank):
            pe.wait_ge(g[n + "_on"], 2)
            for e in range(ND):
                for t in range(NT):
                    last = nc.tensor.transpose(bank[:, e * S + t * P:e * S + (t + 1) * P], b["on"][:, t, e * P:(e + 1) * P], w["ident"][:])
            last.then_inc(g[n + "_ont"], 1)

        def at_out_act(act, n, b, bank):
            act.wait_ge(g[n + "_ont"], 1)
            nc.scalar.activation(b["onT"][:].rearrange("p e s -> p (e s)"), bank[:], ACT.Copy).then_inc(g[n + "_onT"], 1)

        def at_mask_q(pool, n, b, c):
            h = 2 * c
            r = h % b["qr"]
            if h >= b["qr"]:
                pool.wait_ge(g[n + "_s"], h - b["qr"] + 2)
            nc.gpsimd.tensor_tensor(b["qm"][:, r:r + 2, :], b["qT"][:, h // HT, :].unsqueeze(1).broadcast_to([P, 2, S]),
                                    w["hmask"][:, h % HT:h % HT + 2].unsqueeze(2).broadcast_to([P, 2, S]),
                                    ALU.mult).then_inc(g[n + "_qm"], 1)

        def at_mask_later(pool, n, b, s):
            if s % 2 == 0 and QR // 2 <= (s + 6) // 2 < H // 2:
                at_mask_q(pool, n, b, (s + 6) // 2)

        HS = H + 3

        def exps(act, n, b, bank, h):
            act.wait_ge(g[n + "_nm"], h + 1)
            if h >= 2:
                act.wait_ge(g[n + "_tr"], h - 1)
            for t in range(NT):
                a = nc.scalar.activation(b["pr"][:, h % 2, t, :], bank[:, t * S:(t + 1) * S], ACT.Exp,
                                         bias=b["nm"][:, h, t:t + 1])
                a.then_inc(g[n + "_ex"], 1)


        def scores_max(dve, n, b, bank, h):
            dve.wait_ge(g[n + "_s"], h + 1)
            nc.vector.tensor_reduce(b["nm"][:, h, :], bank[:].rearrange("p (t s) -> p t s", t=NT), AX.X, ALU.max,
                                    negate=True).then_inc(g[n + "_nm"], 1)

        def copy_all(act, dst, bank, ready, done):
            act.wait_ge(ready, 1)
            nc.scalar.activation(dst[:].rearrange("p e s -> p (e s)"), bank[:], ACT.Copy).then_inc(done, 1)

        def copy_values(act, n, b, bank):
            act.wait_ge(g[n + "_v"], 1)
            nc.scalar.activation(b["va"][:, :, :, 0:HD], bank[:].rearrange("p (t h c) -> p t h c", t=NT, c=HD),
                                 ACT.Copy).then_inc(g[n + "_va"], 1)

        def add_rows(dve, out, bank, rows, ready, done):
            dve.wait_ge(ready, 1)
            nc.vector.tensor_tensor(out[:].rearrange("p t d -> p (t d)"), bank[:], rows[:].rearrange("p t d -> p (t d)"), ALU.add).then_inc(done, 1)

        A1 = 0
        A2 = A1 + 12
        A3 = A2 + QUADS + 4
        M0 = A3 + 8
        AO = M0 + HS
        NA = AO + 3

        def tensor_a(pe):
            b = bufA
            if mode["mix"]:
                for k in range(12):
                    which, quad = k // 4, k % 4
                    yield A1 + k
                    if k == 4:
                        pe.wait_ge(g["ln1_xT"], 1)
                    if k >= 2:
                        pe.wait_ge(g["hm_ev"], 4 * (k - 1))
                    wt, src = (("xwv", ctxA), ("xwq", lnA["xT"]), ("xwk", ctxA))[which]
                    for hp in range(2):
                        for d in range(ND):
                            c = (quad * 2 + hp) * P
                            last = nc.tensor.matmul(bankA[k % 2][:, hp * S:(hp + 1) * S], w[wt][:, d, c:c + P], src[:, d, :],
                                                    start=(d == 0), stop=(d == ND - 1))
                    last.then_inc(g["hm_proj"], 1)
                    if k == 1:
                        yield A1 + 1.6
                        ln_pe(pe, 1, lnA, bankA[2])
                    if 4 <= k < 8:
                        yield A1 + k + 0.5
                        v = k - 4
                        pe.wait_ge(g["hm_ev"], 16)
                        if v >= 2:
                            pe.wait_ge(g["hm_vev"], v - 1)
                        for i in range(8):
                            last = nc.tensor.transpose(bankA[2 + v % 2][:, i * XD:(i + 1) * XD], xvT[:, v * 8 + i, :], w["ident"][0:XD, 0:XD])
                        last.then_inc(g["hm_vtr"], 1)
                for s in range(QUADS + 4):
                    yield A2 + s
                    if s == 0:
                        pe.wait_ge(g["hm_ev"], 48)
                        pe.wait_ge(g["group_in"], 32)
                    if 3 <= s < QUADS + 3:
                        q = s - 3
                        pe.wait_ge(g["hm_pn"], q + 1)
                        pe.wait_ge(g["hm_vev"], 4)
                        if q >= 1:
                            pe.wait_ge(g["hm_pt"], q)
                        for i in range(4):
                            last = nc.tensor.transpose(bankA[2][:, i * P:(i + 1) * P], xp[q % 3][:, i, :], w["ident"][:])
                        last.then_inc(g["hm_tr"], 1)
                    if s < QUADS:
                        if s >= 2:
                            pe.wait_ge(g["hm_ex"], 4 * (s - 1))
                        for i in range(4):
                            c = 4 * s + i
                            last = nc.tensor.matmul(bankA[s % 2][:, i * P:(i + 1) * P], xqT[:, c, :], xkT[:, c, :], start=True, stop=True)
                        last.then_inc(g["hm_s"], 1)
                    if s >= 4:
                        q = s - 4
                        pe.wait_ge(g["hm_pt"], q + 1)
                        if q >= 1:
                            pe.wait_ge(g["hm_ot"], q)
                        for uh in range(2):
                            for jo in range(2):
                                i = jo * 2 + uh
                                last = nc.tensor.matmul(bankA[3][jo * XD:(jo + 1) * XD, uh * P:(uh + 1) * P],
                                                        xv[:, 4 * q + i, :], xpt[:, q % 2, i, :], start=True, stop=True)
                        last.then_inc(g["hm_o"], 1)
                yield A3
                pe.wait_ge(g["hm_ot"], QUADS)
                for t in range(NT):
                    for jp in range(QUADS):
                        last = nc.tensor.matmul(bankA[0][:, t * D:(t + 1) * D],
                                                xot[:, jp, 8 * t:8 * t + 8].rearrange("p h a b -> p (h a b)"),
                                                w["xwo"][:, jp, :], start=(jp == 0), stop=(jp == QUADS - 1))
                last.then_inc(g["hm_y"], 1)
            if mode["mla"]:
                yield A3 - 0.3
                ln_pe(pe, 0, lnM, bankA[3])
            if mode["mix"]:
                yield A3 + 1.9
                ln_pe(pe, 2, lnA, bankA[1])
                yield A3 + 3.7
                pe.wait_ge(g["ln2_xT"], 1)
                for d in range(ND):
                    last = nc.tensor.matmul(bankA[2][:, 0:S], w["wrt"][:, d, :], lnA["xT"][:, d, :], start=(d == 0), stop=(d == ND - 1))
                last.then_inc(g["md_sps"], 1)
            if mode["mla"]:
                yield A3 + 2
                pe.wait_ge(g["ln0_xT"], 1)
                for d in range(ND):
                    last = nc.tensor.matmul(bankA[3][:, 0:S], w["wlat"][:, d, :], lnM["xT"][:, d, :], start=(d == 0), stop=(d == ND - 1))
                last.then_inc(g["lat_ps"], 1)
                project_T(bankA[1], w["wq0"], lnM["xT"], g["mla_q"])
                yield A3 + 3.6
                pe.wait_ge(g["latT"], 1)
                if mode["mix"]:
                    pe.wait_ge(g["md_srow"], 1)
                for e in range(ND):
                    last = nc.tensor.matmul(bankA[2][:, e * S:(e + 1) * S], w["wkb"][:, e * P:(e + 1) * P], latT, start=True, stop=True)
                last.then_inc(g["mla_k"], 1)
                for t in range(NT):
                    last = nc.tensor.matmul(bankA[3][:, t * D:(t + 1) * D], latT[:, t * P:(t + 1) * P], w["wvb"][:], start=True, stop=True)
                last.then_inc(g["mla_v"], 1)
            if mode["mix"]:
                yield A3 + 4
                pe.wait_ge(g["md_e"], 6)
                for d in range(ND):
                    for t in range(NT):
                        last = nc.tensor.matmul(bankA[0][:, d * P:(d + 1) * P], lnA["xn"][:, t, d * P:(d + 1) * P], pick[:, t, :],
                                                start=(t == 0), stop=(t == NT - 1))
                last.then_inc(g["md_sel"], 1)
                if mode["mla"]:
                    pe.wait_ge(g["mla_va"], 1)
                for t in range(NT):
                    last = nc.tensor.transpose(bankA[3][:, t * P:(t + 1) * P], pick[:, t, :], w["ident"][:])
                last.then_inc(g["md_ptr"], 1)
                for k in range(2):
                    yield A3 + 5 + 0.3 * k + 0.4
                    pe.wait_ge(g["md_selT"], 1)
                    if mode["mla"]:
                        pe.wait_ge(g[("mla_qT", "mla_kT")[k]], 1)
                    for f in range(4):
                        for d in range(ND):
                            c = (4 * k + f) * P
                            last = nc.tensor.matmul(bankA[1 + k][:, f * P:(f + 1) * P], w["w1"][:, d, c:c + P], selT[:, d, :],
                                                    start=(d == 0), stop=(d == ND - 1))
                    last.then_inc(g["md_h"], 1)
                yield A3 + 5.6
                for f in range(FF // P):
                    pe.wait_ge(g["md_hid"], f + 1)
                    nc.tensor.matmul(bankA[0][:, 0:D], hid[:, f, :], w["w2"][:, f, :], start=(f == 0), stop=False)
                nc.tensor.matmul(bankA[0][:, 0:D], ones[0:1, :], w["b2"][:], start=False, stop=True).then_inc(g["md_y"], 1)
                yield A3 + 7
                pe.wait_ge(g["md_yff"], 1)
                pe.wait_ge(g["md_pickT"], 1)
                for t in range(NT):
                    last = nc.tensor.matmul(bankA[3][:, t * D:(t + 1) * D], pickT[:, t, :], yff[:], start=True, stop=True)
                last.then_inc(g["md_u"], 1)
            for h in range(HS):
                if h == 2 and mode["mix"]:
                    yield M0 + 1.5
                    ln_pe(pe, 3, lnA, bankA[3])
                if mode["mla"]:
                    yield M0 + h
                    if h == 0:
                        pe.wait_ge(g["mla_kT"], 1)
                        pe.wait_ge(g["mla_va"], 1)
                    if h == 4 and mode["mix"]:
                        pe.wait_ge(g["ln3_xT"], 1)
                    if h >= 4 and h % 2 == 0:
                        at_values(pe, "mla", b, bankA[3], h - 4)
                    if 2 <= h < H + 2:
                        at_transpose(pe, "mla", b, bankA[2], h - 2)
                    if h < H:
                        at_scores(pe, "mla", b, bankA[h % 2], h, g["mla_ex"], NT)
            if mode["mla"]:
                yield AO + 0.2
                at_out_pe1(pe, "mla", b, bankA[0:2])
                yield AO + 0.8
                at_out_pe2(pe, "mla", b, bankA[2])
                yield AO + 2.2
                pe.wait_ge(g["mla_onT"], 1)
                project_N(bankA[3], b["onT"], w["wo0"], g["mla_y"])
            if mode["mix"]:
                yield AO + 1
                pe.wait_ge(g["ln3_xT"], 1)
                project_T(bankA[0], w["swq"], lnA["xT"], g["spa_q"])
                project_T(bankA[1], w["swk"], lnA["xT"], g["spa_k"])
                project_N(bankA[2], lnA["xT"], w["swv"], g["spa_v"])

        def scalar_a(act):
            b = bufA
            if mode["mix"]:
                for k in range(12):
                    which, quad = k // 4, k % 4
                    yield A1 + k + 0.4
                    act.wait_ge(g["hm_proj"], k + 1)
                    if k == 8:
                        act.wait_ge(g["hm_vtr"], 4)
                    dst = (xvT, xqT, xkT)[which]
                    bias = (w["xb"][:, 2], bq8, w["xb"][:, 1])[which]
                    for hp in range(2):
                        for o in range(2):
                            h = 4 * quad + 2 * hp + o
                            nc.scalar.activation(dst[0:XD, :, 8 * h:8 * h + 8].rearrange("p (j a) u -> p j a u", a=2),
                                                 bankA[k % 2][o * XD:(o + 1) * XD, hp * S:(hp + 1) * S].rearrange("p (a u j) -> p j a u", a=2, j=NJ),
                                                 ACT.Identity, bias=bias[:, h:h + 1],
                                                 scale=(XD ** -0.5 if which == 1 else 1.0)).then_inc(g["hm_ev"], 1)
                    if k == 2:
                        yield A1 + 2.3
                        ln_act(act, 1, lnA, bankA[2])
                    if 4 <= k < 8:
                        v = k - 4
                        yield A1 + k + 0.3
                        act.wait_ge(g["hm_vtr"], v + 1)
                        nc.scalar.activation(xv[:, 8 * v:8 * v + 8, :].rearrange("p g c -> p (g c)"), bankA[2 + v % 2][:], ACT.Copy).then_inc(g["hm_vev"], 1)
                for s in range(QUADS + 4):
                    yield A2 + s + 0.2
                    if 3 <= s < QUADS + 3:
                        q = s - 3
                        act.wait_ge(g["hm_tr"], q + 1)
                        if q >= 2:
                            act.wait_ge(g["hm_o"], q - 1)
                        nc.scalar.activation(xpt[:, q % 2].rearrange("p g c -> p (g c)"), bankA[2][:], ACT.Copy).then_inc(g["hm_pt"], 1)
                    yield A2 + s + 0.9
                    if s < QUADS:
                        act.wait_ge(g["hm_nm"], s + 1)
                        for i in range(4):
                            c = 4 * s + i
                            nc.scalar.activation(xp[s % 3][:, i, :], bankA[s % 2][:, i * P:(i + 1) * P], ACT.Exp,
                                                 bias=xnm[:, c:c + 1], accum_out=xrs[:, c:c + 1]).then_inc(g["hm_ex"], 1)
                    yield A2 + s + 0.9
                    if s >= 4:
                        q = s - 4
                        act.wait_ge(g["hm_o"], q + 1)
                        for uh in range(2):
                            a = nc.scalar.activation(xot[:, q, :, uh, :], bankA[3][:, uh * P:(uh + 1) * P].rearrange("p (h u) -> p h u", u=8), ACT.Copy)
                        a.then_inc(g["hm_ot"], 1)
            if mode["mla"]:
                yield A3 + 1.1
                ln_act(act, 0, lnM, bankA[3])
            if mode["mix"]:
                yield A3 + 2
                ln_act(act, 2, lnA, bankA[1])
                yield A3 + 3.1
                act.wait_ge(g["md_sps"], 1)
                nc.scalar.activation(srow[:], bankA[2][:, 0:S], ACT.Copy).then_inc(g["md_srow"], 1)
            if mode["mla"]:
                yield A3 + 3
                act.wait_ge(g["lat_ps"], 1)
                nc.scalar.activation(latT, bankA[3][:, 0:S], ACT.Copy).then_inc(g["latT"], 1)
                copy_all(act, b["qT"], bankA[1], g["mla_q"], g["mla_qT"])
                yield A3 + 3.2
                copy_all(act, b["kT"], bankA[2], g["mla_k"], g["mla_kT"])
                copy_values(act, "mla", b, bankA[3])
            if mode["mix"]:
                yield A3 + 3
                act.wait_ge(g["md_e"], 2)
                nc.scalar.activation(gate[:], scol[:], ACT.Exp, scale=-1.0).then_inc(g["md_gate"], 1)
                yield A3 + 4
                act.wait_ge(g["md_sel"], 1)
                nc.scalar.activation(selT[:].rearrange("p d c -> p (d c)"), bankA[0][:, 0:D], ACT.Copy).then_inc(g["md_selT"], 1)
                act.wait_ge(g["md_ptr"], 1)
                nc.scalar.activation(pickT[:].rearrange("p d c -> p (d c)"), bankA[3][:, 0:D], ACT.Copy).then_inc(g["md_pickT"], 1)
                yield A3 + 5.5
                for k in range(2):
                    act.wait_ge(g["md_h"], k + 1)
                    for f in range(4):
                        nc.scalar.activation(hid[:, 4 * k + f, :], bankA[1 + k][:, f * P:(f + 1) * P], ACT.Gelu_apprx_tanh,
                                             bias=w["b1"][:, 4 * k + f:4 * k + f + 1]).then_inc(g["md_hid"], 1)
                yield A3 + 7
                act.wait_ge(g["md_y"], 1)
                nc.scalar.activation(yff[:], bankA[0][:, 0:D], ACT.Copy).then_inc(g["md_yff"], 1)
            for h in range(HS):
                if h == 2 and mode["mix"]:
                    yield M0 + 1.5
                    ln_act(act, 3, lnA, bankA[3])
                if mode["mla"]:
                    yield M0 + 0.2 + h - 0.3
                    if h == 11:
                        at_copy_ot(act, "mla", b, bankA[3], 0)
                    if 2 <= h < H + 2:
                        at_copy_pt(act, "mla", b, bankA[2], h - 2)
                    yield M0 + 0.7 + h + 0.3
                    if h < H:
                        exps(act, "mla", b, bankA[h % 2], h)
            if mode["mla"]:
                yield AO + 0.3
                at_copy_ot(act, "mla", b, bankA[3], 1)
                yield AO + 1.8
                at_out_act(act, "mla", b, bankA[2])
            if mode["mix"]:
                yield AO + 1.6
                for n, bank, dst, bias in (("spa_q", bankA[0], "qT", "sbq"), ("spa_k", bankA[1], "kT", "sbk")):
                    act.wait_ge(g[n], 1)
                    for e in range(ND):
                        nc.scalar.activation(bufB[dst][:, e, :], bank[:, e * S:(e + 1) * S], ACT.Identity,
                                             bias=w[bias][:, e:e + 1]).then_inc(g["spa_" + dst], 1)

        def vector_a(dve):
            b = bufA
            link = chain(dve, "dveA")
            if mode["mix"]:
                yield A1 - 0.9
                ln_dve(dve, 1, x1, lnA, [])
                yield A1 + 1.7
                ln_dve2(dve, 1, x1, lnA)
                for s in range(QUADS + 1):
                    yield A2 + s + 0.2
                    if s < QUADS:
                        dve.wait_ge(g["hm_s"], s + 1)
                        nc.vector.tensor_reduce(xnm[:, 4 * s:4 * s + 4], bankA[s % 2][:].rearrange("p (i c) -> p i c", i=4), AX.X, ALU.max,
                                                negate=True).then_inc(g["hm_nm"], 1)
                    if s >= 1:
                        q = s - 1
                        dve.wait_ge(g["hm_ex"], 4 * q + 4)
                        nc.vector.reciprocal(xrr[:, 4 * q:4 * q + 4], xrs[:, 4 * q:4 * q + 4]).then_inc(g["hm_rr"], 1)
            if mode["mla"]:
                yield A2 + QUADS - 0.5
                ln_dve(dve, 0, xin, lnM, [(g["x_in"], 16)])
                yield A2 + QUADS + 2
                ln_dve2(dve, 0, xin, lnM)
            if mode["mix"]:
                yield A3 + 1.5
                dve.wait_ge(g["hm_xb"], 1)
                add_rows(dve, x2, bankA[0], xh, g["hm_y"], g["hm_x2"])
                yield A3 + 1
                ln_dve(dve, 2, x2, lnA, [(g["hm_x2"], 1)])
                yield A3 + 1.6
                ln_dve2(dve, 2, x2, lnA)
                yield A3 + 5.4
                dve.wait_ge(g["md_srow"], 1)
                for t in range(NT):
                    nc.vector.scalar_tensor_tensor(tmpd[:, t, 0:P], srow[:, t * P:(t + 1) * P], 1.0, w["ident"][:], ALU.mult, ALU.mult,
                                                   accum_out=scol[:, t:t + 1]).then_inc(g["md_e"], 1)
                for t in range(NT):
                    dve.wait_ge(g["md_e"], 1 + t)
                    link.inc(nc.vector.scalar_tensor_tensor(tmpd[:, t, :], srow[:], scol[:, t:t + 1], w["lower"][:, t, :], ALU.is_equal, ALU.mult))
                for t in range(NT):
                    link.wait(link.n - 1 + t)
                    nc.vector.scalar_tensor_tensor(tmpd[:, t, :], srow[:], scol[:, t:t + 1], tmpd[:, t, :], ALU.is_gt, ALU.add,
                                                   accum_out=rank[:, t:t + 1]).then_inc(g["md_e"], 1)
                for t in range(NT):
                    dve.wait_ge(g["md_e"], 3 + t)
                    nc.vector.tensor_scalar(pick[:, t, :], w["iota"][:, 0:CAP], rank[:, t:t + 1], None, ALU.is_equal).then_inc(g["md_e"], 1)
                yield A3 + 3.3
                dve.wait_ge(g["md_gate"], 1)
                nc.vector.tensor_scalar(gate1[:], gate[:], 1.0, None, ALU.add).then_inc(g["md_e"], 1)
                dve.wait_ge(g["md_e"], 7)
                nc.vector.reciprocal(gate2[:], gate1[:]).then_inc(g["md_e"], 1)
                yield A3 + 7.6
                dve.wait_ge(g["md_u"], 1)
                dve.wait_ge(g["md_xh"], 1)
                dve.wait_ge(g["md_e"], 8)
                if waits_b():
                    dve.wait_ge(g["sp_xb"], 1)
                for t in range(NT):
                    nc.vector.scalar_tensor_tensor(x3[:, t, :], bankA[3][:, t * D:(t + 1) * D], gate2[:, t:t + 1], xh[:, t, :],
                                                   ALU.mult, ALU.add).then_inc(g["md_x3"], 1)
                yield A3 + 7.7
                ln_dve(dve, 3, x3, lnA, [(g["md_x3"], 2)])
                yield A3 + 8.9
                ln_dve2(dve, 3, x3, lnA)
            if mode["mla"]:
                for h in range(H):
                    yield M0 + 0.4 + h
                    scores_max(dve, "mla", b, bankA[h % 2], h)
                yield AO + 1.2
                at_out_dve(dve, "mla", b, bankA[0:2])
                yield AO + 1.8
                add_rows(dve, x1, bankA[3], xin, g["mla_y"], g["mla_x"])
            if mode["mix"]:
                yield AO + 3
                dve.wait_ge(g["spa_v"], 1)
                nc.vector.tensor_tensor(bufB["va"][:, :, :, 0:HD], bankA[2][:].rearrange("p (t h c) -> p t h c", t=NT, c=HD),
                                        w["sbv"][:].rearrange("p (h c) -> p h c", c=HD).unsqueeze(1).broadcast_to([P, NT, H, HD]),
                                        ALU.add).then_inc(g["spa_va"], 1)

        def pool_a(pool):
            b = bufA
            if mode["mix"]:
                yield A1 + 0.3
                ln_pool(pool, 1, lnA)
                yield A1 + 2.8
                pool.wait_ge(g["ln1_xn"], 2)
                nc.gpsimd.tensor_tensor(xh[:], x1[:], w["xbo"][:].unsqueeze(1).broadcast_to([P, NT, D]), ALU.add).then_inc(g["hm_xb"], 1)
                for q in range(QUADS):
                    yield A2 + q + 1.3
                    pool.wait_ge(g["hm_rr"], q + 1)
                    nc.gpsimd.tensor_tensor(xp[q % 3], xp[q % 3],
                                            xrr[:, 4 * q:4 * q + 4].unsqueeze(2).broadcast_to([P, 4, P]), ALU.mult).then_inc(g["hm_pn"], 1)
            if mode["mla"]:
                yield A2 + QUADS + 0.9
                ln_pool(pool, 0, lnM)
            if mode["mix"]:
                yield A3 + 1.4
                ln_pool(pool, 2, lnA)
                yield A3 + 2
                pool.wait_ge(g["ln2_xn"], 2)
                nc.gpsimd.tensor_tensor(xh[:], x2[:], lnA["xn"][:], ALU.add).then_inc(g["md_xh"], 1)
            if mode["mla"]:
                yield A3 + 3.9
                pool.wait_ge(g["mla_qT"], 1)
                for c in range(H // 2):
                    yield A3 + 3.6 + 0.55 * c - 0.8
                    at_mask_q(pool, "mla", b, c)
            if mode["mix"]:
                yield A3 + 7.9
                ln_pool(pool, 3, lnA)

        BS = H + 4
        BO = 3 + BS
        C0 = BO + 2
        CO = C0 + 2 + HS
        L0 = CO + 2
        NB = L0 + 2

        def tensor_b(pe):
            b = bufB
            for s in range(BS):
                yield 3.1 + s
                if s < H:
                    at_scores(pe, "spa", b, bankB[s % 2], s, g["sp_sc"], 1)
                if s >= 5 and s % 2 == 1:
                    at_values(pe, "spa", b, bankB[3], s - 5)
                if s == 16:
                    pe.wait_ge(g["ctxB_in"], 16)
                    pe.wait_ge(g["sp_sc"], 15)
                    project_T(bankB[0], w["cwk"], ctxB, g["crs_k"])
                if s == 17:
                    pe.wait_ge(g["sp_sc"], 16)
                    project_N(bankB[1], ctxB, w["cwv"], g["crs_v"])
                if 3 <= s < H + 3:
                    at_transpose(pe, "spa", b, bankB[2], s - 3)
            yield BO + 0.4
            pe.wait_ge(g["crs_kT"], 1)
            pe.wait_ge(g["crs_va"], 1)
            at_out_pe1(pe, "spa", b, bankB[0:2])
            yield BO + 0.3
            at_out_pe2(pe, "spa", b, bankB[2])
            yield BO + 1.4
            pe.wait_ge(g["spa_onT"], 1)
            project_N(bankB[3], b["onT"], w["swo"], g["spa_y"])
            yield C0 + 0.5
            ln_pe(pe, 4, lnB, bankB[2])
            yield C0 + 1.7
            pe.wait_ge(g["ln4_xT"], 1)
            project_T(bankB[0], w["cwq"], lnB["xT"], g["crs_q"])
            for h in range(HS):
                yield C0 + 2 + h
                if h == 0:
                    pe.wait_ge(g["crs_kT"], 1)
                    pe.wait_ge(g["mask_row"], 1)
                    pe.wait_ge(g["crs_ones"], 1)
                if h >= 4 and h % 2 == 0:
                    at_values(pe, "crs", bufC, bankB[3], h - 4)
                if 2 <= h < H + 2:
                    at_transpose(pe, "crs", bufC, bankB[2], h - 2)
                if h < H:
                    at_scores(pe, "crs", bufC, bankB[h % 2], h, g["crs_ex"], NT, masked=True)
            yield CO
            at_out_pe1(pe, "crs", bufC, bankB[0:2])
            yield CO + 0.7
            at_out_pe2(pe, "crs", bufC, bankB[2])
            yield CO + 1.4
            pe.wait_ge(g["crs_onT"], 1)
            project_N(bankB[3], b["onT"], w["cwo"], g["crs_y"])
            yield L0 + 0.8
            ln_pe(pe, 5, lnB, bankB[0])
            yield L0 + 0.2
            pe.wait_ge(g["ln5_xT"], 1)
            project_N(bankB[1], lnB["xT"], weff, g["lin_y"])

        def scalar_b(act):
            b = bufB
            for s in range(BS):
                yield 3.1 + s
                if 2 <= s < H + 2:
                    h = s - 2
                    act.wait_ge(g["sp_top"], h + 1)
                    if h >= 2:
                        act.wait_ge(g["spa_tr"], h - 1)
                    nc.scalar.activation(taken[:, h % 2].rearrange("p t s -> p (t s)"), wk[:, h % 2].rearrange("p t s -> p (t s)"),
                                         ACT.Relu, bias=-1.0, scale=-2.0 / BIG).then_inc(g["sp_tk"], 1)
                yield 1.8 + s
                if s < H:
                    act.wait_ge(g["spa_s"], s + 1)
                    if s >= 3:
                        act.wait_ge(g["sp_mul"], s - 2)
                    nc.scalar.activation(sc[:, s % 3].rearrange("p t s -> p (t s)"), bankB[s % 2][:], ACT.Copy).then_inc(g["sp_sc"], 1)
                yield 3.3 + s
                if s == 12:
                    at_copy_ot(act, "spa", b, bankB[3], 0)
                if s == 17:
                    copy_all(act, bufC["kT"], bankB[0], g["crs_k"], g["crs_kT"])
                if s == 18:
                    copy_values(act, "crs", bufC, bankB[1])
                if 3 <= s < H + 3:
                    at_copy_pt(act, "spa", b, bankB[2], s - 3)
                yield 3.6 + s
                if 2 <= s < H + 2:
                    h = s - 2
                    act.wait_ge(g["sp_mul"], h + 1)
                    act.wait_ge(g["spa_nm"], h + 1)
                    for t in range(NT):
                        nc.scalar.activation(b["pr"][:, h % 2, t, :], sp_[:, h % 2, t, :], ACT.Exp,
                                             bias=b["nm"][:, h, t:t + 1]).then_inc(g["spa_ex"], 1)
            yield BO - 0.1
            at_copy_ot(act, "spa", b, bankB[3], 1)
            yield BO + 1.9
            at_out_act(act, "spa", b, bankB[2])
            yield C0 + 0.4
            ln_act(act, 4, lnB, bankB[2])
            yield C0 + 0.1
            copy_all(act, bufC["qT"], bankB[0], g["crs_q"], g["crs_qT"])
            for h in range(HS):
                yield C0 + 2.2 + h - 0.3
                if h == 11:
                    at_copy_ot(act, "crs", bufC, bankB[3], 0)
                if 2 <= h < H + 2:
                    at_copy_pt(act, "crs", bufC, bankB[2], h - 2)
                yield C0 + 2.7 + h
                if h < H:
                    exps(act, "crs", bufC, bankB[h % 2], h)
            yield CO - 0.1
            at_copy_ot(act, "crs", bufC, bankB[3], 1)
            yield CO + 0.8
            at_out_act(act, "crs", bufC, bankB[2])
            yield L0 + 1
            ln_act(act, 5, lnB, bankB[0])

        def vector_b(dve):
            b = bufB
            link = chain(dve, "dveB")
            for h in range(H):
                k = h % 2
                yield 4 + h
                dve.wait_ge(g["sp_sc"], h + 1)
                if h >= 2:
                    dve.wait_ge(g["sp_tk"], h - 1)
                    dve.wait_ge(g["sp_nm"], h - 1)
                src = sc[:, h % 3]
                n0 = link.n
                for r in range(ROUNDS):
                    if r:
                        yield 4 + h + r / ROUNDS
                    for t in range(NT):
                        if r:
                            link.wait(n0 + 2 * NT * r - NT + 1 + t)
                        top = m8[:, k, r, t, :] if r < ROUNDS - 1 else m8_last[:, k, t, 7:15]
                        link.inc(nc.vector.max(top, src[:, t, :]))
                    for t in range(NT):
                        link.wait(n0 + 2 * NT * r + 1 + t)
                        take = m8[:, k, r, t, :] if r < ROUNDS - 1 else m8_last[:, k, t, 0:8]
                        m = nc.vector.match_replace(out=wk[:, k, t, :], in_to_replace=take, in_values=src[:, t, :], imm_value=-BIG)
                        if r == ROUNDS - 1 and t == NT - 1:
                            m.then_inc(g["sp_top"], 1)
                        else:
                            link.inc(m)
                    src = wk[:, k]
            yield BO + 0.5
            at_out_dve(dve, "spa", b, bankB[0:2])
            dve.wait_ge(g["len_in"], 16)
            link(nc.vector.tensor_copy(lenf[:], lenb[:]))
            nc.vector.tensor_scalar(mrow[:], w["iota"][0:1, :].unsqueeze(1).broadcast_to([1, NT, S]), lenf[:, 0:1], NEG,
                                    ALU.is_ge, ALU.mult).then_inc(g["mask_row"], 1)
            yield BO + 2.1
            dve.wait_ge(g["sp_xb"], 1)
            add_rows(dve, x4, bankB[3], x3b, g["spa_y"], g["spa_x"])
            yield C0 + 0.8
            ln_dve(dve, 4, x4, lnB, [(g["spa_x"], 1)])
            yield C0 + 1.9
            ln_dve2(dve, 4, x4, lnB)
            for h in range(H):
                yield C0 + 2.4 + h
                scores_max(dve, "crs", bufC, bankB[h % 2], h)
            yield CO + 0.6
            at_out_dve(dve, "crs", bufC, bankB[0:2])
            yield CO + 2
            add_rows(dve, x5, bankB[3], x4, g["crs_y"], g["crs_x"])
            yield L0
            ln_dve(dve, 5, x5, lnB, [(g["crs_x"], 1)])
            yield L0 - 0.1
            ln_dve2(dve, 5, x5, lnB)
            yield L0 + 1.5
            dve.wait_ge(g["lin_xb"], 1)
            add_rows(dve, xo, bankB[1], xo, g["lin_y"], g["lin_o"])

        def pool_b(pool):
            b = bufB
            for c in range(QR // 2):
                yield 0.7 + 0.5 * c
                at_mask_q(pool, "spa", b, c)
            for s in range(BS):
                yield 2.6 + s
                if s == 1:
                    nc.gpsimd.tensor_tensor(x3b[:], x3[:], w["sbo"][:].unsqueeze(1).broadcast_to([P, NT, D]), ALU.add).then_inc(g["sp_xb"], 1)
                at_mask_later(pool, "spa", b, s)
                if 2 <= s < H + 2:
                    yield 3.1 + s
                    h = s - 2
                    pool.wait_ge(g["sp_top"], h + 1)
                    nc.gpsimd.tensor_scalar(mx0[:, h, :], m8[:, h % 2, 0, :, 0], 0.0, -1.0, ALU.max, ALU.mult).then_inc(g["sp_nm"], 1)
                    pool.wait_ge(g["sp_nm"], h + 1)
                    nc.gpsimd.tensor_copy(b["nm"][:, h, :], mx0[:, h, :]).then_inc(g["spa_nm"], 1)
                    pool.wait_ge(g["sp_tk"], h + 1)
                    nc.gpsimd.tensor_tensor(sp_[:, h % 2], taken[:, h % 2], sc[:, h % 3], ALU.mult).then_inc(g["sp_mul"], 1)
            yield BO + 0.4
            nc.gpsimd.memset(bufC["va"][:, :, :, HD:2 * HD], 1.0).then_inc(g["crs_ones"], 1)
            yield C0 + 1.5
            ln_pool(pool, 4, lnB)
            yield C0 + 2.5
            pool.wait_ge(g["crs_qT"], 1)
            for c in range(QR // 2):
                at_mask_q(pool, "crs", bufC, c)
            for h in range(HS):
                yield C0 + 2.1 + h + 1.1
                at_mask_later(pool, "crs", bufC, h)
            yield L0 + 0.2
            ln_pool(pool, 5, lnB)
            yield L0 + 1.1
            pool.wait_ge(g["ln5_xn"], 2)
            nc.gpsimd.tensor_tensor(xo[:], x5[:], w["fbias"][:].unsqueeze(1).broadcast_to([P, NT, D]), ALU.add).then_inc(g["lin_xb"], 1)

        LEN_A = [(0, 2.2), (A1 + 4, 3.94), (A1 + 8, 1.58), (A2, 2.6), (A3, 4.19), (A3 + 3, 2.21), (A3 + 5, 3), (M0, 2.37), (M0 + 8, 1.84), (AO, 3)]
        LEN_B = [(0, 0.23), (1, 0.5), (2, 0.46), (3, 2.41), (4, 5.5), (11, 5.34), (BO, 2.39), (C0, 1.73), (C0 + 2, 1.15), (C0 + 10, 1.98), (CO, 3.83), (L0, 7.36)]

        def shares(n, lengths):
            each = [max((f, v) for f, v in lengths if f <= k)[1] for k in range(n + 1)]
            return lambda t: (sum(each[:int(t)]) + (t - int(t)) * each[int(t)]) / sum(each[:n])

        keyA = shares(NA, LEN_A)
        keyB = shares(NB, LEN_B)
        mode = {}

        def waits_b():
            return mode["b"]

        def chain(eng, name):
            def link(ins):
                link.inc(ins)
                link.wait(link.n)

            def inc(ins):
                link.n += 1
                ins.then_inc(g[name], 1)
                return ins

            def wait(v):
                eng.wait_ge(g[name], v)
            link.n = 0
            link.inc = inc
            link.wait = wait
            return link

        def merged(a, b):
            ka = keyA(next(a)) if a else 3.0
            kb = keyB(next(b)) if b else 3.0
            while a or b:
                if ka <= kb:
                    v = next(a, None)
                    a, ka = (a, keyA(v)) if v is not None else (None, 3.0)
                else:
                    v = next(b, None)
                    b, kb = (b, keyB(v)) if v is not None else (None, 3.0)

        def one_pass(mix, mla, ib, first=False, last=False):
            A, Bs = mix or mla is not None, ib is not None
            mode["mix"], mode["mla"], mode["b"] = mix, mla is not None, Bs
            with nc.Block() as block:
                @block.sync
                def _(sp):
                    if mode["mla"] and not first:
                        sp.dma_start(xin[:], x_in[mla]).then_inc(g["x_in"], 16)
                    if mode["mla"] and mix and not Bs:
                        sp.dma_start(lenb[:], lens_in[0]).then_inc(s_stored, 16)
                    if Bs:
                        sp.wait_ge(s_stored, 16)
                        sp.sem_clear(s_stored)
                        sp.dma_start(ctxB[:], ctx_in[ib]).then_inc(g["ctxB_in"], 16)
                        sp.dma_start(lenb[:], lens_in[ib]).then_inc(g["len_in"], 16)
                    if mix:
                        sp.dma_start(xq_area[XD:XD + 8, :], w_in["groupq"]).then_inc(g["group_in"], 16)
                        sp.dma_start(vT_qm[XD:XD + 8, :], w_in["groupk"]).then_inc(g["group_in"], 16)
                    if mode["mla"]:
                        if mix:
                            sp.wait_ge(g["hm_proj"], 12)
                        sp.dma_start(ctxA[:], ctx_in[mla]).then_inc(g["ctxA_in"], 16)
                        sp.wait_ge(g["ctxA_in"], 16)
                    if Bs:
                        sp.wait_ge(g["lin_o"], 1)
                        sp.dma_start(out[ib], xo[:]).then_inc(s_stored, 16)
                        if last:
                            sp.wait_ge(s_stored, 16)

                @block.tensor
                def _(pe):
                    merged(tensor_a(pe) if A else None, tensor_b(pe) if Bs else None)

                @block.scalar
                def _(act):
                    merged(scalar_a(act) if A else None, scalar_b(act) if Bs else None)

                @block.vector
                def _(dve):
                    merged(vector_a(dve) if A else None, vector_b(dve) if Bs else None)

                @block.gpsimd
                def _(pool):
                    merged(pool_a(pool) if A else None, pool_b(pool) if Bs else None)

            with nc.Block() as block:
                @block.sync
                def _(sp):
                    sp.sem_clear(range(min(s.num for s in g.values()), max(s.num for s in g.values()) + 1))

        nb = out.shape[0]
        one_pass(False, 0, None, first=True)
        setup_rest()
        one_pass(True, 1, None)
        if nb > 2:
            with nc.Fori(0, nb - 2) as i:
                one_pass(True, i + 2, i)
        one_pass(True, None, nb - 2)
        one_pass(False, None, nb - 1, last=True)


def layouts(inp):
    c = lambda a: np.ascontiguousarray(a)
    f = np.float32
    i = {k: np.asarray(v) for k, v in inp.items()}
    rows = lambda a, n=P: c(a.reshape(a.shape[0] // n, n, a.shape[1]).transpose(1, 0, 2))
    swap = np.arange(D) ^ 1
    head = np.arange(H, dtype=f)[:, None]
    inv = f(1.0) / f(10000.0) ** (np.arange(0, HD, 2, dtype=f) / f(HD))
    ang = (head * inv[None, :]).astype(f)
    cos, sin = (np.repeat(t(ang).astype(f), 2, 1).reshape(1, D) for t in (np.cos, np.sin))
    p = np.arange(P)
    ropec = np.repeat(cos, P, 0)
    ropes = np.repeat(sin * np.where(np.arange(D) % 2 == 0, -1.0, 1.0)[None, :], P, 0)
    padrow = lambda a, top: np.concatenate([a, np.zeros((P - a.shape[0], a.shape[1]), f)][:: 1 if top else -1], 0)
    wide = lambda v: c(np.broadcast_to(v[None, :], (P, v.shape[0])))
    cols = lambda v, n=P: c(v.reshape(-1, n).T)
    u8 = np.tile(np.arange(8), 2 * NJ * H)
    onehot = (u8[None, :] == np.arange(8)[:, None]).astype(f)
    tok = p[:, None] + P * np.arange(NT)[None, :]
    w = {
        "wq0": rows(i["L0_attn_wq"].T), "wq0s": rows(i["L0_attn_wq"].T[:, swap]),
        "wlat": rows(np.concatenate([i["L0_attn_wk_a"].T, i["L0_attn_wv_a"].T], 1)),
        "wkb": padrow(i["L0_attn_wk_b"].T, True), "wkbs": padrow(i["L0_attn_wk_b"].T[:, swap], True),
        "wvb": padrow(i["L0_attn_wv_b"].T, False), "wo0": rows(i["L0_attn_wo"].T),
        "ropec": ropec, "ropes": ropes, "hmask": 0.25 * (p[:, None] // HD == np.arange(HT)[None, :]),
        "xwq": rows(i["L0_xattn_Wq"].T), "xwk": rows(i["L0_xattn_Wk"].T), "xwv": rows(i["L0_xattn_Wv"].T),
        "xwo": rows(i["L0_xattn_Wo"].T),
        "xb": np.stack([cols(i["L0_xattn_b" + k], XD) for k in "qkv"], 1), "xbo": wide(i["L0_xattn_bo"]),
        "wrt": rows(np.repeat(i["L0_ffn_w_router"][:, None], P, 1)),
        "w1": rows(i["L0_ffn_W1"]), "b1": cols(i["L0_ffn_b1"]), "w2": rows(i["L0_ffn_W2"]), "b2": i["L0_ffn_b2"][None, :],
        "swq": rows(i["L1_attn_Wq"]), "swk": rows(i["L1_attn_Wk"]), "swv": rows(i["L1_attn_Wv"]), "swo": rows(i["L1_attn_Wo"]),
        "sbq": cols(i["L1_attn_bq"]), "sbk": cols(i["L1_attn_bk"]), "sbv": wide(i["L1_attn_bv"]), "sbo": wide(i["L1_attn_bo"]),
        "cwq": rows(i["L1_xattn_Wq"]), "cwk": rows(i["L1_xattn_Wk"]), "cwv": rows(i["L1_xattn_Wv"]), "cwo": rows(i["L1_xattn_Wo"]),
        "wt": rows(i["L1_ffn_weight"].T), "alpha": c(np.broadcast_to(i["L1_ffn_alpha"][None, :], (P, 1))), "fbias": wide(i["L1_ffn_bias"]),
        "ident": np.eye(P), "iota": np.broadcast_to(np.arange(S)[None, :], (P, S)),
        "lower": np.arange(S)[None, None, :] < tok[:, :, None],
        "groupq": onehot, "groupk": -FAR * (1 - onehot),
    }
    w = {k: c(v if v.dtype == f else v.astype(f)) for k, v in w.items()}
    x = c(i["x"].reshape(-1, NT, P, D).transpose(0, 2, 1, 3))
    ctx = c(i["ctx_1024"].reshape(-1, S, ND, P).transpose(0, 3, 2, 1))
    return w, x, ctx, c(i["_lenS2"].reshape(-1, 1, 1))


def declare(nc, nb):
    ext = lambda n, s, dt, k="ExternalInput": nc.dram_tensor(n, tuple(s), dt, kind=k).ap()
    w_in = {n: ext("w_" + n, s, F32) for n, s in WEIGHTS.items()}
    x_in = ext("x_in", (nb, P, NT, D), F32)
    ctx_in = ext("ctx_in", (nb, P, ND, S), F32)
    lens_in = ext("lens_in", (nb, 1, 1), I32)
    out = ext("out", (nb, P, NT, D), F32, "ExternalOutput")
    program(nc, x_in, ctx_in, lens_in, w_in, out)


def kernel(**inputs):
    import concourse.bacc as bacc
    from concourse.bass_utils import run_bass_kernel_spmd
    w, x, ctx, lens = layouts(inputs)
    arrays = {"w_" + k: v for k, v in w.items()}
    arrays.update(x_in=x, ctx_in=ctx, lens_in=lens)
    nc = bacc.Bacc("TRN2", target_bir_lowering=False, num_devices=1)
    declare(nc, B)
    r = run_bass_kernel_spmd(nc, [arrays], core_ids=[0])
    y = r.results[0]["out"]
    return np.ascontiguousarray(y.transpose(0, 2, 1, 3).reshape(B, S, D))
```
